# Optimizing a Trainium2 kernel written in Bass

```python
import numpy as np
import jax
import jax.numpy as jnp

def _softmax(x, axis=-1):
    return jax.nn.softmax(x, axis=axis)

def _gelu(x):
    return jax.nn.gelu(x, approximate=True)

def _silu(x):
    return jax.nn.silu(x)

def _sigmoid(x):
    return jax.nn.sigmoid(x)

def _layernorm(x, axis=-1, eps=1e-05):
    m = jnp.mean(x, axis=axis, keepdims=True)
    v = jnp.var(x, axis=axis, keepdims=True)
    return (x - m) / jnp.sqrt(v + eps)

def _scatter_add(tgt, idx, src, axis=0):
    return tgt.at[idx].add(src)

def _segment_sum(src, seg, n):
    return jax.ops.segment_sum(src, seg, n)
kernel_name = 'mk_gnn_preln_d2_gnn_r8_24889a'

def setup_inputs(seed: int=0):
    np.random.seed(seed)
    _w = jnp.asarray

    def _rec_inputs():
        import jax
        import jax.numpy as jnp
        _gk = jax.random.key(seed)
        x = -0.0002117 + 1 * jax.random.normal(jax.random.fold_in(_gk, 1), (1250, 512), jnp.float32)
        src = jax.random.randint(jax.random.fold_in(_gk, 2), (20000,), 0, 1250, jnp.int32)
        dst = jnp.minimum((1250 * jax.random.uniform(jax.random.fold_in(_gk, 3), (20000,)) ** 2.0).astype(jnp.int32), 9999)
        _o = jnp.argsort(dst, stable=True)
        src = src[_o]
        dst = dst[_o]
        node_vec1 = jax.random.uniform(jax.random.fold_in(_gk, 12), (1250, 1), jnp.float32, 0.0, 0.999957)
        return (x, src, dst, node_vec1)
    x, src, dst, node_vec1 = _rec_inputs()

    def _L0_gnn_setup():
        import jax, jax.numpy as jnp
        import numpy as np
        N = 6250
        E = 200000
        IN_DIM, HID, LAT = (512, 128, 64)
        DEC_DIMS = [128, 256]
        OUT_DIM = 512

        def _glorot(key, shape):
            fan_in, fan_out = (shape[1], shape[0])
            lim = (6.0 / (fan_in + fan_out)) ** 0.5
            return jax.random.uniform(key, shape, jnp.float32, -lim, lim)

        def gcn_conv(x, W, b, src, dst, n):
            h = x @ W.T
            loop = jnp.arange(n, dtype=src.dtype)
            s = jnp.concatenate([src, loop])
            d = jnp.concatenate([dst, loop])
            deg = jnp.zeros((n,), h.dtype).at[d].add(1.0)
            dinv = jnp.where(deg > 0, deg ** (-0.5), 0.0)
            norm = dinv[s] * dinv[d]
            msg = h[s] * norm[:, None]
            out = jax.ops.segment_sum(msg, d, num_segments=n)
            return out + b
        key = jax.random.key(seed)
        ks = jax.random.split(key, 12)
        x = jax.random.normal(ks[0], (N, IN_DIM), jnp.float32)
        edge_index = jax.random.randint(ks[1], (2, E), 0, N, jnp.int64)
        W1 = _glorot(ks[2], (HID, IN_DIM))
        b1 = jnp.zeros((HID,), jnp.float32)
        W2 = _glorot(ks[3], (LAT, HID))
        b2 = jnp.zeros((LAT,), jnp.float32)
        Wd1 = _glorot(ks[4], (DEC_DIMS[0], LAT))
        bd1 = jnp.zeros((DEC_DIMS[0],), jnp.float32)
        Wd2 = _glorot(ks[5], (DEC_DIMS[1], DEC_DIMS[0]))
        bd2 = jnp.zeros((DEC_DIMS[1],), jnp.float32)
        Wd3 = _glorot(ks[6], (OUT_DIM, DEC_DIMS[1]))
        bd3 = jnp.zeros((OUT_DIM,), jnp.float32)
        return dict(x=x, edge_index=edge_index, W1=W1, b1=b1, W2=W2, b2=b2, Wd1=Wd1, bd1=bd1, Wd2=Wd2, bd2=bd2, Wd3=Wd3, bd3=bd3)
    _L0_gnn_all = _L0_gnn_setup()
    _L0_gnn_in = {k: v for k, v in _L0_gnn_all.items() if k in ('W1', 'b1', 'W2', 'b2', 'Wd1', 'bd1', 'Wd2', 'bd2', 'Wd3', 'bd3')}
    del _L0_gnn_all

    def _L1_gnn_setup():
        import jax, jax.numpy as jnp
        import numpy as np
        N_NODES = 40962
        LATENT_DIM = 512
        N_EDGES = 81924
        NUM_BLOCKS = 4
        NUM_HEADS = 4
        NUM_FREQ = 32
        BASE_PERIOD = 16
        NOISE_EMB_DIM = 16
        EPS = 1e-05

        def _cond_layer_norm(x, cond, sw, sb, bw, bb):
            mu = jnp.mean(x, axis=-1, keepdims=True)
            var = jnp.var(x, axis=-1, keepdims=True)
            xn = (x - mu) * jax.lax.rsqrt(var + EPS)
            scale = cond @ sw + sb
            bias = cond @ bw + bb
            return xn * (1.0 + scale) + bias

        def _sparse_attention(x, src, dst, wq, bq, wk, bk, wv, bv, wo, bo):
            N, D = x.shape
            H, Dh = (NUM_HEADS, D // NUM_HEADS)
            q = (x @ wq + bq).reshape(N, H, Dh) * Dh ** (-0.5)
            k = (x @ wk + bk).reshape(N, H, Dh)
            v = (x @ wv + bv).reshape(N, H, Dh)
            scores = jnp.einsum('ehd,ehd->eh', q[src], k[dst])
            smax = jax.ops.segment_max(scores, src, num_segments=N)
            ex = jnp.exp(scores - smax[src])
            denom = jax.ops.segment_sum(ex, src, num_segments=N)
            attn = ex / denom[src]
            out = jax.ops.segment_sum(attn[:, :, None] * v[dst], src, num_segments=N)
            return out.reshape(N, D) @ wo + bo

        def _forward(x, edge_index, noise_levels, f_w1, f_b1, f_w2, f_b2, s1_w, s1_b, b1_w, b1_b, wq, bq, wk, bk, wv, bv, wo, bo, s2_w, s2_b, b2_w, b2_b, m_w1, m_b1, m_w2, m_b2):
            src, dst = (edge_index[0], edge_index[1])
            freqs = jnp.arange(1, NUM_FREQ + 1, dtype=x.dtype) * (2.0 * np.pi / BASE_PERIOD)
            ph = noise_levels * freqs
            emb = jnp.concatenate([jnp.sin(ph), jnp.cos(ph)], axis=-1)
            cond = jax.nn.silu(emb @ f_w1 + f_b1) @ f_w2 + f_b2
            for i in range(NUM_BLOCKS):
                y = _cond_layer_norm(x, cond, s1_w[i], s1_b[i], b1_w[i], b1_b[i])
                y = _sparse_attention(y, src, dst, wq[i], bq[i], wk[i], bk[i], wv[i], bv[i], wo[i], bo[i])
                x = x + y
                y = _cond_layer_norm(x, cond, s2_w[i], s2_b[i], b2_w[i], b2_b[i])
                y = jax.nn.relu(y @ m_w1[i] + m_b1[i]) @ m_w2[i] + m_b2[i]
                x = x + y
            return x
        key = jax.random.key(seed)
        ks = jax.random.split(key, 20)

        def w(k, shape, s=0.02):
            return jax.random.normal(k, shape, dtype=jnp.float32) * s
        D, B, C = (LATENT_DIM, NUM_BLOCKS, NOISE_EMB_DIM)
        z = lambda *s: jnp.zeros(s, jnp.float32)
        return {'latent_mesh_nodes': jax.random.normal(ks[0], (N_NODES, D), dtype=jnp.float32), 'edge_index': jax.random.randint(ks[1], (2, N_EDGES), 0, N_NODES, dtype=jnp.int32), 'noise_levels': jax.random.uniform(ks[2], (N_NODES, 1), dtype=jnp.float32), 'f_w1': w(ks[3], (2 * NUM_FREQ, C)), 'f_b1': z(C), 'f_w2': w(ks[4], (C, C)), 'f_b2': z(C), 's1_w': w(ks[5], (B, C, D)), 's1_b': z(B, D), 'b1_w': w(ks[6], (B, C, D)), 'b1_b': z(B, D), 'wq': w(ks[7], (B, D, D)), 'bq': z(B, D), 'wk': w(ks[8], (B, D, D)), 'bk': z(B, D), 'wv': w(ks[9], (B, D, D)), 'bv': z(B, D), 'wo': w(ks[10], (B, D, D)), 'bo': z(B, D), 's2_w': w(ks[11], (B, C, D)), 's2_b': z(B, D), 'b2_w': w(ks[12], (B, C, D)), 'b2_b': z(B, D), 'm_w1': w(ks[13], (B, D, D)), 'm_b1': z(B, D), 'm_w2': w(ks[14], (B, D, D)), 'm_b2': z(B, D)}
    _L1_gnn_all = _L1_gnn_setup()
    _L1_gnn_in = {k: v for k, v in _L1_gnn_all.items() if k in ('f_w1', 'f_b1', 'f_w2', 'f_b2', 's1_w', 's1_b', 'b1_w', 'b1_b', 'wq', 'bq', 'wk', 'bk', 'wv', 'bv', 'wo', 'bo', 's2_w', 's2_b', 'b2_w', 'b2_b', 'm_w1', 'm_b1', 'm_w2', 'm_b2')}
    del _L1_gnn_all
    return {'x': x, 'src': src, 'dst': dst, 'node_vec1': node_vec1, 'L0_gnn_W1': _L0_gnn_in['W1'], 'L0_gnn_b1': _L0_gnn_in['b1'], 'L0_gnn_W2': _L0_gnn_in['W2'], 'L0_gnn_b2': _L0_gnn_in['b2'], 'L0_gnn_Wd1': _L0_gnn_in['Wd1'], 'L0_gnn_bd1': _L0_gnn_in['bd1'], 'L0_gnn_Wd2': _L0_gnn_in['Wd2'], 'L0_gnn_bd2': _L0_gnn_in['bd2'], 'L0_gnn_Wd3': _L0_gnn_in['Wd3'], 'L0_gnn_bd3': _L0_gnn_in['bd3'], 'L1_gnn_f_w1': _L1_gnn_in['f_w1'], 'L1_gnn_f_b1': _L1_gnn_in['f_b1'], 'L1_gnn_f_w2': _L1_gnn_in['f_w2'], 'L1_gnn_f_b2': _L1_gnn_in['f_b2'], 'L1_gnn_s1_w': _L1_gnn_in['s1_w'], 'L1_gnn_s1_b': _L1_gnn_in['s1_b'], 'L1_gnn_b1_w': _L1_gnn_in['b1_w'], 'L1_gnn_b1_b': _L1_gnn_in['b1_b'], 'L1_gnn_wq': _L1_gnn_in['wq'], 'L1_gnn_bq': _L1_gnn_in['bq'], 'L1_gnn_wk': _L1_gnn_in['wk'], 'L1_gnn_bk': _L1_gnn_in['bk'], 'L1_gnn_wv': _L1_gnn_in['wv'], 'L1_gnn_bv': _L1_gnn_in['bv'], 'L1_gnn_wo': _L1_gnn_in['wo'], 'L1_gnn_bo': _L1_gnn_in['bo'], 'L1_gnn_s2_w': _L1_gnn_in['s2_w'], 'L1_gnn_s2_b': _L1_gnn_in['s2_b'], 'L1_gnn_b2_w': _L1_gnn_in['b2_w'], 'L1_gnn_b2_b': _L1_gnn_in['b2_b'], 'L1_gnn_m_w1': _L1_gnn_in['m_w1'], 'L1_gnn_m_b1': _L1_gnn_in['m_b1'], 'L1_gnn_m_w2': _L1_gnn_in['m_w2'], 'L1_gnn_m_b2': _L1_gnn_in['m_b2']}

def reference(x, src, dst, node_vec1, L0_gnn_W1, L0_gnn_b1, L0_gnn_W2, L0_gnn_b2, L0_gnn_Wd1, L0_gnn_bd1, L0_gnn_Wd2, L0_gnn_bd2, L0_gnn_Wd3, L0_gnn_bd3, L1_gnn_f_w1, L1_gnn_f_b1, L1_gnn_f_w2, L1_gnn_f_b2, L1_gnn_s1_w, L1_gnn_s1_b, L1_gnn_b1_w, L1_gnn_b1_b, L1_gnn_wq, L1_gnn_bq, L1_gnn_wk, L1_gnn_bk, L1_gnn_wv, L1_gnn_bv, L1_gnn_wo, L1_gnn_bo, L1_gnn_s2_w, L1_gnn_s2_b, L1_gnn_b2_w, L1_gnn_b2_b, L1_gnn_m_w1, L1_gnn_m_b1, L1_gnn_m_w2, L1_gnn_m_b2):
    import jax
    import jax.numpy as jnp

    def _L0_gnn_ref(x, edge_index, W1, b1, W2, b2, Wd1, bd1, Wd2, bd2, Wd3, bd3):
        import jax, jax.numpy as jnp
        import numpy as np
        N = 6250
        E = 200000
        IN_DIM, HID, LAT = (512, 128, 64)
        DEC_DIMS = [128, 256]
        OUT_DIM = 512

        def _glorot(key, shape):
            fan_in, fan_out = (shape[1], shape[0])
            lim = (6.0 / (fan_in + fan_out)) ** 0.5
            return jax.random.uniform(key, shape, jnp.float32, -lim, lim)

        def gcn_conv(x, W, b, src, dst, n):
            h = x @ W.T
            loop = jnp.arange(n, dtype=src.dtype)
            s = jnp.concatenate([src, loop])
            d = jnp.concatenate([dst, loop])
            deg = jnp.zeros((n,), h.dtype).at[d].add(1.0)
            dinv = jnp.where(deg > 0, deg ** (-0.5), 0.0)
            norm = dinv[s] * dinv[d]
            msg = h[s] * norm[:, None]
            out = jax.ops.segment_sum(msg, d, num_segments=n)
            return out + b
        src, dst = (edge_index[0], edge_index[1])
        n = x.shape[0]
        h = gcn_conv(x, W1, b1, src, dst, n)
        h = jax.nn.relu(h)
        z = gcn_conv(h, W2, b2, src, dst, n)
        y = jax.nn.relu(z @ Wd1.T + bd1)
        y = jax.nn.relu(y @ Wd2.T + bd2)
        return y @ Wd3.T + bd3

    def _L1_gnn_ref(latent_mesh_nodes, edge_index, noise_levels, f_w1, f_b1, f_w2, f_b2, s1_w, s1_b, b1_w, b1_b, wq, bq, wk, bk, wv, bv, wo, bo, s2_w, s2_b, b2_w, b2_b, m_w1, m_b1, m_w2, m_b2):
        import jax, jax.numpy as jnp
        import numpy as np
        N_NODES = 40962
        LATENT_DIM = 512
        N_EDGES = 81924
        NUM_BLOCKS = 4
        NUM_HEADS = 4
        NUM_FREQ = 32
        BASE_PERIOD = 16
        NOISE_EMB_DIM = 16
        EPS = 1e-05

        def _cond_layer_norm(x, cond, sw, sb, bw, bb):
            mu = jnp.mean(x, axis=-1, keepdims=True)
            var = jnp.var(x, axis=-1, keepdims=True)
            xn = (x - mu) * jax.lax.rsqrt(var + EPS)
            scale = cond @ sw + sb
            bias = cond @ bw + bb
            return xn * (1.0 + scale) + bias

        def _sparse_attention(x, src, dst, wq, bq, wk, bk, wv, bv, wo, bo):
            N, D = x.shape
            H, Dh = (NUM_HEADS, D // NUM_HEADS)
            q = (x @ wq + bq).reshape(N, H, Dh) * Dh ** (-0.5)
            k = (x @ wk + bk).reshape(N, H, Dh)
            v = (x @ wv + bv).reshape(N, H, Dh)
            scores = jnp.einsum('ehd,ehd->eh', q[src], k[dst])
            smax = jax.ops.segment_max(scores, src, num_segments=N)
            ex = jnp.exp(scores - smax[src])
            denom = jax.ops.segment_sum(ex, src, num_segments=N)
            attn = ex / denom[src]
            out = jax.ops.segment_sum(attn[:, :, None] * v[dst], src, num_segments=N)
            return out.reshape(N, D) @ wo + bo

        def _forward(x, edge_index, noise_levels, f_w1, f_b1, f_w2, f_b2, s1_w, s1_b, b1_w, b1_b, wq, bq, wk, bk, wv, bv, wo, bo, s2_w, s2_b, b2_w, b2_b, m_w1, m_b1, m_w2, m_b2):
            src, dst = (edge_index[0], edge_index[1])
            freqs = jnp.arange(1, NUM_FREQ + 1, dtype=x.dtype) * (2.0 * np.pi / BASE_PERIOD)
            ph = noise_levels * freqs
            emb = jnp.concatenate([jnp.sin(ph), jnp.cos(ph)], axis=-1)
            cond = jax.nn.silu(emb @ f_w1 + f_b1) @ f_w2 + f_b2
            for i in range(NUM_BLOCKS):
                y = _cond_layer_norm(x, cond, s1_w[i], s1_b[i], b1_w[i], b1_b[i])
                y = _sparse_attention(y, src, dst, wq[i], bq[i], wk[i], bk[i], wv[i], bv[i], wo[i], bo[i])
                x = x + y
                y = _cond_layer_norm(x, cond, s2_w[i], s2_b[i], b2_w[i], b2_b[i])
                y = jax.nn.relu(y @ m_w1[i] + m_b1[i]) @ m_w2[i] + m_b2[i]
                x = x + y
            return x
        return _forward(latent_mesh_nodes, edge_index, noise_levels, f_w1, f_b1, f_w2, f_b2, s1_w, s1_b, b1_w, b1_b, wq, bq, wk, bk, wv, bv, wo, bo, s2_w, s2_b, b2_w, b2_b, m_w1, m_b1, m_w2, m_b2)
    edge_index = jnp.stack([src, dst])
    h = jnp.maximum(_layernorm(x, axis=-1), 0.0)
    x = x + _L0_gnn_ref(h, edge_index, L0_gnn_W1, L0_gnn_b1, L0_gnn_W2, L0_gnn_b2, L0_gnn_Wd1, L0_gnn_bd1, L0_gnn_Wd2, L0_gnn_bd2, L0_gnn_Wd3, L0_gnn_bd3)
    h = jnp.maximum(_layernorm(x, axis=-1), 0.0)
    x = x + _L1_gnn_ref(h, edge_index, node_vec1, L1_gnn_f_w1, L1_gnn_f_b1, L1_gnn_f_w2, L1_gnn_f_b2, L1_gnn_s1_w, L1_gnn_s1_b, L1_gnn_b1_w, L1_gnn_b1_b, L1_gnn_wq, L1_gnn_bq, L1_gnn_wk, L1_gnn_bk, L1_gnn_wv, L1_gnn_bv, L1_gnn_wo, L1_gnn_bo, L1_gnn_s2_w, L1_gnn_s2_b, L1_gnn_b2_w, L1_gnn_b2_b, L1_gnn_m_w1, L1_gnn_m_b1, L1_gnn_m_w2, L1_gnn_m_b2)
    return x

_drawn_inputs = setup_inputs


def setup_inputs(seed=0):
    import zlib

    import numpy as np

    out = dict(_drawn_inputs(seed))
    spreads = {'L0_gnn_b1': (0.0, 0.362),
     'L0_gnn_b2': (0.0, 0.288),
     'L0_gnn_bd1': (0.0, 0.1),
     'L0_gnn_bd2': (0.0, 0.1),
     'L0_gnn_bd3': (0.0, 0.1),
     'L1_gnn_f_b1': (0.0, 0.8),
     'L1_gnn_f_b2': (0.0, 0.8),
     'L1_gnn_s1_b': (0.0, 0.673),
     'L1_gnn_b1_b': (0.0, 0.291),
     'L1_gnn_bq': (0.0, 0.8),
     'L1_gnn_bk': (0.0, 0.8),
     'L1_gnn_bv': (0.0, 0.1),
     'L1_gnn_bo': (0.0, 0.1),
     'L1_gnn_s2_b': (0.0, 0.435),
     'L1_gnn_b2_b': (0.0, 0.439),
     'L1_gnn_m_b1': (0.0, 0.1),
     'L1_gnn_m_b2': (0.0, 0.1)}
    factors = {'node_vec1': 8.0,
     'L1_gnn_f_w1': 8.0,
     'L1_gnn_f_w2': 8.0,
     'L1_gnn_s1_w': 8.0,
     'L1_gnn_b1_w': 8.0,
     'L1_gnn_wq': 4.623,
     'L1_gnn_wk': 4.533,
     'L1_gnn_s2_w': 8.0,
     'L1_gnn_b2_w': 8.0}
    for name, (base, spread) in spreads.items():
        noise = np.random.default_rng([zlib.crc32(name.encode()), seed]).standard_normal(out[name].shape)
        drawn = base * np.exp(spread * noise) if base else spread * noise
        out[name] = jnp.asarray(drawn.astype(out[name].dtype))
    for name, factor in factors.items():
        out[name] = (out[name] * factor).astype(out[name].dtype)
    return out
```

```python
from contextlib import ExitStack

import numpy as np

import concourse.bass as bass
from concourse import mybir

F32 = mybir.dt.float32
BF16 = mybir.dt.bfloat16
F16 = mybir.dt.float16
I32 = mybir.dt.int32
ALU = mybir.AluOpType
ACT = mybir.ActivationFunctionType

N = 1250
NT = 10
R = N // NT
E = 20000
D = 512
KT = D // 128
EPS = 1e-5
BLOCKS, HEADS = 4, 4
DH = D // HEADS
QSCALE = float(DH) ** -0.5
NEVER = -1e37

ET = E // R
GT = 16
GROUPS = ET // GT
HALF = N // 2
HPITCH = HALF + 1
SHIFT = 11
BASE = 1 << SHIFT
assert GT * R < BASE and GROUPS * GT == ET

NFREQ = 32
NOISE = 16
TWO_PI = 2.0 * np.pi
PI_A = 6.28125
PI_B = float(np.float32(np.float16(TWO_PI - PI_A)))
PI_C = float(np.float32(TWO_PI - PI_A - PI_B))
PI_MAX = 3.1415925

CHUNKS = [(0, 512), (512, 512), (1024, N - 1024)]


def broadcast_rows(row_ap, rows):
    return bass.AP(row_ap.tensor, row_ap.offset, [[0, rows]] + [list(p) for p in row_ap.ap])


def identity(pool, zeroed, done, t):
    pool.memset(t, 0.0).then_inc(zeroed, 1)
    pool.wait_ge(zeroed, 1)
    pool.affine_select(out=t, in_=t, compare_op=ALU.not_equal, fill=1.0, base=0,
                       pattern=[[-1, 128]], channel_multiplier=1).then_inc(done, 1)


def count_edges(nc, src, dst, counts, onehot_a, scratch):
    ctx = ExitStack()
    with ctx:
        def sb(name, shape, dt):
            return ctx.enter_context(nc.sbuf_tensor(name, shape, dt))

        def sem(name):
            return ctx.enter_context(nc.semaphore(name))

        onehot_b = sb("onehot_b", [R, GT, N], BF16)
        ohs = [onehot_a, onehot_b[:, :, :]]
        ohd = sb("onehot_dst", [R, 2, GT, HPITCH], BF16)
        ids = sb("ids", [R, N], F16)
        raw = sb("raw_edges", [R, 2, ET], I32)
        ends = sb("edge_ends", [R, 2, ET], F32)
        upper = sb("upper_half", [R, ET], F32)
        weight = sb("weight", [R, ET], F32)
        now = sb("group_pair", [R, 3, 2 * GT], F32)
        packed = scratch[:, 0:2 * HALF].bitcast(I32).rearrange("p (b c) -> p b c", b=2)
        parts = scratch[:, 2 * HALF:4 * HALF].bitcast(I32).rearrange("p (b c) -> p b c", b=2)
        ps = ctx.enter_context(nc.psum_tensor("count_ps", [128, 4, 2, 512], F32))
        edges_in, ids_in, counts_zero = sem("edges_in"), sem("ids_in"), sem("counts_zero")
        prep, group_copied, onehots_ready = sem("prep"), sem("group_copied"), sem("onehots_ready")
        ps_filled, ps_drained = sem("ps_filled"), sem("ps_drained")
        parts_ready, parts_added = sem("parts_ready"), sem("parts_added")
        H1 = 313
        split = [(0, H1), (H1, HALF - H1)]

        with nc.Block() as block:
            @block.sync
            def _(sp):
                sp.dma_start(raw[:, 0, :], src.rearrange("(p t) -> p t", t=ET)).then_inc(edges_in, 16)
                sp.dma_start(raw[:, 1, :], dst.rearrange("(p t) -> p t", t=ET)).then_inc(edges_in, 16)

            @block.gpsimd
            def _(pool):
                pool.iota(ids[:, :], pattern=[[1, N]], base=0, channel_multiplier=0,
                          allow_small_or_imprecise_dtypes=True).then_inc(ids_in, 1)
                pool.sem_inc(ps_drained, 1)
                pool.sem_inc(parts_added, 1)
                for i in range(NT):
                    pool.memset(counts[:, i, :], 0.0).then_inc(counts_zero, 1)

            @block.vector
            def _(v):
                v.wait_ge(edges_in, 32)
                v.tensor_copy(ends[:, :, :], raw[:, :, :]).then_inc(prep, 1)
                v.wait_ge(prep, 1)
                v.tensor_scalar(upper[:, :], ends[:, 1, :], float(HALF), None, ALU.is_ge).then_inc(prep, 1)
                v.wait_ge(prep, 2)
                v.tensor_scalar(weight[:, :], upper[:, :], float(BASE - 1), 1.0, ALU.mult,
                                ALU.add).then_inc(prep, 1)
                v.scalar_tensor_tensor(ends[:, 1, :], upper[:, :], -float(HALF), ends[:, 1, :],
                                       ALU.mult, ALU.add).then_inc(prep, 1)
                v.wait_ge(prep, 4)
                v.wait_ge(ids_in, 1)
                v.wait_ge(counts_zero, NT)

                def onehots(half, first, pair):
                    for k, of in enumerate((ends[:, 0, :], ends[:, 1, :], weight[:, :])):
                        v.tensor_copy(now[:, k, half * GT:(half + 1) * GT],
                                      of[:, bass.ds(first, GT)]).then_inc(group_copied, 1)
                    v.wait_ge(group_copied, pair * 6 + (half + 1) * 3)
                    for t in range(GT):
                        c = half * GT + t
                        v.tensor_scalar(ohs[half][:, t, :], ids[:, :], now[:, 0, c:c + 1], None,
                                        ALU.is_equal)
                        last = v.tensor_scalar(ohd[:, half, t, 0:HALF], ids[:, 0:HALF], now[:, 1, c:c + 1],
                                               now[:, 2, c:c + 1], ALU.is_equal, ALU.mult)
                    last.then_inc(onehots_ready, 1)

                def add_group(half, p):
                    for m in range(NT):
                        k = half * NT + m
                        v.wait_ge(ps_drained, p * 2 * NT + (k + 2))
                        v.tensor_scalar(parts[:, 0, :], packed[:, k % 2, :], BASE - 1, None, ALU.bitwise_and)
                        v.tensor_scalar(parts[:, 1, :], packed[:, k % 2, :], SHIFT, None,
                                        ALU.logical_shift_right).then_inc(parts_ready, 1)
                        v.wait_ge(parts_ready, p * 2 * NT + (k + 1))
                        both = counts[:, m, :].rearrange("p (b c) -> p b c", b=2)
                        v.tensor_tensor(both, both, parts, ALU.add).then_inc(parts_added, 1)
                        v.wait_ge(parts_added, p * 2 * NT + (k + 2))

                onehots(0, 0, 0)
                onehots(1, GT, 0)
                with v.Fori(0, GROUPS // 2 - 1) as p:
                    for half in range(2):
                        add_group(half, p)
                        onehots(half, p * (2 * GT) + (2 + half) * GT, p + 1)
                for half in range(2):
                    add_group(half, GROUPS // 2 - 1)

            @block.tensor
            def _(pe):
                with pe.Fori(0, GROUPS // 2) as p:
                    for half in range(2):
                        pe.wait_ge(onehots_ready, 2 * p + (half + 1))
                        for m in range(NT):
                            k = half * NT + m
                            pe.wait_ge(ps_drained, p * 2 * NT + (max(k - 3, 0) + 1))
                            for t in range(GT):
                                for c, (at, n) in enumerate(split):
                                    last = pe.matmul(ps[0:R, k % 4, c, 0:n], ohs[half][:, t, m * R:(m + 1) * R],
                                                     ohd[:, half, t, at:at + n], start=(t == 0),
                                                     stop=(t == GT - 1))
                            last.then_inc(ps_filled, 1)

            @block.scalar
            def _(act):
                with act.Fori(0, GROUPS // 2) as p:
                    for half in range(2):
                        for m in range(NT):
                            k = half * NT + m
                            act.wait_ge(ps_filled, p * 2 * NT + (k + 1))
                            act.wait_ge(parts_added, p * 2 * NT + (max(k - 1, 0) + 1))
                            act.activation(packed[:, k % 2, 0:H1], ps[0:R, k % 4, 0, 0:H1], ACT.Copy)
                            act.activation(packed[:, k % 2, H1:HALF], ps[0:R, k % 4, 1, 0:HALF - H1],
                                           ACT.Copy).then_inc(ps_drained, 1)


def row_stats(v, x, i, stats, mean_var, done, count):
    v.bn_stats(stats[:, i, :], x[:, i, :]).then_inc(done, 1)
    v.wait_ge(done, count + 1)
    v.bn_aggr(mean_var[:, i, :], stats[:, i, :]).then_inc(done, 1)


def gcn_layer(nc, x_in, w1, b1, w2, b2, wd1, bd1, wd2, bd2, wd3, bd3, x_keep, x, counts, logc, has_edge,
              ident):
    HID, LAT, DEC = w1.shape[0], w2.shape[0], wd2.shape[0]
    MC = DEC // 128
    ctx = ExitStack()
    with ctx:
        def sb(name, shape, dt=F32):
            return ctx.enter_context(nc.sbuf_tensor(name, shape, dt))

        def sem(name):
            return ctx.enter_context(nc.semaphore(name))

        xb = sb("xb", [R, NT, D])
        h = sb("h_tile", [R, 2, D])
        hT = sb("hT", [128, KT, N])
        y1T = hT[:, 0, :]
        y2T = hT[:, 1:1 + MC, :]
        no_edge = hT[0:R, 1 + MC, :]
        g1, t1 = sb("g1", [R, NT, HID]), sb("t1", [R, NT, HID])
        g2, t2 = sb("g2", [R, NT, LAT]), sb("t2", [R, NT, LAT])
        rT, zT = sb("rT", [HID, N]), sb("zT", [LAT, N])
        w1r, w1T = sb("w1r", [HID, D]), sb("w1T", [128, KT, HID])
        w2r, w2T = sb("w2r", [LAT, HID]), sb("w2T", [HID, LAT])
        wd1r, wd1T = sb("wd1r", [HID, LAT]), sb("wd1T", [LAT, HID])
        wd2r, wd2T = sb("wd2r", [128, MC, HID]), sb("wd2T", [HID, DEC])
        wd3r, wd3T = sb("wd3r", [128, KT, DEC]), sb("wd3T", [128, MC, D])
        b1c, b2c, bd1c, bd2c = sb("b1c", [HID, 1]), sb("b2c", [LAT, 1]), sb("bd1c", [HID, 1]), sb("bd2c", [128, MC])
        bd3b = sb("bd3b", [R, D])
        eps_col = sb("eps_col", [R, 1])
        stats, mean_var = sb("stats", [R, NT, 6]), sb("mean_var", [R, NT, 2])
        rstd, shift = sb("rstd", [R, NT]), sb("shift", [R, NT])
        ones, deg, dinv = sb("ones", [R, 1]), sb("deg", [R, NT]), sb("dinv", [R, NT])
        psd = ctx.enter_context(nc.psum_tensor("ring_dve", [128, 4, 512], F32))
        psa = ctx.enter_context(nc.psum_tensor("ring_act", [128, 4, 512], F32))
        x_loaded, w_loaded, b_loaded = sem("x_loaded"), sem("w_loaded"), sem("b_loaded")
        ones_in, zeroed, ident_in = sem("ones_in"), sem("ident_zeroed"), sem("ident_in")
        stats_done, sqrt_done, rstd_done, h_ready = sem("stats_done"), sem("sqrt_done"), sem("rstd_done"), sem("h_ready")
        d_filled, d_drained = sem("d_filled"), sem("d_drained")
        a_filled, a_drained = sem("a_filled"), sem("a_drained")
        deg_ready, deg_sqrt, dinv_ready = sem("deg_ready"), sem("deg_sqrt"), sem("dinv_ready")
        t_sum, t_ready = sem("t_sum"), sem("t_ready")
        x_biased, x1_ready, x1_stored = sem("x_biased"), sem("x1_ready"), sem("x1_stored")
        log_in, log_done, log_masked = sem("log_in"), sem("log_done"), sem("log_masked")

        a_jobs = {"w": 0}
        a_jobs["t1T"] = 4 + MC
        a_jobs["t2T"] = a_jobs["t1T"] + NT
        a_jobs["y1"] = a_jobs["t2T"] + NT
        a_jobs["y2"] = a_jobs["y1"] + len(CHUNKS)
        a_end = a_jobs["y2"] + MC * len(CHUNKS)
        d_jobs = {"hT": 0, "deg": NT}
        for at, name in enumerate(["hw1", "agg1", "hw2", "agg2", "y3"]):
            d_jobs[name] = NT + 1 + at * NT

        with nc.Block() as block:
            @block.sync
            def _(sp):
                xv = x_in.rearrange("(t p) d -> p t d", p=R)
                for i in range(NT):
                    sp.dma_start(xb[:, i, :], xv[:, i, :]).then_inc(x_loaded, 16)
                sp.dma_start(bd3b[:, :], broadcast_rows(bd3, R)).then_inc(b_loaded, 16)
                sp.dma_start(b1c[:, :], b1.rearrange("(p a) -> p a", a=1)).then_inc(b_loaded, 16)
                sp.dma_start(b2c[:, :], b2.rearrange("(p a) -> p a", a=1)).then_inc(b_loaded, 16)
                sp.dma_start(bd1c[:, :], bd1.rearrange("(p a) -> p a", a=1)).then_inc(b_loaded, 16)
                with nc.allow_non_contiguous_dma(reason="a bias of 256"):
                    sp.dma_start(bd2c[:, :], bd2.rearrange("(m p) -> p m", p=128)).then_inc(b_loaded, 16)
                for i in range(NT):
                    sp.wait_ge(x1_ready, i + 1)
                    sp.dma_start(x_keep.rearrange("(t p) d -> p t d", p=R)[:, i, :], xb[:, i, :])\
                      .then_inc(x1_stored, 16)
                sp.wait_ge(x1_stored, 16 * NT)

            @block.gpsimd
            def _(pool):
                pool.memset(ones[:, :], 1.0).then_inc(ones_in, 1)
                pool.memset(eps_col[:, :], EPS).then_inc(ones_in, 1)
                identity(pool, zeroed, ident_in, ident)
                pool.wait_ge(b_loaded, 80)
                for i in range(NT):
                    pool.wait_ge(h_ready, i + 1)
                    pool.tensor_tensor(xb[:, i, :], xb[:, i, :], bd3b[:, :], ALU.add).then_inc(x_biased, 1)

            @block.vector
            def _(v):
                for i in range(NT):
                    v.wait_ge(x_loaded, 160)
                    row_stats(v, xb, i, stats, mean_var, stats_done, 2 * i)
                v.wait_ge(sqrt_done, 1)
                v.reciprocal(rstd[:, :], rstd[:, :]).then_inc(rstd_done, 1)
                v.wait_ge(rstd_done, 1)
                v.scalar_tensor_tensor(shift[:, :], mean_var[:, :, 0], -1.0, rstd[:, :], ALU.mult,
                                       ALU.mult).then_inc(rstd_done, 1)
                for i in range(NT):
                    v.wait_ge(d_filled, i + 1)
                    v.tensor_copy(hT[:, :, i * R:(i + 1) * R],
                                  psd[:, i % 4, 0:KT * R].rearrange("p (k n) -> p k n", k=KT))\
                        .then_inc(d_drained, 1)
                v.wait_ge(d_filled, NT + 1)
                v.tensor_scalar(deg[:, :], psd[0:R, NT % 4, 0:NT], 1.0, None, ALU.add).then_inc(d_drained, 1)
                v.wait_ge(deg_sqrt, 1)
                v.reciprocal(dinv[:, :], deg[:, :]).then_inc(dinv_ready, 1)
                v.wait_ge(dinv_ready, 1)

                def scale_rows(job, g, width):
                    for i in range(NT):
                        k = d_jobs[job] + i
                        v.wait_ge(d_filled, k + 1)
                        v.tensor_scalar(g[:, i, :], psd[0:R, k % 4, 0:width], dinv[:, i:i + 1], None,
                                        ALU.mult).then_inc(d_drained, 1)

                def aggregate(job, g, t, width):
                    for i in range(NT):
                        k = d_jobs[job] + i
                        v.wait_ge(d_filled, k + 1)
                        v.tensor_tensor(t[:, i, :], psd[0:R, k % 4, 0:width], g[:, i, :], ALU.add)\
                            .then_inc(d_drained, 1)
                        v.wait_ge(d_drained, k + 1)
                        v.tensor_scalar(t[:, i, :], t[:, i, :], dinv[:, i:i + 1], None, ALU.mult)\
                            .then_inc(t_ready, 1)

                scale_rows("hw1", g1, HID)
                for i in range(NT):
                    v.tensor_scalar(logc[:, i, :], counts[:, i, :], 1.0, None, ALU.max).then_inc(log_in, 1)
                aggregate("agg1", g1, t1, HID)
                for i in range(NT):
                    v.tensor_scalar(no_edge, counts[:, i, :], 0.0, NEVER, ALU.is_equal, ALU.mult)\
                        .then_inc(log_masked, 1)
                    v.wait_ge(log_done, i + 1)
                    v.wait_ge(log_masked, 2 * i + 1)
                    v.tensor_tensor_reduce(out=logc[:, i, :], in0=logc[:, i, :], in1=no_edge, scale=1.0,
                                           scalar=NEVER, op0=ALU.add, op1=ALU.max,
                                           accum_out=has_edge[:, i:i + 1]).then_inc(log_masked, 1)
                    v.wait_ge(log_masked, 2 * i + 2)
                v.tensor_scalar(has_edge, has_edge, -1.0, None, ALU.is_gt)
                scale_rows("hw2", g2, LAT)
                aggregate("agg2", g2, t2, LAT)
                for i in range(NT):
                    k = d_jobs["y3"] + i
                    v.wait_ge(d_filled, k + 1)
                    v.wait_ge(x_biased, i + 1)
                    v.tensor_tensor(xb[:, i, :], xb[:, i, :], psd[0:R, k % 4, :], ALU.add)\
                        .then_inc(d_drained, 1)
                    v.wait_ge(d_drained, k + 1)
                    v.bn_stats(stats[:, i, :], xb[:, i, :]).then_inc(x1_ready, 1)
                    v.wait_ge(x1_ready, i + 1)
                    v.bn_aggr(mean_var[:, i, :], stats[:, i, :]).then_inc(stats_done, 1)
                v.wait_ge(sqrt_done, 2)
                v.reciprocal(rstd[:, :], rstd[:, :]).then_inc(rstd_done, 1)
                v.wait_ge(rstd_done, 3)
                v.scalar_tensor_tensor(shift[:, :], mean_var[:, :, 0], -1.0, rstd[:, :], ALU.mult,
                                       ALU.mult).then_inc(rstd_done, 1)

            @block.scalar
            def _(act):
                act.dma_start(w1r[:, :], w1).then_inc(w_loaded, 16)
                act.dma_start(w2r[:, :], w2).then_inc(w_loaded, 16)
                act.dma_start(wd1r[:, :], wd1).then_inc(w_loaded, 16)
                act.dma_start(wd2r[:, :, :], wd2.rearrange("(m p) k -> p m k", p=128)).then_inc(w_loaded, 16)
                act.dma_start(wd3r[:, :, :], wd3.rearrange("(m p) k -> p m k", p=128)).then_inc(w_loaded, 16)

                act.wait_ge(ones_in, 2)

                def root(variance_count):
                    act.wait_ge(stats_done, variance_count)
                    act.activation(rstd[:, :], mean_var[:, :, 1], ACT.Sqrt, bias=eps_col[:, 0:1]).then_inc(sqrt_done, 1)

                def drain(k, out, rows, cols, func=ACT.Copy, bias=0.0):
                    act.wait_ge(a_filled, k + 1)
                    act.activation(out, psa[0:rows, k % 4, 0:cols], func, bias=bias).then_inc(a_drained, 1)

                drain(0, w1T[:, :, :].rearrange("p k m -> p (k m)"), 128, KT * HID)
                drain(1, w2T[:, :], HID, LAT)
                drain(2, wd1T[:, :], LAT, HID)
                drain(3, wd2T[:, :], HID, DEC)
                for c in range(MC):
                    drain(4 + c, wd3T[:, c, :], 128, D)
                root(2 * NT)
                for i in range(NT):
                    if i == 0:
                        act.wait_ge(rstd_done, 2)
                    if i >= 2:
                        act.wait_ge(d_filled, i - 1)
                    act.activation(h[:, i % 2, :], xb[:, i, :], ACT.Relu, bias=shift[:, i:i + 1],
                                   scale=rstd[:, i:i + 1]).then_inc(h_ready, 1)
                act.wait_ge(d_drained, NT + 1)
                act.activation(deg[:, :], deg[:, :], ACT.Sqrt).then_inc(deg_sqrt, 1)
                for i in range(NT):
                    act.wait_ge(log_in, i + 1)
                    act.activation(logc[:, i, :], logc[:, i, :], ACT.Ln).then_inc(log_done, 1)
                act.wait_ge(b_loaded, 80)
                for i in range(NT):
                    drain(a_jobs["t1T"] + i, rT[:, i * R:(i + 1) * R], HID, R, ACT.Relu, b1c[:, 0:1])
                for i in range(NT):
                    drain(a_jobs["t2T"] + i, zT[:, i * R:(i + 1) * R], LAT, R, ACT.Identity, b2c[:, 0:1])
                for c, (at, n) in enumerate(CHUNKS):
                    drain(a_jobs["y1"] + c, y1T[:, at:at + n], HID, n, ACT.Relu, bd1c[:, 0:1])
                for m in range(MC):
                    for c, (at, n) in enumerate(CHUNKS):
                        drain(a_jobs["y2"] + m * len(CHUNKS) + c, y2T[:, m, at:at + n], 128, n, ACT.Relu,
                              bd2c[:, m:m + 1])
                root(3 * NT)
                act.wait_ge(rstd_done, 4)
                for i in range(NT):
                    act.activation(x[:, i, :], xb[:, i, :], ACT.Relu, bias=shift[:, i:i + 1],
                                   scale=rstd[:, i:i + 1])

            @block.tensor
            def _(pe):
                def free_a(k):
                    if k >= 4:
                        pe.wait_ge(a_drained, k - 3)

                def free_d(k):
                    if k >= 4:
                        pe.wait_ge(d_drained, k - 3)

                pe.wait_ge(w_loaded, 80)
                pe.wait_ge(ident_in, 1)
                for k in range(KT):
                    last = pe.transpose(psa[:, 0, k * 128:k * 128 + HID], w1r[:, k * 128:(k + 1) * 128],
                                        ident[0:HID, 0:HID])
                last.then_inc(a_filled, 1)
                pe.transpose(psa[0:HID, 1, 0:LAT], w2r[:, :], ident[0:LAT, 0:LAT]).then_inc(a_filled, 1)
                pe.transpose(psa[0:LAT, 2, 0:HID], wd1r[:, :], ident[0:HID, 0:HID]).then_inc(a_filled, 1)
                for m in range(MC):
                    last = pe.transpose(psa[0:HID, 3, m * 128:(m + 1) * 128], wd2r[:, m, :], ident)
                last.then_inc(a_filled, 1)
                for c in range(MC):
                    free_a(4 + c)
                    for m in range(KT):
                        last = pe.transpose(psa[:, (4 + c) % 4, m * 128:(m + 1) * 128],
                                            wd3r[:, m, c * 128:(c + 1) * 128], ident)
                    last.then_inc(a_filled, 1)
                pe.wait_ge(ones_in, 2)
                for i in range(NT):
                    free_d(i)
                    pe.wait_ge(h_ready, i + 1)
                    for k in range(KT):
                        last = pe.transpose(psd[:, i % 4, k * R:(k + 1) * R],
                                            h[:, i % 2, k * 128:(k + 1) * 128], ident[0:R, 0:R])
                    last.then_inc(d_filled, 1)
                free_d(NT)
                for i in range(NT):
                    for s in range(NT):
                        last = pe.matmul(psd[0:R, NT % 4, i:i + 1], counts[:, s, i * R:(i + 1) * R], ones[:, :],
                                         start=(s == 0), stop=(s == NT - 1))
                last.then_inc(d_filled, 1)
                pe.wait_ge(d_drained, NT)
                pe.wait_ge(a_drained, 1)

                def rows(job, srcT, w, width, tiles):
                    for i in range(NT):
                        k = d_jobs[job] + i
                        free_d(k)
                        for c in range(tiles):
                            last = pe.matmul(psd[0:R, k % 4, 0:width], srcT(c)[:, i * R:(i + 1) * R], w(c),
                                             start=(c == 0), stop=(c == tiles - 1))
                        last.then_inc(d_filled, 1)

                def neighbours(job, g, width):
                    for i in range(NT):
                        k = d_jobs[job] + i
                        free_d(k)
                        for s in range(NT):
                            last = pe.matmul(psd[0:R, k % 4, 0:width], counts[:, s, i * R:(i + 1) * R],
                                             g[:, s, :], start=(s == 0), stop=(s == NT - 1))
                        last.then_inc(d_filled, 1)

                def transposes(job, t, width, ready):
                    for i in range(NT):
                        k = a_jobs[job] + i
                        free_a(k)
                        pe.wait_ge(t_ready, ready + i + 1)
                        pe.transpose(psa[0:width, k % 4, 0:R], t[:, i, :], ident[0:R, 0:R])\
                            .then_inc(a_filled, 1)

                rows("hw1", lambda c: hT[:, c, :], lambda c: w1T[:, c, :], HID, KT)
                pe.wait_ge(d_drained, d_jobs["hw1"] + NT)
                neighbours("agg1", g1, HID)
                transposes("t1T", t1, HID, 0)
                pe.wait_ge(a_drained, a_jobs["t1T"] + NT)
                rows("hw2", lambda c: rT[:, :], lambda c: w2T[:, :], LAT, 1)
                pe.wait_ge(d_drained, d_jobs["hw2"] + NT)
                neighbours("agg2", g2, LAT)
                transposes("t2T", t2, LAT, NT)
                pe.wait_ge(a_drained, a_jobs["t2T"] + NT)
                for c, (at, n) in enumerate(CHUNKS):
                    k = a_jobs["y1"] + c
                    free_a(k)
                    pe.matmul(psa[:, k % 4, 0:n], wd1T[:, :], zT[:, at:at + n], start=True, stop=True)\
                        .then_inc(a_filled, 1)
                pe.wait_ge(a_drained, a_jobs["y2"])
                for m in range(MC):
                    for c, (at, n) in enumerate(CHUNKS):
                        k = a_jobs["y2"] + m * len(CHUNKS) + c
                        free_a(k)
                        pe.matmul(psa[:, k % 4, 0:n], wd2T[:, m * 128:(m + 1) * 128], y1T[:, at:at + n],
                                  start=True, stop=True).then_inc(a_filled, 1)
                pe.wait_ge(a_drained, a_end)
                rows("y3", lambda c: y2T[:, c, :], lambda c: wd3T[:, c, :], D, MC)


HALF_NT = NT // 2
HEAD_USES = {"A": 9, "B": 8, "T": 3 * NT, "V": HALF_NT}
MLP_USES = {"A": 4, "B": 4, "T": 0, "V": 0}
BLOCK_USES = {s: 2 * HALF_NT + HEADS * HEAD_USES[s] + MLP_USES[s] for s in "ABTV"}
OUT_BATCHES = [("A", (0, 1, 2)), ("B", (3, 4, 5)), ("A", (6, 7, 8)), ("B", (9,))]


def in_ln1(s, b, u):
    return b * BLOCK_USES[s] + u


def in_head(s, b, h, u):
    return b * BLOCK_USES[s] + h * HEAD_USES[s] + (HALF_NT + u)


def in_ln2(s, b, u):
    return b * BLOCK_USES[s] + (HALF_NT + HEADS * HEAD_USES[s] + u)


def in_mlp(s, b, u):
    return b * BLOCK_USES[s] + (2 * HALF_NT + HEADS * HEAD_USES[s] + u)


def transformer(nc, noise, p, x_keep, out, x, logc, has_edge, ident):
    ctx = ExitStack()
    with ctx:
        def sb(name, shape, dt=F32):
            return ctx.enter_context(nc.sbuf_tensor("c_" + name, shape, dt))

        def sem(name):
            return ctx.enter_context(nc.semaphore("c_" + name))

        yT_rows = sb("yT", [128, NT * D])
        yT = yT_rows[:, 0:KT * N].rearrange("p (k n) -> p k n", k=KT)
        x1 = yT_rows[0:R, :].rearrange("p (t d) -> p t d", t=NT)
        probsT = sb("probsT", [128, 2, NT, 2 * R])
        upT = probsT[:, :, :, :].rearrange("p a b c -> p (a b c)").rearrange("p (k n) -> p k n", k=KT)
        probs = sb("probs", [R, 2, N])
        q, k_, v_ = sb("q", [DH, N]), sb("k", [DH, N]), sb("v", [R, NT, DH])
        oT = sb("oT", [DH, N])
        wq, wk, wv = sb("wq", [128, KT, DH]), sb("wk", [128, KT, DH]), sb("wv", [128, KT, DH])
        wo = sb("wo", [DH, D])
        w1, w2 = sb("w1", [128, KT, D]), sb("w2", [128, KT, D])
        sw1, bw1, sw2, bw2 = (sb(n, [NOISE + 1, D]) for n in ("sw1", "bw1", "sw2", "bw2"))
        bq, bk, bv = sb("bq", [DH, 1]), sb("bk", [DH, 1]), sb("bv", [R, DH])
        bo, mb1, mb2 = sb("bo", [R, D]), sb("mb1", [128, KT]), sb("mb2", [R, D])
        cond = sb("cond", [32, N])
        xn, y = sb("xn", [R, 2, D]), sb("y", [R, 2, D])
        stats, mean_var = sb("stats", [R, NT, 6]), sb("mean_var", [R, NT, 2])
        rstd, shift, eps_col = sb("rstd", [R, NT]), sb("shift", [R, NT]), sb("eps_col", [R, 1])
        row_max, neg_max = sb("row_max", [R, NT]), sb("neg_max", [R, NT])
        row_sum, inv_sum = sb("row_sum", [R, NT]), sb("inv_sum", [R, NT])

        slot = {"A": ctx.enter_context(nc.psum_tensor("slot_A", [128, 3 * 512], F32)),
                "B": ctx.enter_context(nc.psum_tensor("slot_B", [128, 3 * 512], F32)),
                "T": ctx.enter_context(nc.psum_tensor("slot_T", [128, 512], F32)),
                "V": ctx.enter_context(nc.psum_tensor("slot_V", [128, 512], F32))}
        filled = {s: sem(f"slot_{s}_filled") for s in "ABTV"}
        drained = {s: sem(f"slot_{s}_drained") for s in "ABTV"}
        ln_w_in, head_w_in, wo_in, mlp_w_in = sem("ln_w_in"), sem("head_w_in"), sem("wo_in"), sem("mlp_w_in")
        stats_done, rstd_ready = sem("stats_done"), sem("rstd_ready")
        root_done, xn_ready, x_biased, scaled = sem("root_done"), sem("xn_ready"), sem("x_biased"), sem("scaled")
        y_ready = sem("y_ready")
        max_ready, probs_ready, inv_ready = sem("max_ready"), sem("probs_ready"), sem("inv_ready")
        x1_in, sum_ready, stored = sem("x1_in"), sem("sum_ready"), sem("stored")

        waits_passed = {nc.vector: sem("dve_waits_passed"), nc.sync: sem("sp_waits_passed")}

        def apart(engine):
            engine.sem_inc(waits_passed[engine], 1)

        embed_noise(nc, ctx, noise, p, cond, eps_col, slot, probs, q)

        with nc.Block() as block:
            @block.sync
            def _(sp):
                def head_weights(b, h):
                    of_head = [(wq, p["wq"]), (wk, p["wk"]), (wv, p["wv"])]
                    for t, w in of_head:
                        w = w.rearrange("b (k p) (h c) -> b h p k c", p=128, h=HEADS)
                        sp.dma_start(t[:, :, :], w[b, h]).then_inc(head_w_in, 16)
                    for t, w in ((bq, p["bq"]), (bk, p["bk"])):
                        w = w.rearrange("b (h c) -> (b h) c", h=HEADS)
                        sp.dma_start(t[:, :], w[bass.ds(b * HEADS + h, 1)].rearrange("a c -> c a"))\
                            .then_inc(head_w_in, 16)
                    w = p["bv"].rearrange("b (h c) -> (b h) c", h=HEADS)[bass.ds(b * HEADS + h, 1)]
                    sp.dma_start(bv[:, :], w.to_broadcast([R, DH])).then_inc(head_w_in, 16)

                def head_output_weights(b, h):
                    w = p["wo"].rearrange("b (h c) n -> (b h) c n", h=HEADS)[bass.ds(b * HEADS + h, 1)]
                    sp.dma_start(wo[:, :], w.rearrange("a c n -> (a c) n")).then_inc(wo_in, 16)

                with sp.Fori(0, BLOCKS) as b:
                    for s in "AB":
                        sp.wait_ge(drained[s], b * BLOCK_USES[s] + 1)
                        apart(sp)
                    for t, w, bias in ((sw1, "s1_w", "s1_b"), (bw1, "b1_w", "b1_b"),
                                       (sw2, "s2_w", "s2_b"), (bw2, "b2_w", "b2_b")):
                        sp.dma_start(t[0:NOISE, :], p[w][b]).then_inc(ln_w_in, 16)
                        sp.dma_start(t[NOISE:NOISE + 1, :], p[bias][bass.ds(b, 1)]).then_inc(ln_w_in, 16)
                    for t, w in ((bo, "bo"), (mb2, "m_b2")):
                        sp.dma_start(t[:, :], p[w][bass.ds(b, 1)].to_broadcast([R, D])).then_inc(ln_w_in, 16)
                    head_weights(b, 0)
                    head_output_weights(b, 0)
                    for t, w in ((w1, "m_w1"), (w2, "m_w2")):
                        sp.dma_start(t[:, :, :], p[w].rearrange("b (k p) n -> b p k n", p=128)[b])\
                            .then_inc(mlp_w_in, 16)
                    with nc.allow_non_contiguous_dma(reason="a bias of 512 by columns"):
                        sp.dma_start(mb1[:, :], p["m_b1"].rearrange("b (k p) -> b p k", p=128)[b])\
                            .then_inc(mlp_w_in, 16)
                    with sp.Fori(1, HEADS) as h:
                        sp.wait_ge(drained["A"], in_head("A", b, h, 2 - HEAD_USES["A"]) + 1)
                        apart(sp)
                        sp.wait_ge(drained["B"], in_head("B", b, h, 1 - HEAD_USES["B"]) + 1)
                        apart(sp)
                        head_weights(b, h)
                        sp.wait_ge(filled["B"], in_head("B", b, h, 0))
                        apart(sp)
                        head_output_weights(b, h)
                sp.wait_ge(filled["B"], BLOCKS * BLOCK_USES["B"])
                sp.wait_ge(filled["A"], BLOCKS * BLOCK_USES["A"])
                sp.dma_start(x1, x_keep.rearrange("(t p) d -> p t d", p=R)).then_inc(x1_in, 16)
                outv = out.rearrange("(t p) d -> p t d", p=R)
                for i in range(NT):
                    sp.wait_ge(sum_ready, i + 1)
                    sp.dma_start(outv[:, i, :], x[:, i, :]).then_inc(stored, 16)
                sp.wait_ge(stored, 16 * NT)

            @block.gpsimd
            def _(pool):
                for s in "ABTV":
                    pool.sem_inc(drained[s], 1)
                with pool.Fori(0, BLOCKS) as b:
                    pool.wait_ge(ln_w_in, b * 160 + 160)
                    for ln, bias in enumerate((bo, mb2)):
                        for i in range(NT):
                            pool.wait_ge(xn_ready, b * 2 * NT + (ln * NT + i + 1))
                            pool.tensor_tensor(x[:, i, :], x[:, i, :], bias[:, :], ALU.add)\
                                .then_inc(x_biased, 1)

            @block.vector
            def _(v):
                def modulate(b, ln, at):
                    for s in "AB":
                        v.wait_ge(drained[s], at(s, b, 0) + 1)
                    for i in range(NT):
                        last = v.bn_stats(stats[:, i, :], x[:, i, :])
                    last.then_inc(stats_done, 1)
                    v.wait_ge(stats_done, b * 4 + (2 * ln + 1))
                    apart(v)
                    for i in range(NT):
                        last = v.bn_aggr(mean_var[:, i, :], stats[:, i, :])
                    last.then_inc(stats_done, 1)
                    v.wait_ge(root_done, b * 2 + (ln + 1))
                    v.reciprocal(rstd[:, :], rstd[:, :]).then_inc(rstd_ready, 1)
                    v.wait_ge(rstd_ready, b * 4 + (2 * ln + 1))
                    v.scalar_tensor_tensor(shift[:, :], mean_var[:, :, 0], -1.0, rstd[:, :], ALU.mult,
                                           ALU.mult).then_inc(rstd_ready, 1)
                    for i in range(NT):
                        s = "AB"[i % 2]
                        t = b * 2 * NT + (ln * NT + i)
                        v.wait_ge(filled[s], at(s, b, i // 2) + 1)
                        v.wait_ge(xn_ready, t + 1)
                        if i >= 2:
                            v.wait_ge(filled["TV"[i % 2]], at("TV"[i % 2], b, i // 2 - 1) + 1)
                        v.scalar_tensor_tensor(y[:, i % 2, :], slot[s][0:R, 0:D], 1.0, xn[:, i % 2, :],
                                               ALU.add, ALU.mult).then_inc(scaled, 1)
                        v.wait_ge(scaled, t + 1)
                        v.tensor_tensor(y[:, i % 2, :], y[:, i % 2, :], slot[s][0:R, 512:512 + D], ALU.add)\
                            .then_inc(drained[s], 1)

                def scores(b, h, i):
                    s, u = ("B", 1 + i // 2) if i % 2 == 0 else ("A", 2 + i // 2)
                    n = b * HEADS * NT + h * NT + i
                    v.wait_ge(filled[s], in_head(s, b, h, u) + 1)
                    if i >= 2:
                        v.wait_ge(filled["T"], in_head("T", b, h, 3 * (i - 1)))
                    apart(v)
                    v.tensor_tensor_reduce(out=probs[:, i % 2, :], in0=slot[s][0:R, 0:N], in1=logc[:, i, :],
                                           scale=1.0, scalar=3 * NEVER, op0=ALU.add, op1=ALU.max,
                                           accum_out=row_max[:, i:i + 1]).then_inc(drained[s], 1)
                    v.wait_ge(drained[s], in_head(s, b, h, u) + 2)
                    v.tensor_scalar(neg_max[:, i:i + 1], row_max[:, i:i + 1], -1.0, None, ALU.mult)\
                        .then_inc(max_ready, 1)

                def transposed(b, h, i):
                    v.wait_ge(filled["T"], in_head("T", b, h, 3 * i + 1) + 1)
                    if i % 2 == 0 and i >= 4:
                        v.wait_ge(filled["V"], in_head("V", b, h, i // 2 - 2) + 1)
                    v.tensor_copy(probsT[0:R, i // 2 % 2, 4:8, i % 2 * R:(i % 2 + 1) * R],
                                  slot["T"][0:R, 0:4 * R].rearrange("p (j n) -> p j n", j=4))\
                        .then_inc(drained["T"], 1)

                def add_tiles(at, scale):
                    for s, tiles in OUT_BATCHES:
                        u = at[s]
                        at[s] = u + 1
                        v.wait_ge(filled[s], u + 1)
                        for c, i in enumerate(tiles):
                            ps = slot[s][0:R, c * 512:c * 512 + D]
                            if scale:
                                last = v.scalar_tensor_tensor(x[:, i, :], ps, inv_sum[:, i:i + 1], x[:, i, :],
                                                              ALU.mult, ALU.add)
                            else:
                                last = v.tensor_tensor(x[:, i, :], x[:, i, :], ps, ALU.add)
                        last.then_inc(drained[s], 1)

                with v.Fori(0, BLOCKS) as b:
                    modulate(b, 0, in_ln1)
                    with v.Fori(0, HEADS) as h:
                        n = b * HEADS + h
                        v.wait_ge(filled["A"], in_head("A", b, h, 0) + 1)
                        v.tensor_scalar(q[:, :], slot["A"][:, 0:N], bq[:, 0:1], QSCALE, ALU.add, ALU.mult)\
                            .then_inc(drained["A"], 1)
                        v.wait_ge(filled["A"], in_head("A", b, h, 1) + 1)
                        v.tensor_tensor(v_[:, :, :], slot["A"][0:R, 0:NT * DH].rearrange("p (t c) -> p t c", c=DH),
                                        bv[:, :].unsqueeze(1).to_broadcast([R, NT, DH]), ALU.add)\
                            .then_inc(drained["A"], 1)
                        scores(b, h, 0)
                        for i in range(NT):
                            if i + 1 < NT:
                                scores(b, h, i + 1)
                            transposed(b, h, i)
                        v.wait_ge(probs_ready, n * NT + NT)
                        v.reciprocal(inv_sum[:, :], row_sum[:, :]).then_inc(inv_ready, 1)
                        v.wait_ge(inv_ready, 2 * n + 1)
                        v.tensor_tensor(inv_sum[:, :], inv_sum[:, :], has_edge, ALU.mult).then_inc(inv_ready, 1)
                        v.wait_ge(inv_ready, 2 * n + 2)
                        v.wait_ge(x_biased, b * 2 * NT + NT)
                        add_tiles({"A": in_head("A", b, h, 7), "B": in_head("B", b, h, 6)}, True)
                    modulate(b, 1, in_ln2)
                    v.wait_ge(x_biased, b * 2 * NT + 2 * NT)
                    add_tiles({"A": in_mlp("A", b, 2), "B": in_mlp("B", b, 2)}, False)
                for s in "AB":
                    v.wait_ge(drained[s], BLOCKS * BLOCK_USES[s] + 1)
                v.wait_ge(x1_in, 16)
                for i in range(NT):
                    v.tensor_tensor(x[:, i, :], x[:, i, :], x1[:, i, :], ALU.add).then_inc(sum_ready, 1)

            @block.scalar
            def _(act):
                def norm(b, ln, at):
                    act.wait_ge(stats_done, b * 4 + (2 * ln + 2))
                    act.activation(rstd[:, :], mean_var[:, :, 1], ACT.Sqrt, bias=eps_col[:, 0:1])\
                        .then_inc(root_done, 1)
                    act.wait_ge(rstd_ready, b * 4 + (2 * ln + 2))

                    def drain(i):
                        s = "TV"[i % 2]
                        act.wait_ge(filled[s], at(s, b, i // 2) + 1)
                        act.activation(yT[:, :, i * R:(i + 1) * R],
                                       slot[s][:, 0:KT * R].rearrange("p (k n) -> p k n", k=KT), ACT.Copy)\
                            .then_inc(drained[s], 1)

                    for i in range(NT):
                        if i >= 2:
                            act.wait_ge(scaled, b * 2 * NT + (ln * NT + i - 1))
                        act.activation(xn[:, i % 2, :], x[:, i, :], ACT.Identity, bias=shift[:, i:i + 1],
                                       scale=rstd[:, i:i + 1]).then_inc(xn_ready, 1)
                        if i >= 2:
                            drain(i - 2)
                    drain(NT - 2)
                    drain(NT - 1)

                def exponentials(b, h, i):
                    n = b * HEADS * NT + h * NT + i
                    act.wait_ge(max_ready, n + 1)
                    act.activation(probs[:, i % 2, :], probs[:, i % 2, :], ACT.Exp, bias=neg_max[:, i:i + 1],
                                   accum_out=row_sum[:, i:i + 1]).then_inc(probs_ready, 1)

                def transposed(b, h, i, f, j, m):
                    act.wait_ge(filled["T"], in_head("T", b, h, 3 * i + f) + 1)
                    if f == 0 and i % 2 == 0 and i >= 4:
                        act.wait_ge(filled["V"], in_head("V", b, h, i // 2 - 2) + 1)
                    act.activation(probsT[0:R, i // 2 % 2, j:j + m, i % 2 * R:(i % 2 + 1) * R],
                                   slot["T"][0:R, 0:m * R].rearrange("p (j n) -> p j n", j=m), ACT.Copy)\
                        .then_inc(drained["T"], 1)

                def head_out(b, h, g):
                    act.wait_ge(filled["V"], in_head("V", b, h, g) + 1)
                    act.activation(oT[:, g * 2 * R:(g + 1) * 2 * R], slot["V"][:, 0:2 * R], ACT.Copy)\
                        .then_inc(drained["V"], 1)

                with act.Fori(0, BLOCKS) as b:
                    norm(b, 0, in_ln1)
                    with act.Fori(0, HEADS) as h:
                        act.wait_ge(filled["B"], in_head("B", b, h, 0) + 1)
                        act.activation(k_[:, :], slot["B"][:, 0:N], ACT.Identity, bias=bk[:, 0:1])\
                            .then_inc(drained["B"], 1)
                        exponentials(b, h, 0)
                        for i in range(NT):
                            transposed(b, h, i, 0, 0, 4)
                            if i + 1 < NT:
                                exponentials(b, h, i + 1)
                            transposed(b, h, i, 2, 8, 2)
                            if i % 2 == 1 and i >= 3:
                                head_out(b, h, i // 2 - 1)
                        head_out(b, h, HALF_NT - 1)
                    norm(b, 1, in_ln2)
                    act.wait_ge(mlp_w_in, b * 48 + 48)
                    for m in range(KT):
                        s = "AB"[m % 2]
                        act.wait_ge(filled[s], in_mlp(s, b, m // 2) + 1)
                        act.activation(upT[:, m, :], slot[s][:, 0:N], ACT.Relu, bias=mb1[:, m:m + 1])\
                            .then_inc(drained[s], 1)

            @block.tensor
            def _(pe):
                def free(s, u):
                    pe.wait_ge(drained[s], u + 1)

                def norm(b, ln, at, sw, bw):
                    pe.wait_ge(ln_w_in, b * 160 + 160)

                    def transposes(i):
                        s = "AB"[i % 2]
                        t = "TV"[i % 2]
                        pe.wait_ge(drained[s], at(s, b, i // 2) + 2)
                        free(t, at(t, b, i // 2))
                        for k in range(KT):
                            last = pe.transpose(slot[t][:, k * R:(k + 1) * R],
                                                y[:, i % 2, k * 128:(k + 1) * 128], ident[0:R, 0:R])
                        last.then_inc(filled[t], 1)

                    for i in range(NT):
                        s = "AB"[i % 2]
                        free(s, at(s, b, i // 2))
                        rows = cond[0:NOISE + 1, i * R:(i + 1) * R]
                        pe.matmul(slot[s][0:R, 0:D], rows, sw[:, :], start=True, stop=True)
                        pe.matmul(slot[s][0:R, 512:512 + D], rows, bw[:, :], start=True, stop=True)\
                            .then_inc(filled[s], 1)
                        if i >= 1:
                            transposes(i - 1)
                    transposes(NT - 1)

                def yT_whole(b, at):
                    for s in "TV":
                        pe.wait_ge(drained[s], at(s, b, HALF_NT) + 1)

                def wide(s, w, src):
                    for k in range(KT):
                        for at, n in CHUNKS:
                            last = pe.matmul(slot[s][:, at:at + n], w(k), src(k)[:, at:at + n],
                                             start=(k == 0), stop=(k == KT - 1))
                    last.then_inc(filled[s], 1)

                def scores(b, h, i, c):
                    s, u = ("B", 1 + i // 2) if i % 2 == 0 else ("A", 2 + i // 2)
                    at, n = CHUNKS[c]
                    if c == 0:
                        free(s, in_head(s, b, h, u))
                    last = pe.matmul(slot[s][0:R, at:at + n], q[:, i * R:(i + 1) * R], k_[:, at:at + n],
                                     start=True, stop=True)
                    if c == len(CHUNKS) - 1:
                        last.then_inc(filled[s], 1)

                def transposes(b, h, i, f):
                    free("T", in_head("T", b, h, 3 * i + f))
                    for c, j in enumerate(range(4 * f, min(4 * f + 4, NT))):
                        last = pe.transpose(slot["T"][0:R, c * R:(c + 1) * R],
                                            probs[:, i % 2, j * R:(j + 1) * R], ident[0:R, 0:R])
                    last.then_inc(filled["T"], 1)

                def head_out(b, h, g):
                    pe.wait_ge(drained["T"], in_head("T", b, h, 6 * g + 6) + 1)
                    free("V", in_head("V", b, h, g))
                    for j in range(NT):
                        last = pe.matmul(slot["V"][:, 0:2 * R], v_[:, j, :], probsT[0:R, g % 2, j, :],
                                         start=(j == 0), stop=(j == NT - 1))
                    last.then_inc(filled["V"], 1)

                def row_tiles(at, tile):
                    for s, tiles in OUT_BATCHES:
                        u = at[s]
                        at[s] = u + 1
                        free(s, u)
                        for c, i in enumerate(tiles):
                            last = tile(slot[s][0:R, c * 512:c * 512 + D], i)
                        last.then_inc(filled[s], 1)

                def out_tile(ps, i):
                    return pe.matmul(ps, oT[:, i * R:(i + 1) * R], wo[:, :], start=True, stop=True)

                def down_tile(ps, i):
                    for k in range(KT):
                        last = pe.matmul(ps, upT[:, k, i * R:(i + 1) * R], w2[:, k, :],
                                         start=(k == 0), stop=(k == KT - 1))
                    return last

                with pe.Fori(0, BLOCKS) as b:
                    norm(b, 0, in_ln1, sw1, bw1)
                    with pe.Fori(0, HEADS) as h:
                        n = b * HEADS + h
                        pe.wait_ge(head_w_in, n * 96 + 96)
                        yT_whole(b, in_ln1)
                        for s, w in (("A", wq), ("B", wk)):
                            free(s, in_head(s, b, h, 0))
                            wide(s, lambda k: w[:, k, :], lambda k: yT[:, k, :])
                        free("A", in_head("A", b, h, 1))
                        for i in range(NT):
                            for k in range(KT):
                                last = pe.matmul(slot["A"][0:R, i * DH:(i + 1) * DH], yT[:, k, i * R:(i + 1) * R],
                                                 wv[:, k, :], start=(k == 0), stop=(k == KT - 1))
                        last.then_inc(filled["A"], 1)
                        pe.wait_ge(drained["A"], in_head("A", b, h, 1) + 1)
                        for i in range(2):
                            for c in range(3):
                                scores(b, h, i, c)
                        for i in range(NT):
                            pe.wait_ge(probs_ready, n * NT + (i + 1))
                            for f in range(3):
                                transposes(b, h, i, f)
                                if i + 2 < NT:
                                    scores(b, h, i + 2, f)
                            if i % 2 == 1 and i >= 3:
                                head_out(b, h, i // 2 - 1)
                        head_out(b, h, HALF_NT - 1)
                        pe.wait_ge(drained["V"], in_head("V", b, h, HALF_NT) + 1)
                        pe.wait_ge(wo_in, n * 16 + 16)
                        row_tiles({"A": in_head("A", b, h, 7), "B": in_head("B", b, h, 6)}, out_tile)
                    norm(b, 1, in_ln2, sw2, bw2)
                    pe.wait_ge(mlp_w_in, b * 48 + 48)
                    yT_whole(b, in_ln2)
                    for m in range(KT):
                        s = "AB"[m % 2]
                        free(s, in_mlp(s, b, m // 2))
                        wide(s, lambda k: w1[:, k, m * 128:(m + 1) * 128], lambda k: yT[:, k, :])
                    for s in "AB":
                        pe.wait_ge(drained[s], in_mlp(s, b, 2) + 1)
                    row_tiles({"A": in_mlp("A", b, 2), "B": in_mlp("B", b, 2)}, down_tile)


def embed_noise(nc, ctx_out, noise, p, cond, eps_col, slot, probs, q):
    ctx = ExitStack()
    with ctx:
        def sb(name, shape, dt=F32):
            return ctx.enter_context(nc.sbuf_tensor(name, shape, dt))

        def sem(name):
            return ctx.enter_context(nc.semaphore(name))

        F2 = 2 * NFREQ
        ph, turns = probs[0:F2, 0, :], probs[0:F2, 1, :]
        turns_i = q[0:F2, :].bitcast(I32)
        e = q[0:NOISE, :]
        freq, offset, start = sb("freq", [F2, 1]), sb("offset", [F2, 1]), sb("start", [F2, 1])
        fw1, fb1, fw2, fb2 = sb("fw1", [F2, NOISE]), sb("fb1", [NOISE, 1]), sb("fw2", [NOISE, NOISE]), sb("fb2", [NOISE, 1])
        neg_fb1 = sb("neg_fb1", [NOISE, 1])
        loaded, consts, step = sem("cond_loaded"), sem("cond_consts"), sem("cond_step")
        sin_done, z_done, e_done, silu_done, c_done = (sem(n) for n in ("sin_done", "z_done", "e_done", "silu_done", "c_done"))
        with nc.Block() as block:
            @block.sync
            def _(sp):
                sp.dma_start(ph, broadcast_rows(noise.rearrange("n a -> (n a)"), F2)).then_inc(loaded, 16)
                sp.dma_start(fw1[:, :], p["f_w1"]).then_inc(loaded, 16)
                sp.dma_start(fw2[:, :], p["f_w2"]).then_inc(loaded, 16)
                sp.dma_start(fb1[:, :], p["f_b1"].rearrange("(p a) -> p a", a=1)).then_inc(loaded, 16)
                sp.dma_start(fb2[:, :], p["f_b2"].rearrange("(p a) -> p a", a=1)).then_inc(loaded, 16)

            @block.gpsimd
            def _(pool):
                for half in range(2):
                    at = slice(half * NFREQ, (half + 1) * NFREQ)
                    pool.iota(freq[at, :], pattern=[[0, 1]], base=1, channel_multiplier=1,
                              allow_small_or_imprecise_dtypes=True).then_inc(consts, 1)
                    pool.memset(offset[at, :], 0.25 * half).then_inc(consts, 1)
                    pool.memset(start[at, :], float(np.pi / 2) * half).then_inc(consts, 1)
                    pool.wait_ge(consts, 3 * half + 3)
                pool.memset(eps_col[:, :], EPS).then_inc(consts, 1)
                pool.memset(cond[:, :], 1.0).then_inc(consts, 1)

            @block.vector
            def _(v):
                n = [0]

                def link(instruction):
                    n[0] += 1
                    instruction.then_inc(step, 1)
                    v.wait_ge(step, n[0])

                v.wait_ge(consts, 8)
                v.wait_ge(loaded, 80)
                link(v.tensor_scalar(freq[:, :], freq[:, :], float(np.float32(TWO_PI / 16)), None, ALU.mult))
                link(v.tensor_scalar(ph, ph, freq[:, 0:1], None, ALU.mult))
                link(v.tensor_scalar(turns, ph, float(1 / TWO_PI), offset[:, 0:1], ALU.mult, ALU.add))
                link(v.tensor_copy(turns_i, turns))
                link(v.tensor_copy(turns, turns_i))
                for part in (PI_A, PI_B, PI_C):
                    link(v.scalar_tensor_tensor(ph, turns, -part, ph, ALU.mult, ALU.add))
                link(v.tensor_scalar(ph, ph, start[:, 0:1], None, ALU.add))
                link(v.tensor_scalar(ph, ph, PI_MAX, -PI_MAX, ALU.min, ALU.max))
                link(v.tensor_scalar(neg_fb1[:, :], fb1[:, :], -1.0, None, ALU.mult))
                v.wait_ge(e_done, 1)
                link(v.tensor_scalar(e, e, 1.0, None, ALU.add))
                link(v.reciprocal(e, e))
                v.scalar_tensor_tensor(e, slot["A"][0:NOISE, 0:N], fb1[:, 0:1], e, ALU.add, ALU.mult)\
                    .then_inc(silu_done, 1)
                v.wait_ge(c_done, 1)
                v.tensor_scalar(cond[0:NOISE, :], slot["B"][0:NOISE, 0:N], fb2[:, 0:1], None, ALU.add)

            @block.scalar
            def _(act):
                act.wait_ge(step, 11)
                act.activation(ph, ph, ACT.Sin).then_inc(sin_done, 1)
                act.wait_ge(z_done, 1)
                act.activation(e, slot["A"][0:NOISE, 0:N], ACT.Exp, bias=neg_fb1[:, 0:1], scale=-1.0)\
                    .then_inc(e_done, 1)

            @block.tensor
            def _(pe):
                pe.wait_ge(loaded, 80)
                for w, src, ps, before, after in ((fw1, ph, slot["A"], sin_done, z_done),
                                                  (fw2, e, slot["B"], silu_done, c_done)):
                    pe.wait_ge(before, 1)
                    for at, m in CHUNKS:
                        last = pe.matmul(ps[0:NOISE, at:at + m], w[:, :], src[:, at:at + m], start=True, stop=True)
                    last.then_inc(after, 1)


PARAMS = ["f_w1", "f_b1", "f_w2", "f_b2", "s1_w", "s1_b", "b1_w", "b1_b", "wq", "bq", "wk", "bk", "wv", "bv",
          "wo", "bo", "s2_w", "s2_b", "b2_w", "b2_b", "m_w1", "m_b1", "m_w2", "m_b2"]
GCN_PARAMS = ["W1", "b1", "W2", "b2", "Wd1", "bd1", "Wd2", "bd2", "Wd3", "bd3"]


def build(nc, ap, out):
    x_keep = nc.dram_tensor("x1_keep", [N, D], F32, kind="Internal").ap()
    ctx = ExitStack()
    with ctx:
        def sb(name, shape, dt=F32):
            return ctx.enter_context(nc.sbuf_tensor(name, shape, dt))

        ident = sb("ident", [128, 128])
        x = sb("x", [R, NT, D])
        logc = sb("logc", [R, NT, N])
        has_edge = sb("has_edge", [R, NT])
        with nc.sbuf_tensor("counts", [R, NT, N], F32) as counts:
            onehot_a = logc[:, :, :].rearrange("p t n -> p (t n)")[:, 0:GT * N // 2].bitcast(BF16)\
                .rearrange("p (t n) -> p t n", t=GT)
            count_edges(nc, ap["src"], ap["dst"], counts[:, :, :], onehot_a,
                        x[:, :, :].rearrange("p t d -> p (t d)"))
            gcn_layer(nc, ap["x"], *(ap["L0_gnn_" + n] for n in GCN_PARAMS), x_keep, x[:, :, :],
                      counts[:, :, :], logc[:, :, :], has_edge[:, :], ident[:, :])
        transformer(nc, ap["node_vec1"], {n: ap["L1_gnn_" + n] for n in PARAMS}, x_keep, out,
                    x[:, :, :], logc[:, :, :], has_edge[:, :], ident[:, :])


INPUTS = ["x", "src", "dst", "node_vec1"] + ["L0_gnn_" + n for n in GCN_PARAMS] + ["L1_gnn_" + n for n in PARAMS]


def kernel(**inputs):
    import concourse.bacc as bacc
    from concourse.bass_utils import run_bass_kernel_spmd

    nc = bacc.Bacc("TRN2", target_bir_lowering=False, num_devices=1)
    arrays, ap = {}, {}
    for name in INPUTS:
        a = np.ascontiguousarray(inputs[name])
        arrays[f"in_{name}_dram"] = a
        ap[name] = nc.dram_tensor(f"in_{name}_dram", a.shape, mybir.dt.from_np(a.dtype), kind="ExternalInput").ap()
    out = nc.dram_tensor("out_0_dram", (N, D), F32, kind="ExternalOutput").ap()
    build(nc, ap, out)
    r = run_bass_kernel_spmd(nc, [arrays], core_ids=[0])
    return r.results[0]["out_0_dram"]
```

```python
from contextlib import ExitStack

import numpy as np

import concourse.bass as bass
from concourse import mybir

F32 = mybir.dt.float32
F32R = mybir.dt.float32r
BF16 = mybir.dt.bfloat16
F16 = mybir.dt.float16
I32 = mybir.dt.int32
ALU = mybir.AluOpType
ACT = mybir.ActivationFunctionType

N = 1250
NT = 10
R = N // NT
E = 20000
D = 512
KT = D // 128
EPS = 1e-5
BLOCKS, HEADS = 4, 4
DH = D // HEADS
QSCALE = float(DH) ** -0.5
NEVER = -1e37
NEVER_MAX = 1e30

ET = E // R
GT = 16
GROUPS = ET // GT
HALF = N // 2
HPITCH = HALF + 1
SHIFT = 11
BASE = 1 << SHIFT
assert GT * R < BASE and GROUPS * GT == ET

NFREQ = 32
NOISE = 16
TWO_PI = 2.0 * np.pi
PI_A = 6.28125
PI_B = float(np.float32(np.float16(TWO_PI - PI_A)))
PI_C = float(np.float32(TWO_PI - PI_A - PI_B))
PI_MAX = 3.1415925

CHUNKS = [(0, 512), (512, 512), (1024, N - 1024)]


def broadcast_rows(row_ap, rows):
    return bass.AP(row_ap.tensor, row_ap.offset, [[0, rows]] + [list(p) for p in row_ap.ap])


def identity(pool, zeroed, done, t):
    pool.memset(t, 0.0).then_inc(zeroed, 1)
    pool.wait_ge(zeroed, 1)
    pool.affine_select(out=t, in_=t, compare_op=ALU.not_equal, fill=1.0, base=0,
                       pattern=[[-1, 128]], channel_multiplier=1).then_inc(done, 1)


def count_edges(nc, src, dst, counts, onehot_a, scratch):
    ctx = ExitStack()
    with ctx:
        def sb(name, shape, dt):
            return ctx.enter_context(nc.sbuf_tensor(name, shape, dt))

        def sem(name):
            return ctx.enter_context(nc.semaphore(name))

        onehot_b = sb("onehot_b", [R, GT, N], BF16)
        ohs = [onehot_a, onehot_b[:, :, :]]
        ohd = sb("onehot_dst", [R, 2, GT, HPITCH], BF16)
        ids = sb("ids", [R, N], F16)
        raw = sb("raw_edges", [R, 2, ET], I32)
        ends = sb("edge_ends", [R, 2, ET], F32)
        upper = sb("upper_half", [R, ET], F32)
        weight = sb("weight", [R, ET], F32)
        now = sb("group_pair", [R, 3, 2 * GT], F32)
        packed = scratch[:, 0:2 * HALF].bitcast(I32).rearrange("p (b c) -> p b c", b=2)
        parts = scratch[:, 2 * HALF:4 * HALF].bitcast(I32).rearrange("p (b c) -> p b c", b=2)
        ps = ctx.enter_context(nc.psum_tensor("count_ps", [128, 4, 2, 512], F32))
        edges_in, ids_in, counts_zero = sem("edges_in"), sem("ids_in"), sem("counts_zero")
        prep, group_copied, onehots_ready = sem("prep"), sem("group_copied"), sem("onehots_ready")
        ps_filled, ps_drained = sem("ps_filled"), sem("ps_drained")
        parts_ready, parts_added = sem("parts_ready"), sem("parts_added")
        H1 = 313
        split = [(0, H1), (H1, HALF - H1)]

        with nc.Block() as block:
            @block.sync
            def _(sp):
                sp.dma_start(raw[:, 0, :], src.rearrange("(p t) -> p t", t=ET)).then_inc(edges_in, 16)
                sp.dma_start(raw[:, 1, :], dst.rearrange("(p t) -> p t", t=ET)).then_inc(edges_in, 16)

            @block.gpsimd
            def _(pool):
                pool.iota(ids[:, :], pattern=[[1, N]], base=0, channel_multiplier=0,
                          allow_small_or_imprecise_dtypes=True).then_inc(ids_in, 1)
                pool.sem_inc(ps_drained, 1)
                pool.sem_inc(parts_added, 1)
                for i in range(NT):
                    pool.memset(counts[:, i, :], 0.0).then_inc(counts_zero, 1)

            @block.vector
            def _(v):
                v.wait_ge(edges_in, 32)
                v.tensor_copy(ends[:, :, :], raw[:, :, :]).then_inc(prep, 1)
                v.wait_ge(prep, 1)
                v.tensor_scalar(upper[:, :], ends[:, 1, :], float(HALF), None, ALU.is_ge).then_inc(prep, 1)
                v.wait_ge(prep, 2)
                v.tensor_scalar(weight[:, :], upper[:, :], float(BASE - 1), 1.0, ALU.mult,
                                ALU.add).then_inc(prep, 1)
                v.scalar_tensor_tensor(ends[:, 1, :], upper[:, :], -float(HALF), ends[:, 1, :],
                                       ALU.mult, ALU.add).then_inc(prep, 1)
                v.wait_ge(prep, 4)
                v.wait_ge(ids_in, 1)
                v.wait_ge(counts_zero, NT)

                def onehots(half, first, pair):
                    for k, of in enumerate((ends[:, 0, :], ends[:, 1, :], weight[:, :])):
                        v.tensor_copy(now[:, k, half * GT:(half + 1) * GT],
                                      of[:, bass.ds(first, GT)]).then_inc(group_copied, 1)
                    v.wait_ge(group_copied, pair * 6 + (half + 1) * 3)
                    for t in range(GT):
                        c = half * GT + t
                        v.tensor_scalar(ohs[half][:, t, :], ids[:, :], now[:, 0, c:c + 1], None,
                                        ALU.is_equal)
                        last = v.tensor_scalar(ohd[:, half, t, 0:HALF], ids[:, 0:HALF], now[:, 1, c:c + 1],
                                               now[:, 2, c:c + 1], ALU.is_equal, ALU.mult)
                    last.then_inc(onehots_ready, 1)

                def add_group(half, p):
                    for m in range(NT):
                        k = half * NT + m
                        v.wait_ge(ps_drained, p * 2 * NT + (k + 2))
                        v.tensor_scalar(parts[:, 0, :], packed[:, k % 2, :], BASE - 1, None, ALU.bitwise_and)
                        v.tensor_scalar(parts[:, 1, :], packed[:, k % 2, :], SHIFT, None,
                                        ALU.logical_shift_right).then_inc(parts_ready, 1)
                        v.wait_ge(parts_ready, p * 2 * NT + (k + 1))
                        both = counts[:, m, :].rearrange("p (b c) -> p b c", b=2)
                        v.tensor_tensor(both, both, parts, ALU.add).then_inc(parts_added, 1)
                        v.wait_ge(parts_added, p * 2 * NT + (k + 2))

                onehots(0, 0, 0)
                onehots(1, GT, 0)
                with v.Fori(0, GROUPS // 2 - 1) as p:
                    for half in range(2):
                        add_group(half, p)
                        onehots(half, p * (2 * GT) + (2 + half) * GT, p + 1)
                for half in range(2):
                    add_group(half, GROUPS // 2 - 1)

            @block.tensor
            def _(pe):
                with pe.Fori(0, GROUPS // 2) as p:
                    for half in range(2):
                        pe.wait_ge(onehots_ready, 2 * p + (half + 1))
                        for m in range(NT):
                            k = half * NT + m
                            pe.wait_ge(ps_drained, p * 2 * NT + (max(k - 3, 0) + 1))
                            for t in range(GT):
                                for c, (at, n) in enumerate(split):
                                    last = pe.matmul(ps[0:R, k % 4, c, 0:n], ohs[half][:, t, m * R:(m + 1) * R],
                                                     ohd[:, half, t, at:at + n], start=(t == 0),
                                                     stop=(t == GT - 1))
                            last.then_inc(ps_filled, 1)

            @block.scalar
            def _(act):
                with act.Fori(0, GROUPS // 2) as p:
                    for half in range(2):
                        for m in range(NT):
                            k = half * NT + m
                            act.wait_ge(ps_filled, p * 2 * NT + (k + 1))
                            act.wait_ge(parts_added, p * 2 * NT + (max(k - 1, 0) + 1))
                            act.activation(packed[:, k % 2, 0:H1], ps[0:R, k % 4, 0, 0:H1], ACT.Copy)
                            act.activation(packed[:, k % 2, H1:HALF], ps[0:R, k % 4, 1, 0:HALF - H1],
                                           ACT.Copy).then_inc(ps_drained, 1)


def row_stats(v, x, i, stats, mean_var, done, count):
    v.bn_stats(stats[:, i, :], x[:, i, :]).then_inc(done, 1)
    v.wait_ge(done, count + 1)
    v.bn_aggr(mean_var[:, i, :], stats[:, i, :]).then_inc(done, 1)


def gcn_layer(nc, x_in, w1, b1, w2, b2, wd1, bd1, wd2, bd2, wd3, bd3, x_keep, x, counts, logc, ident):
    HID, LAT, DEC = w1.shape[0], w2.shape[0], wd2.shape[0]
    MC = DEC // 128
    ctx = ExitStack()
    with ctx:
        def sb(name, shape, dt=F32):
            return ctx.enter_context(nc.sbuf_tensor(name, shape, dt))

        def sem(name):
            return ctx.enter_context(nc.semaphore(name))

        xb = sb("xb", [R, NT, D])
        h = sb("h_tile", [R, 2, D])
        hT = sb("hT", [128, KT, N])
        y1T = hT[:, 0, :]
        y2T = hT[:, 1:1 + MC, :]
        no_edge = hT[0:R, 1 + MC, :]
        g1, t1 = sb("g1", [R, NT, HID]), sb("t1", [R, NT, HID])
        g2, t2 = sb("g2", [R, NT, LAT]), sb("t2", [R, NT, LAT])
        rT, zT = sb("rT", [HID, N]), sb("zT", [LAT, N])
        w1r, w1T = sb("w1r", [HID, D]), sb("w1T", [128, KT, HID])
        w2r, w2T = sb("w2r", [LAT, HID]), sb("w2T", [HID, LAT])
        wd1r, wd1T = sb("wd1r", [HID, LAT]), sb("wd1T", [LAT, HID])
        wd2r, wd2T = sb("wd2r", [128, MC, HID]), sb("wd2T", [HID, DEC])
        wd3r, wd3T = sb("wd3r", [128, KT, DEC]), sb("wd3T", [128, MC, D])
        b1c, b2c, bd1c, bd2c = sb("b1c", [HID, 1]), sb("b2c", [LAT, 1]), sb("bd1c", [HID, 1]), sb("bd2c", [128, MC])
        bd3b = sb("bd3b", [R, D])
        eps_col = sb("eps_col", [R, 1])
        stats, mean_var = sb("stats", [R, NT, 6]), sb("mean_var", [R, NT, 2])
        rstd, shift = sb("rstd", [R, NT]), sb("shift", [R, NT])
        ones, deg, dinv = sb("ones", [R, 1]), sb("deg", [R, NT]), sb("dinv", [R, NT])
        psd = ctx.enter_context(nc.psum_tensor("ring_dve", [128, 4, 512], F32))
        psa = ctx.enter_context(nc.psum_tensor("ring_act", [128, 4, 512], F32))
        x_loaded, w_loaded, b_loaded = sem("x_loaded"), sem("w_loaded"), sem("b_loaded")
        ones_in, zeroed, ident_in = sem("ones_in"), sem("ident_zeroed"), sem("ident_in")
        stats_done, sqrt_done, rstd_done, h_ready = sem("stats_done"), sem("sqrt_done"), sem("rstd_done"), sem("h_ready")
        d_filled, d_drained = sem("d_filled"), sem("d_drained")
        a_filled, a_drained = sem("a_filled"), sem("a_drained")
        deg_ready, deg_sqrt, dinv_ready = sem("deg_ready"), sem("deg_sqrt"), sem("dinv_ready")
        t_sum, t_ready = sem("t_sum"), sem("t_ready")
        x_biased, x1_ready, x1_stored = sem("x_biased"), sem("x1_ready"), sem("x1_stored")
        log_in, log_done, log_masked = sem("log_in"), sem("log_done"), sem("log_masked")

        a_jobs = {"w": 0}
        a_jobs["t1T"] = 4 + MC
        a_jobs["t2T"] = a_jobs["t1T"] + NT
        a_jobs["y1"] = a_jobs["t2T"] + NT
        a_jobs["y2"] = a_jobs["y1"] + len(CHUNKS)
        a_end = a_jobs["y2"] + MC * len(CHUNKS)
        d_jobs = {"hT": 0, "deg": NT}
        for at, name in enumerate(["hw1", "agg1", "hw2", "agg2", "y3"]):
            d_jobs[name] = NT + 1 + at * NT

        with nc.Block() as block:
            @block.sync
            def _(sp):
                xv = x_in.rearrange("(t p) d -> p t d", p=R)
                for i in range(NT):
                    sp.dma_start(xb[:, i, :], xv[:, i, :]).then_inc(x_loaded, 16)
                sp.dma_start(bd3b[:, :], broadcast_rows(bd3, R)).then_inc(b_loaded, 16)
                sp.dma_start(b1c[:, :], b1.rearrange("(p a) -> p a", a=1)).then_inc(b_loaded, 16)
                sp.dma_start(b2c[:, :], b2.rearrange("(p a) -> p a", a=1)).then_inc(b_loaded, 16)
                sp.dma_start(bd1c[:, :], bd1.rearrange("(p a) -> p a", a=1)).then_inc(b_loaded, 16)
                with nc.allow_non_contiguous_dma(reason="a bias of 256"):
                    sp.dma_start(bd2c[:, :], bd2.rearrange("(m p) -> p m", p=128)).then_inc(b_loaded, 16)
                for i in range(NT):
                    sp.wait_ge(x1_ready, i + 1)
                    sp.dma_start(x_keep.rearrange("(t p) d -> p t d", p=R)[:, i, :], xb[:, i, :])\
                      .then_inc(x1_stored, 16)
                sp.wait_ge(x1_stored, 16 * NT)

            @block.gpsimd
            def _(pool):
                pool.memset(ones[:, :], 1.0).then_inc(ones_in, 1)
                pool.memset(eps_col[:, :], EPS).then_inc(ones_in, 1)
                identity(pool, zeroed, ident_in, ident)
                pool.wait_ge(b_loaded, 80)
                for i in range(NT):
                    pool.wait_ge(h_ready, i + 1)
                    pool.tensor_tensor(xb[:, i, :], xb[:, i, :], bd3b[:, :], ALU.add).then_inc(x_biased, 1)

            @block.vector
            def _(v):
                for i in range(NT):
                    v.wait_ge(x_loaded, 160)
                    row_stats(v, xb, i, stats, mean_var, stats_done, 2 * i)
                v.wait_ge(sqrt_done, 1)
                v.reciprocal(rstd[:, :], rstd[:, :]).then_inc(rstd_done, 1)
                v.wait_ge(rstd_done, 1)
                v.scalar_tensor_tensor(shift[:, :], mean_var[:, :, 0], -1.0, rstd[:, :], ALU.mult,
                                       ALU.mult).then_inc(rstd_done, 1)
                for i in range(NT):
                    v.wait_ge(d_filled, i + 1)
                    v.tensor_copy(hT[:, :, i * R:(i + 1) * R],
                                  psd[:, i % 4, 0:KT * R].rearrange("p (k n) -> p k n", k=KT))\
                        .then_inc(d_drained, 1)
                v.wait_ge(d_filled, NT + 1)
                v.tensor_scalar(deg[:, :], psd[0:R, NT % 4, 0:NT], 1.0, None, ALU.add).then_inc(d_drained, 1)
                v.wait_ge(deg_sqrt, 1)
                v.reciprocal(dinv[:, :], deg[:, :]).then_inc(dinv_ready, 1)
                v.wait_ge(dinv_ready, 1)

                def scale_rows(job, g, width):
                    for i in range(NT):
                        k = d_jobs[job] + i
                        v.wait_ge(d_filled, k + 1)
                        v.tensor_scalar(g[:, i, :], psd[0:R, k % 4, 0:width], dinv[:, i:i + 1], None,
                                        ALU.mult).then_inc(d_drained, 1)

                def aggregate(job, g, t, width):
                    for i in range(NT):
                        k = d_jobs[job] + i
                        v.wait_ge(d_filled, k + 1)
                        v.tensor_tensor(t[:, i, :], psd[0:R, k % 4, 0:width], g[:, i, :], ALU.add)\
                            .then_inc(d_drained, 1)
                        v.wait_ge(d_drained, k + 1)
                        v.tensor_scalar(t[:, i, :], t[:, i, :], dinv[:, i:i + 1], None, ALU.mult)\
                            .then_inc(t_ready, 1)

                scale_rows("hw1", g1, HID)
                for i in range(NT):
                    v.tensor_scalar(logc[:, i, :], counts[:, i, :], 1.0, None, ALU.max).then_inc(log_in, 1)
                aggregate("agg1", g1, t1, HID)
                for i in range(NT):
                    v.tensor_scalar(no_edge, counts[:, i, :], 0.0, NEVER, ALU.is_equal, ALU.mult)\
                        .then_inc(log_masked, 1)
                    v.wait_ge(log_done, i + 1)
                    v.wait_ge(log_masked, 2 * i + 1)
                    v.scalar_tensor_tensor(logc[:, i, :], logc[:, i, :], 1 / QSCALE, no_edge, ALU.mult,
                                           ALU.add).then_inc(log_masked, 1)
                    v.wait_ge(log_masked, 2 * i + 2)
                scale_rows("hw2", g2, LAT)
                aggregate("agg2", g2, t2, LAT)
                for i in range(NT):
                    k = d_jobs["y3"] + i
                    v.wait_ge(d_filled, k + 1)
                    v.wait_ge(x_biased, i + 1)
                    v.tensor_tensor(xb[:, i, :], xb[:, i, :], psd[0:R, k % 4, :], ALU.add)\
                        .then_inc(d_drained, 1)
                    v.wait_ge(d_drained, k + 1)
                    v.bn_stats(stats[:, i, :], xb[:, i, :]).then_inc(x1_ready, 1)
                    v.wait_ge(x1_ready, i + 1)
                    v.bn_aggr(mean_var[:, i, :], stats[:, i, :]).then_inc(stats_done, 1)
                v.wait_ge(sqrt_done, 2)
                v.reciprocal(rstd[:, :], rstd[:, :]).then_inc(rstd_done, 1)
                v.wait_ge(rstd_done, 3)
                v.scalar_tensor_tensor(shift[:, :], mean_var[:, :, 0], -1.0, rstd[:, :], ALU.mult,
                                       ALU.mult).then_inc(rstd_done, 1)

            @block.scalar
            def _(act):
                act.dma_start(w1r[:, :], w1).then_inc(w_loaded, 16)
                act.dma_start(w2r[:, :], w2).then_inc(w_loaded, 16)
                act.dma_start(wd1r[:, :], wd1).then_inc(w_loaded, 16)
                act.dma_start(wd2r[:, :, :], wd2.rearrange("(m p) k -> p m k", p=128)).then_inc(w_loaded, 16)
                act.dma_start(wd3r[:, :, :], wd3.rearrange("(m p) k -> p m k", p=128)).then_inc(w_loaded, 16)

                act.wait_ge(ones_in, 2)

                def root(variance_count):
                    act.wait_ge(stats_done, variance_count)
                    act.activation(rstd[:, :], mean_var[:, :, 1], ACT.Sqrt, bias=eps_col[:, 0:1]).then_inc(sqrt_done, 1)

                def drain(k, out, rows, cols, func=ACT.Copy, bias=0.0):
                    act.wait_ge(a_filled, k + 1)
                    act.activation(out, psa[0:rows, k % 4, 0:cols], func, bias=bias).then_inc(a_drained, 1)

                drain(0, w1T[:, :, :].rearrange("p k m -> p (k m)"), 128, KT * HID)
                drain(1, w2T[:, :], HID, LAT)
                drain(2, wd1T[:, :], LAT, HID)
                drain(3, wd2T[:, :], HID, DEC)
                for c in range(MC):
                    drain(4 + c, wd3T[:, c, :], 128, D)
                root(2 * NT)
                for i in range(NT):
                    if i == 0:
                        act.wait_ge(rstd_done, 2)
                    if i >= 2:
                        act.wait_ge(d_filled, i - 1)
                    act.activation(h[:, i % 2, :], xb[:, i, :], ACT.Relu, bias=shift[:, i:i + 1],
                                   scale=rstd[:, i:i + 1]).then_inc(h_ready, 1)
                act.wait_ge(d_drained, NT + 1)
                act.activation(deg[:, :], deg[:, :], ACT.Sqrt).then_inc(deg_sqrt, 1)
                for i in range(NT):
                    act.wait_ge(log_in, i + 1)
                    act.activation(logc[:, i, :], logc[:, i, :], ACT.Ln).then_inc(log_done, 1)
                act.wait_ge(b_loaded, 80)
                for i in range(NT):
                    drain(a_jobs["t1T"] + i, rT[:, i * R:(i + 1) * R], HID, R, ACT.Relu, b1c[:, 0:1])
                for i in range(NT):
                    drain(a_jobs["t2T"] + i, zT[:, i * R:(i + 1) * R], LAT, R, ACT.Identity, b2c[:, 0:1])
                for c, (at, n) in enumerate(CHUNKS):
                    drain(a_jobs["y1"] + c, y1T[:, at:at + n], HID, n, ACT.Relu, bd1c[:, 0:1])
                for m in range(MC):
                    for c, (at, n) in enumerate(CHUNKS):
                        drain(a_jobs["y2"] + m * len(CHUNKS) + c, y2T[:, m, at:at + n], 128, n, ACT.Relu,
                              bd2c[:, m:m + 1])
                root(3 * NT)
                act.wait_ge(rstd_done, 4)
                for i in range(NT):
                    act.activation(x[:, i, :], xb[:, i, :], ACT.Relu, bias=shift[:, i:i + 1],
                                   scale=rstd[:, i:i + 1])

            @block.tensor
            def _(pe):
                def free_a(k):
                    if k >= 4:
                        pe.wait_ge(a_drained, k - 3)

                def free_d(k):
                    if k >= 4:
                        pe.wait_ge(d_drained, k - 3)

                pe.wait_ge(w_loaded, 80)
                pe.wait_ge(ident_in, 1)
                for k in range(KT):
                    last = pe.transpose(psa[:, 0, k * 128:k * 128 + HID], w1r[:, k * 128:(k + 1) * 128],
                                        ident[0:HID, 0:HID])
                last.then_inc(a_filled, 1)
                pe.transpose(psa[0:HID, 1, 0:LAT], w2r[:, :], ident[0:LAT, 0:LAT]).then_inc(a_filled, 1)
                pe.transpose(psa[0:LAT, 2, 0:HID], wd1r[:, :], ident[0:HID, 0:HID]).then_inc(a_filled, 1)
                for m in range(MC):
                    last = pe.transpose(psa[0:HID, 3, m * 128:(m + 1) * 128], wd2r[:, m, :], ident)
                last.then_inc(a_filled, 1)
                for c in range(MC):
                    free_a(4 + c)
                    for m in range(KT):
                        last = pe.transpose(psa[:, (4 + c) % 4, m * 128:(m + 1) * 128],
                                            wd3r[:, m, c * 128:(c + 1) * 128], ident)
                    last.then_inc(a_filled, 1)
                pe.wait_ge(ones_in, 2)
                for i in range(NT):
                    free_d(i)
                    pe.wait_ge(h_ready, i + 1)
                    for k in range(KT):
                        last = pe.transpose(psd[:, i % 4, k * R:(k + 1) * R],
                                            h[:, i % 2, k * 128:(k + 1) * 128], ident[0:R, 0:R])
                    last.then_inc(d_filled, 1)
                free_d(NT)
                for i in range(NT):
                    for s in range(NT):
                        last = pe.matmul(psd[0:R, NT % 4, i:i + 1], counts[:, s, i * R:(i + 1) * R], ones[:, :],
                                         start=(s == 0), stop=(s == NT - 1))
                last.then_inc(d_filled, 1)
                pe.wait_ge(d_drained, NT)
                pe.wait_ge(a_drained, 1)

                def rows(job, srcT, w, width, tiles):
                    for i in range(NT):
                        k = d_jobs[job] + i
                        free_d(k)
                        for c in range(tiles):
                            last = pe.matmul(psd[0:R, k % 4, 0:width], srcT(c)[:, i * R:(i + 1) * R], w(c),
                                             start=(c == 0), stop=(c == tiles - 1))
                        last.then_inc(d_filled, 1)

                def neighbours(job, g, width):
                    for i in range(NT):
                        k = d_jobs[job] + i
                        free_d(k)
                        for s in range(NT):
                            last = pe.matmul(psd[0:R, k % 4, 0:width], counts[:, s, i * R:(i + 1) * R],
                                             g[:, s, :], start=(s == 0), stop=(s == NT - 1))
                        last.then_inc(d_filled, 1)

                def transposes(job, t, width, ready):
                    for i in range(NT):
                        k = a_jobs[job] + i
                        free_a(k)
                        pe.wait_ge(t_ready, ready + i + 1)
                        pe.transpose(psa[0:width, k % 4, 0:R], t[:, i, :], ident[0:R, 0:R])\
                            .then_inc(a_filled, 1)

                rows("hw1", lambda c: hT[:, c, :], lambda c: w1T[:, c, :], HID, KT)
                pe.wait_ge(d_drained, d_jobs["hw1"] + NT)
                neighbours("agg1", g1, HID)
                transposes("t1T", t1, HID, 0)
                pe.wait_ge(a_drained, a_jobs["t1T"] + NT)
                rows("hw2", lambda c: rT[:, :], lambda c: w2T[:, :], LAT, 1)
                pe.wait_ge(d_drained, d_jobs["hw2"] + NT)
                neighbours("agg2", g2, LAT)
                transposes("t2T", t2, LAT, NT)
                pe.wait_ge(a_drained, a_jobs["t2T"] + NT)
                for c, (at, n) in enumerate(CHUNKS):
                    k = a_jobs["y1"] + c
                    free_a(k)
                    pe.matmul(psa[:, k % 4, 0:n], wd1T[:, :], zT[:, at:at + n], start=True, stop=True)\
                        .then_inc(a_filled, 1)
                pe.wait_ge(a_drained, a_jobs["y2"])
                for m in range(MC):
                    for c, (at, n) in enumerate(CHUNKS):
                        k = a_jobs["y2"] + m * len(CHUNKS) + c
                        free_a(k)
                        pe.matmul(psa[:, k % 4, 0:n], wd2T[:, m * 128:(m + 1) * 128], y1T[:, at:at + n],
                                  start=True, stop=True).then_inc(a_filled, 1)
                pe.wait_ge(a_drained, a_end)
                rows("y3", lambda c: y2T[:, c, :], lambda c: wd3T[:, c, :], D, MC)


PAIRS = NT // 2


def turns():
    uses, v_parts, parts, outs, at = {"T": 0, "U": 0}, [], {}, {}, 0

    def take():
        nonlocal at
        s = "TU"[at % 2]
        at += 1
        uses[s] += 1
        return s, uses[s] - 1

    for f in range(3):
        v_parts.append(take())
    for g in range(PAIRS):
        for i in (2 * g, 2 * g + 1):
            for f in range(3):
                parts[i, f] = take()
        outs[g] = take()
    return uses, v_parts, parts, outs


TU_USES, V_SLOT, PART_SLOT, OUT_SLOT = turns()
PARTS = [(0, 4), (4, 4), (8, 2)]
HEAD_USES = {"A": 9, "B": 8, **TU_USES}
MLP_USES = {"A": 4, "B": 4, "T": 0, "U": 0}
BLOCK_USES = {s: 2 * PAIRS + HEADS * HEAD_USES[s] + MLP_USES[s] for s in "ABTU"}
OUT_BATCHES = [("A", (0, 1, 2)), ("B", (3, 4, 5)), ("A", (6, 7)), ("B", (8, 9))]
TOP_ITEMS, HEAD_ITEMS, LAST_ITEMS, MLP_ITEMS = 5, 4, 3, 2 * KT
BLOCK_ITEMS = TOP_ITEMS + (HEADS - 1) * HEAD_ITEMS + LAST_ITEMS + MLP_ITEMS


def in_ln1(s, b, u):
    return b * BLOCK_USES[s] + u


def in_head(s, b, h, u):
    return b * BLOCK_USES[s] + h * HEAD_USES[s] + (PAIRS + u)


def in_ln2(s, b, u):
    return b * BLOCK_USES[s] + (PAIRS + HEADS * HEAD_USES[s] + u)


def in_mlp(s, b, u):
    return b * BLOCK_USES[s] + (2 * PAIRS + HEADS * HEAD_USES[s] + u)


def score_slot(i):
    return ("B", 1 + i // 2) if i % 2 == 0 else ("A", 2 + i // 2)


def transformer(nc, noise, p, x_keep, out, x, logc, ident):
    ctx = ExitStack()
    with ctx:
        def sb(name, shape, dt=F32):
            return ctx.enter_context(nc.sbuf_tensor("c_" + name, shape, dt))

        def halves(name, shape):
            return sb(name + "h", shape, F32R), sb(name + "l", shape, F32R)

        def sem(name):
            return ctx.enter_context(nc.semaphore("c_" + name))

        def overlay(*tensors):
            with ExitStack() as scope:
                return [scope.enter_context(nc.sbuf_tensor("c_" + n, s, d)) for n, s, d in tensors]

        yTh, yTl = halves("yT", [128, KT, N])
        wqh, wql = halves("wq", [128, KT, DH])
        wkh, wkl = halves("wk", [128, KT, DH])
        wvh, wvl = halves("wv", [128, KT, DH])
        stage = sb("stage", [128, D])
        mod_w = sb("mod_w", [128, 2, D], F32R)
        condh = sb("cond_parts", [128, N], F32R)
        bq, bk, bv = sb("bq", [DH, 1]), sb("bk", [DH, 1]), sb("bv", [DH, 1])
        row_bias, mb1 = sb("row_bias", [R, D]), sb("mb1", [128, KT])
        stats, mean_var = sb("stats", [R, NT, 6]), sb("mean_var", [R, NT, 2])
        rstd, shift, eps_col = sb("rstd", [R, NT]), sb("shift", [R, NT]), sb("eps_col", [R, 1])
        row_max, neg_max = sb("row_max", [R, NT]), sb("neg_max", [R, NT])
        row_sum, inv_sum = sb("row_sum", [R, NT]), sb("inv_sum", [R, NT])
        xn, y = overlay(("xn", [R, 2, D], F32), ("y", [R, 2, D], F32))
        uph, upl, w1h, w1l, w2h, w2l = overlay(*((n, [128, KT, N], F32R) for n in ("uph", "upl")),
                                               *((n, [128, KT, D], F32R) for n in ("w1h", "w1l", "w2h", "w2l")))
        x1, = overlay(("x1", [R, NT, D], F32))
        angle, turn, turn_i, hidden, cond = overlay(
            ("angle", [2 * NFREQ, N], F32), ("turn", [2 * NFREQ, N], F32), ("turn_i", [2 * NFREQ, N], I32),
            ("hidden", [NOISE, N], F32), ("cond", [32, N], F32))
        probsTh, probsTl = halves("probsT", [R, NT, 2 * R])
        probs = sb("probs", [R, 2, N])
        qh, ql = halves("q", [DH, N])
        kh, kl = halves("k", [DH, N])
        vh, vl = halves("v", [R, NT, DH])
        vT, = overlay(("vT", [DH, N], F32))
        oTh, oTl = halves("oT", [DH, N])
        woh, wol = halves("wo", [DH, D])

        slot = {"A": ctx.enter_context(nc.psum_tensor("slot_A", [128, 3 * 512], F32)),
                "B": ctx.enter_context(nc.psum_tensor("slot_B", [128, 3 * 512], F32)),
                "T": ctx.enter_context(nc.psum_tensor("slot_T", [128, 512], F32)),
                "U": ctx.enter_context(nc.psum_tensor("slot_U", [128, 512], F32))}
        filled = {s: sem(f"slot_{s}_filled") for s in "ABTU"}
        drained = {s: sem(f"slot_{s}_drained") for s in "ABTU"}
        staged, mod_staged, hi_split, lo_split = sem("staged"), sem("mod_staged"), sem("weight_hi"), sem("weight_lo")
        head_b_in, mlp_b_in, row_bias_in = sem("head_biases_in"), sem("mlp_bias_in"), sem("row_bias_in")
        stats_done, rstd_ready = sem("stats_done"), sem("rstd_ready")
        root_done, xn_ready, x_biased, scaled = sem("root_done"), sem("xn_ready"), sem("x_biased"), sem("scaled")
        yT_hi, q_hi, k_hi, v_hi, probsT_hi, oT_hi, up_hi = (
            sem(n) for n in ("yT_hi", "q_hi", "k_hi", "v_hi", "probsT_hi", "oT_hi", "up_hi"))
        k_part, k_lo, up_relu = sem("k_part_filled"), sem("k_lo"), sem("up_relu")
        max_ready, probs_ready, inv_ready = sem("max_ready"), sem("probs_ready"), sem("inv_ready")
        x1_in, sum_ready, stored = sem("x1_in"), sem("sum_ready"), sem("stored")
        waits_passed = {nc.vector: sem("dve_waits_passed"), nc.sync: sem("sp_waits_passed")}

        def apart(engine):
            engine.sem_inc(waits_passed[engine], 1)

        embed_noise(nc, noise, p, cond, condh, stage, eps_col, slot, angle, turn, turn_i, hidden)

        def item(b, n):
            return b * BLOCK_ITEMS + n

        def head_item(b, h, n):
            return b * BLOCK_ITEMS + h * HEAD_ITEMS + (TOP_ITEMS + n)

        mlp_first = TOP_ITEMS + (HEADS - 1) * HEAD_ITEMS + LAST_ITEMS

        with nc.Block() as block:
            @block.sync
            def _(sp):
                def mod_weights(b, n, w, bias):
                    sp.wait_ge(lo_split, n + 1)
                    apart(sp)
                    for c in range(4):
                        sp.dma_start(stage[32 * c:32 * c + NOISE, :], p[w][b]).then_inc(mod_staged, 16)
                        sp.dma_start(stage[32 * c + NOISE:32 * c + NOISE + 1, :], p[bias][bass.ds(b, 1)])\
                            .then_inc(mod_staged, 16)

                def matrix(n, w, t=None):
                    sp.wait_ge(lo_split, n + 1)
                    apart(sp)
                    sp.dma_start(stage[:, :] if t is None else t, w).then_inc(staged, 16)

                def head_matrix(b, h, n, name):
                    matrix(n, p[name].rearrange("b (k p) (h c) -> b h p k c", p=128, h=HEADS)[b, h],
                           stage[:, :].rearrange("p (k c) -> p k c", k=KT))

                def head_out_matrix(b, h, n):
                    matrix(n, p["wo"].rearrange("b (h c) n -> (b h) c n", h=HEADS)[b * HEADS + h])

                def head_biases(b, h):
                    for t, w in ((bq, p["bq"]), (bk, p["bk"]), (bv, p["bv"])):
                        w = w.rearrange("b (h c) -> (b h) c", h=HEADS)
                        sp.dma_start(t[:, :], w[bass.ds(b * HEADS + h, 1)].rearrange("a c -> c a"))\
                            .then_inc(head_b_in, 16)

                with sp.Fori(0, BLOCKS) as b:
                    mod_weights(b, item(b, 0), "s1_w", "s1_b")
                    mod_weights(b, item(b, 1), "b1_w", "b1_b")
                    for n, name in enumerate(("wq", "wk", "wv")):
                        head_matrix(b, 0, item(b, 2 + n), name)
                    for s in "AB":
                        sp.wait_ge(drained[s], in_ln1(s, b, 0) + 1)
                        apart(sp)
                    sp.dma_start(row_bias[:, :], p["bo"][bass.ds(b, 1)].to_broadcast([R, D]))\
                        .then_inc(row_bias_in, 16)
                    head_biases(b, 0)
                    with nc.allow_non_contiguous_dma(reason="a bias of 512 by columns"):
                        sp.dma_start(mb1[:, :], p["m_b1"].rearrange("b (k p) -> b p k", p=128)[b])\
                            .then_inc(mlp_b_in, 16)
                    with sp.Fori(0, HEADS - 1) as h:
                        head_out_matrix(b, h, head_item(b, h, 0))
                        for n, name in enumerate(("wq", "wk", "wv")):
                            head_matrix(b, h + 1, head_item(b, h, 1 + n), name)
                        sp.wait_ge(drained["A"], in_head("A", b, h, 2) + 1)
                        apart(sp)
                        sp.wait_ge(drained["B"], in_head("B", b, h, 1) + 1)
                        apart(sp)
                        head_biases(b, h + 1)
                    head_out_matrix(b, HEADS - 1, head_item(b, HEADS - 1, 0))
                    mod_weights(b, head_item(b, HEADS - 1, 1), "s2_w", "s2_b")
                    mod_weights(b, head_item(b, HEADS - 1, 2), "b2_w", "b2_b")
                    sp.wait_ge(x_biased, b * 2 * NT + NT)
                    apart(sp)
                    sp.dma_start(row_bias[:, :], p["m_b2"][bass.ds(b, 1)].to_broadcast([R, D]))\
                        .then_inc(row_bias_in, 16)
                    for n, name in enumerate(("m_w1", "m_w2")):
                        for k in range(KT):
                            matrix(item(b, mlp_first + n * KT + k), p[name][b, k * 128:(k + 1) * 128, :])
                for s in "AB":
                    sp.wait_ge(filled[s], BLOCKS * BLOCK_USES[s])
                sp.dma_start(x1[:, :, :], x_keep.rearrange("(t p) d -> p t d", p=R)).then_inc(x1_in, 16)
                outv = out.rearrange("(t p) d -> p t d", p=R)
                for i in range(NT):
                    sp.wait_ge(sum_ready, i + 1)
                    sp.dma_start(outv[:, i, :], x[:, i, :]).then_inc(stored, 16)
                sp.wait_ge(stored, 16 * NT)

            @block.gpsimd
            def _(pool):
                for s in "ABTU":
                    pool.sem_inc(drained[s], 1)
                pool.sem_inc(lo_split, 1)

                def lo(n, dest, hi):
                    pool.wait_ge(hi_split, n + 1)
                    pool.tensor_tensor(dest, stage[:, :], hi.bitcast(F32), ALU.subtract).then_inc(lo_split, 1)

                def mod_lo(n, c):
                    pool.wait_ge(hi_split, n + 1)
                    for q in (1, 3):
                        rows = slice(32 * q, 32 * q + NOISE + 1)
                        last = pool.tensor_tensor(mod_w[rows, c, :], stage[rows, :],
                                                  mod_w[rows, c, :].bitcast(F32), ALU.subtract)
                    last.then_inc(lo_split, 1)

                def flat(t):
                    return t[:, :, :].rearrange("p k c -> p (k c)")

                def add_bias(b, ln):
                    pool.wait_ge(row_bias_in, b * 32 + (16 * ln + 16))
                    for i in range(NT):
                        pool.wait_ge(xn_ready, b * 2 * NT + (ln * NT + i + 1))
                        pool.tensor_tensor(x[:, i, :], x[:, i, :], row_bias[:, :], ALU.add)\
                            .then_inc(x_biased, 1)

                qkv = ((wqh, wql), (wkh, wkl), (wvh, wvl))
                with pool.Fori(0, BLOCKS) as b:
                    mod_lo(item(b, 0), 0)
                    mod_lo(item(b, 1), 1)
                    for n, (h_, l_) in enumerate(qkv):
                        lo(item(b, 2 + n), flat(l_), flat(h_))
                    add_bias(b, 0)
                    with pool.Fori(0, HEADS - 1) as h:
                        lo(head_item(b, h, 0), wol[:, :], woh[:, :])
                        for n, (h_, l_) in enumerate(qkv):
                            lo(head_item(b, h, 1 + n), flat(l_), flat(h_))
                    lo(head_item(b, HEADS - 1, 0), wol[:, :], woh[:, :])
                    mod_lo(head_item(b, HEADS - 1, 1), 0)
                    mod_lo(head_item(b, HEADS - 1, 2), 1)
                    for k in range(KT):
                        lo(item(b, mlp_first + k), w1l[:, k, :], w1h[:, k, :])
                    add_bias(b, 1)
                    for k in range(KT):
                        lo(item(b, mlp_first + KT + k), w2l[:, k, :], w2h[:, k, :])

            @block.vector
            def _(v):
                def modulate(b, ln, at):
                    for s in "AB":
                        v.wait_ge(drained[s], at(s, b, 0) + 1)
                    for i in range(NT):
                        last = v.bn_stats(stats[:, i, :], x[:, i, :])
                    last.then_inc(stats_done, 1)
                    v.wait_ge(stats_done, b * 4 + (2 * ln + 1))
                    apart(v)
                    for i in range(NT):
                        last = v.bn_aggr(mean_var[:, i, :], stats[:, i, :])
                    last.then_inc(stats_done, 1)
                    v.wait_ge(root_done, b * 2 + (ln + 1))
                    v.reciprocal(rstd[:, :], rstd[:, :]).then_inc(rstd_ready, 1)
                    v.wait_ge(rstd_ready, b * 4 + (2 * ln + 1))
                    v.scalar_tensor_tensor(shift[:, :], mean_var[:, :, 0], -1.0, rstd[:, :], ALU.mult,
                                           ALU.mult).then_inc(rstd_ready, 1)

                    def low(i):
                        s = "TU"[i % 2]
                        v.wait_ge(yT_hi, b * 2 * NT + (ln * NT + i + 1))
                        at_i = slice(i * R, (i + 1) * R)
                        v.tensor_tensor(yTl[:, :, at_i], slot[s][:, 0:KT * R].rearrange("p (k n) -> p k n", k=KT),
                                        yTh[:, :, at_i].bitcast(F32), ALU.subtract).then_inc(drained[s], 1)

                    for i in range(NT):
                        s = "AB"[i % 2]
                        t = b * 2 * NT + (ln * NT + i)
                        v.wait_ge(filled[s], at(s, b, i // 2) + 1)
                        v.wait_ge(xn_ready, t + 1)
                        if i >= 2:
                            v.wait_ge(filled["TU"[i % 2]], at("TU"[i % 2], b, i // 2 - 1) + 1)
                        v.scalar_tensor_tensor(y[:, i % 2, :], slot[s][0:R, 0:D], 1.0, xn[:, i % 2, :],
                                               ALU.add, ALU.mult).then_inc(scaled, 1)
                        v.wait_ge(scaled, t + 1)
                        v.tensor_tensor(y[:, i % 2, :], y[:, i % 2, :], slot[s][0:R, 512:512 + D], ALU.add)\
                            .then_inc(drained[s], 1)
                        if i >= 1:
                            low(i - 1)
                    low(NT - 1)

                def scores(b, h, i):
                    s, u = score_slot(i)
                    v.wait_ge(filled[s], in_head(s, b, h, u) + 1)
                    if i >= 2:
                        t, w = PART_SLOT[i - 2, 2]
                        v.wait_ge(filled[t], in_head(t, b, h, w) + 1)
                    apart(v)
                    v.tensor_tensor_reduce(out=probs[:, i % 2, :], in0=slot[s][0:R, 0:N], in1=logc[:, i, :],
                                           scale=1.0, scalar=-3e38, op0=ALU.add, op1=ALU.max,
                                           accum_out=row_max[:, i:i + 1]).then_inc(drained[s], 1)
                    v.wait_ge(drained[s], in_head(s, b, h, u) + 2)
                    v.tensor_scalar(neg_max[:, i:i + 1], row_max[:, i:i + 1], -QSCALE, NEVER_MAX, ALU.mult,
                                    ALU.min).then_inc(max_ready, 1)

                def transposed(b, h, i, f):
                    j, m = PARTS[f]
                    s, u = PART_SLOT[i, f]
                    v.wait_ge(probsT_hi, b * HEADS * NT * 3 + h * NT * 3 + (3 * i + f + 1))
                    dest = (slice(0, R), slice(j, j + m), slice(i % 2 * R, (i % 2 + 1) * R))
                    v.tensor_tensor(probsTl[dest], slot[s][0:R, 0:m * R].rearrange("p (j n) -> p j n", j=m),
                                    probsTh[dest].bitcast(F32), ALU.subtract).then_inc(drained[s], 1)

                def k_low(b, h, c):
                    at, n = CHUNKS[c]
                    v.wait_ge(k_hi, b * HEADS * 3 + h * 3 + (c + 1))
                    v.scalar_tensor_tensor(kl[:, at:at + n], slot["A"][:, at:at + n], bk[:, 0:1],
                                           kh[:, at:at + n].bitcast(F32), ALU.add, ALU.subtract)\
                        .then_inc(k_lo if c < 2 else drained["A"], 1)

                def v_low(b, h, f):
                    j, m = PARTS[f]
                    s, u = V_SLOT[f]
                    v.wait_ge(v_hi, b * HEADS * 3 + h * 3 + (f + 1))
                    v.tensor_tensor(vl[:, j:j + m, :], slot[s][0:R, 0:m * DH].rearrange("p (j c) -> p j c", j=m),
                                    vh[:, j:j + m, :].bitcast(F32), ALU.subtract).then_inc(drained[s], 1)

                def head_out(b, h, g):
                    s, u = OUT_SLOT[g]
                    v.wait_ge(oT_hi, b * HEADS * PAIRS + h * PAIRS + (g + 1))
                    cols = slice(g * 2 * R, (g + 1) * 2 * R)
                    v.tensor_tensor(oTl[:, cols], slot[s][:, 0:2 * R], oTh[:, cols].bitcast(F32),
                                    ALU.subtract).then_inc(drained[s], 1)

                def add_tiles(at, scale):
                    for s, tiles in OUT_BATCHES:
                        u = at[s]
                        at[s] = u + 1
                        v.wait_ge(filled[s], u + 1)
                        for c, i in enumerate(tiles):
                            ps = slot[s][0:R, c * 512:c * 512 + D]
                            if scale:
                                last = v.scalar_tensor_tensor(x[:, i, :], ps, inv_sum[:, i:i + 1], x[:, i, :],
                                                              ALU.mult, ALU.add)
                            else:
                                last = v.tensor_tensor(x[:, i, :], x[:, i, :], ps, ALU.add)
                        last.then_inc(drained[s], 1)

                with v.Fori(0, BLOCKS) as b:
                    modulate(b, 0, in_ln1)
                    with v.Fori(0, HEADS) as h:
                        n = b * HEADS + h
                        v.wait_ge(q_hi, n + 1)
                        v.scalar_tensor_tensor(ql[:, :], slot["B"][:, 0:N], bq[:, 0:1], qh[:, :].bitcast(F32),
                                               ALU.add, ALU.subtract).then_inc(drained["B"], 1)
                        v_low(b, h, 0)
                        v_low(b, h, 1)
                        k_low(b, h, 0)
                        v_low(b, h, 2)
                        k_low(b, h, 1)
                        k_low(b, h, 2)
                        scores(b, h, 0)
                        scores(b, h, 1)
                        for g in range(PAIRS):
                            if g > 0:
                                head_out(b, h, g - 1)
                            for f in range(3):
                                transposed(b, h, 2 * g, f)
                            if g + 1 < PAIRS:
                                scores(b, h, 2 * g + 2)
                            transposed(b, h, 2 * g + 1, 0)
                            transposed(b, h, 2 * g + 1, 1)
                            if g + 1 < PAIRS:
                                scores(b, h, 2 * g + 3)
                            transposed(b, h, 2 * g + 1, 2)
                        v.tensor_scalar(row_sum[:, :], row_sum[:, :], 1e-30, None, ALU.max).then_inc(inv_ready, 1)
                        v.wait_ge(inv_ready, 2 * n + 1)
                        v.reciprocal(inv_sum[:, :], row_sum[:, :]).then_inc(inv_ready, 1)
                        head_out(b, h, PAIRS - 1)
                        v.wait_ge(inv_ready, 2 * n + 2)
                        v.wait_ge(x_biased, b * 2 * NT + NT)
                        add_tiles({"A": in_head("A", b, h, 7), "B": in_head("B", b, h, 6)}, True)
                    modulate(b, 1, in_ln2)
                    for m in range(KT):
                        s = "AB"[m % 2]
                        v.wait_ge(up_hi, b * KT + (m + 1))
                        v.tensor_tensor(upl[:, m, :], slot[s][:, 0:N], uph[:, m, :].bitcast(F32), ALU.subtract)\
                            .then_inc(drained[s], 1)
                    v.wait_ge(x_biased, b * 2 * NT + 2 * NT)
                    add_tiles({"A": in_mlp("A", b, 2), "B": in_mlp("B", b, 2)}, False)
                for s in "AB":
                    v.wait_ge(drained[s], BLOCKS * BLOCK_USES[s] + 1)
                v.wait_ge(x1_in, 16)
                for i in range(NT):
                    v.tensor_tensor(x[:, i, :], x[:, i, :], x1[:, i, :], ALU.add).then_inc(sum_ready, 1)

            @block.scalar
            def _(act):
                def hi(n, dest, loads, sem_in):
                    act.wait_ge(sem_in, loads)
                    act.activation(dest, stage[:, :], ACT.Copy).then_inc(hi_split, 1)

                matrices = BLOCK_ITEMS - 4

                def matrix_hi(b, n, dest, h=None):
                    count = b * matrices * 16 + (16 * (n + 1))
                    if h is not None:
                        count = b * matrices * 16 + h * HEAD_ITEMS * 16 + (16 * (3 + n + 1))
                    hi(None, dest, count, staged)

                def mod_hi(b, n):
                    hi(None, mod_w[:, n % 2, :], b * 4 * 128 + 128 * (n + 1), mod_staged)

                def flat(t):
                    return t[:, :, :].rearrange("p k c -> p (k c)")

                def norm(b, ln, at, between):
                    act.wait_ge(stats_done, b * 4 + (2 * ln + 2))
                    act.activation(rstd[:, :], mean_var[:, :, 1], ACT.Sqrt, bias=eps_col[:, 0:1])\
                        .then_inc(root_done, 1)
                    act.wait_ge(rstd_ready, b * 4 + (2 * ln + 2))

                    def high(i):
                        s = "TU"[i % 2]
                        act.wait_ge(filled[s], at(s, b, i // 2) + 1)
                        act.activation(yTh[:, :, i * R:(i + 1) * R],
                                       slot[s][:, 0:KT * R].rearrange("p (k n) -> p k n", k=KT), ACT.Copy)\
                            .then_inc(yT_hi, 1)

                    for i in range(NT):
                        if i >= 2:
                            act.wait_ge(scaled, b * 2 * NT + (ln * NT + i - 1))
                        act.activation(xn[:, i % 2, :], x[:, i, :], ACT.Identity, bias=shift[:, i:i + 1],
                                       scale=rstd[:, i:i + 1]).then_inc(xn_ready, 1)
                        if i >= 2:
                            high(i - 2)
                        if i % 2 == 1 and i >= 3:
                            between(i // 2 - 1)
                    high(NT - 2)
                    high(NT - 1)

                def exponentials(b, h, i):
                    n = b * HEADS * NT + h * NT + i
                    act.wait_ge(max_ready, n + 1)
                    act.activation(probs[:, i % 2, :], probs[:, i % 2, :], ACT.Exp, bias=neg_max[:, i:i + 1],
                                   scale=QSCALE, accum_out=row_sum[:, i:i + 1]).then_inc(probs_ready, 1)

                def transposed(b, h, i, f):
                    j, m = PARTS[f]
                    s, u = PART_SLOT[i, f]
                    act.wait_ge(filled[s], in_head(s, b, h, u) + 1)
                    act.activation(probsTh[0:R, j:j + m, i % 2 * R:(i % 2 + 1) * R],
                                   slot[s][0:R, 0:m * R].rearrange("p (j n) -> p j n", j=m), ACT.Copy)\
                        .then_inc(probsT_hi, 1)

                def head_out(b, h, g):
                    s, u = OUT_SLOT[g]
                    act.wait_ge(filled[s], in_head(s, b, h, u) + 1)
                    act.activation(oTh[:, g * 2 * R:(g + 1) * 2 * R], slot[s][:, 0:2 * R], ACT.Copy)\
                        .then_inc(oT_hi, 1)

                def k_high(b, h, c):
                    at, n = CHUNKS[c]
                    if c < 2:
                        act.wait_ge(k_part, b * HEADS * 2 + h * 2 + (c + 1))
                    else:
                        act.wait_ge(filled["A"], in_head("A", b, h, 1) + 1)
                    act.activation(kh[:, at:at + n], slot["A"][:, at:at + n], ACT.Identity, bias=bk[:, 0:1])\
                        .then_inc(k_hi, 1)

                def v_high(b, h, f):
                    j, m = PARTS[f]
                    s, u = V_SLOT[f]
                    act.wait_ge(filled[s], in_head(s, b, h, u) + 1)
                    act.activation(vh[:, j:j + m, :], slot[s][0:R, 0:m * DH].rearrange("p (j c) -> p j c", j=m),
                                   ACT.Copy).then_inc(v_hi, 1)

                def head(b, h, weights):
                    act.wait_ge(filled["A"], in_head("A", b, h, 0) + 1)
                    act.activation(vT[:, :], slot["A"][:, 0:N], ACT.Identity, bias=bv[:, 0:1])\
                        .then_inc(drained["A"], 1)
                    act.wait_ge(filled["B"], in_head("B", b, h, 0) + 1)
                    act.activation(qh[:, :], slot["B"][:, 0:N], ACT.Identity, bias=bq[:, 0:1])\
                        .then_inc(q_hi, 1)
                    v_high(b, h, 0)
                    v_high(b, h, 1)
                    k_high(b, h, 0)
                    v_high(b, h, 2)
                    k_high(b, h, 1)
                    k_high(b, h, 2)
                    exponentials(b, h, 0)
                    exponentials(b, h, 1)
                    for g in range(PAIRS):
                        if g > 0:
                            head_out(b, h, g - 1)
                        for f in range(3):
                            transposed(b, h, 2 * g, f)
                        if g + 1 < PAIRS:
                            weights(g)
                        transposed(b, h, 2 * g + 1, 0)
                        transposed(b, h, 2 * g + 1, 1)
                        if g + 1 < PAIRS:
                            exponentials(b, h, 2 * g + 2)
                        transposed(b, h, 2 * g + 1, 2)
                        if g + 1 < PAIRS:
                            exponentials(b, h, 2 * g + 3)
                    head_out(b, h, PAIRS - 1)

                with act.Fori(0, BLOCKS) as b:
                    mod_hi(b, 0)
                    mod_hi(b, 1)
                    for n, w in enumerate((wqh, wkh, wvh)):
                        matrix_hi(b, n, flat(w))
                    norm(b, 0, in_ln1, lambda n: None)
                    with act.Fori(0, HEADS - 1) as h:
                        act.wait_ge(head_b_in, b * HEADS * 48 + h * 48 + 48)
                        head(b, h, lambda g: matrix_hi(b, g, (woh[:, :], flat(wqh), flat(wkh), flat(wvh))[g], h))

                    def last_head_weights(g):
                        if g == 0:
                            matrix_hi(b, 0, woh[:, :], HEADS - 1)
                        elif g < 3:
                            mod_hi(b, g + 1)

                    act.wait_ge(head_b_in, b * HEADS * 48 + HEADS * 48)
                    head(b, HEADS - 1, last_head_weights)
                    before = 3 + (HEADS - 1) * HEAD_ITEMS + 1
                    norm(b, 1, in_ln2, lambda k: matrix_hi(b, before + k, w1h[:, k, :]))
                    act.wait_ge(mlp_b_in, b * 16 + 16)
                    for m in range(KT):
                        s = "AB"[m % 2]
                        act.wait_ge(filled[s], in_mlp(s, b, m // 2) + 1)
                        act.activation(slot[s][:, 0:N], slot[s][:, 0:N], ACT.Relu, bias=mb1[:, m:m + 1])\
                            .then_inc(up_relu, 1)
                        act.wait_ge(up_relu, b * KT + (m + 1))
                        act.activation(uph[:, m, :], slot[s][:, 0:N], ACT.Copy).then_inc(up_hi, 1)
                        matrix_hi(b, before + KT + m, w2h[:, m, :])

            @block.tensor
            def _(pe):
                def free(s, u):
                    pe.wait_ge(drained[s], u + 1)

                def product(ps, w, src, start, stop):
                    (wh, wl), (sh, sl) = w, src
                    pe.matmul(ps, wh, sh, start=start, stop=False)
                    pe.matmul(ps, wh, sl, start=False, stop=False)
                    return pe.matmul(ps, wl, sh, start=False, stop=stop)

                def weights_split(n):
                    pe.wait_ge(lo_split, n + 2)

                def norm(b, ln, at):
                    def transposes(i):
                        s = "AB"[i % 2]
                        t = "TU"[i % 2]
                        pe.wait_ge(drained[s], at(s, b, i // 2) + 2)
                        free(t, at(t, b, i // 2))
                        for k in range(KT):
                            last = pe.transpose(slot[t][:, k * R:(k + 1) * R],
                                                y[:, i % 2, k * 128:(k + 1) * 128], ident[0:R, 0:R])
                        last.then_inc(filled[t], 1)

                    for i in range(NT):
                        s = "AB"[i % 2]
                        free(s, at(s, b, i // 2))
                        rows = condh[:, i * R:(i + 1) * R]
                        pe.matmul(slot[s][0:R, 0:D], rows, mod_w[:, 0, :], start=True, stop=True)
                        pe.matmul(slot[s][0:R, 512:512 + D], rows, mod_w[:, 1, :], start=True, stop=True)\
                            .then_inc(filled[s], 1)
                        if i >= 1:
                            transposes(i - 1)
                    transposes(NT - 1)

                def yT_whole(b, at):
                    for s in "TU":
                        pe.wait_ge(drained[s], at(s, b, PAIRS) + 1)

                def wide(s, w, src):
                    for k in range(KT):
                        (wh, wl), (sh, sl) = w(k), src(k)
                        for n_pass, (lhs, rhs) in enumerate(((wh, sh), (wh, sl), (wl, sh))):
                            for at, n in CHUNKS:
                                last = pe.matmul(slot[s][:, at:at + n], lhs, rhs[:, at:at + n],
                                                 start=(k == 0 and n_pass == 0), stop=(k == KT - 1 and n_pass == 2))
                    last.then_inc(filled[s], 1)

                def yT(k):
                    return yTh[:, k, :], yTl[:, k, :]

                def scores(b, h, i, c):
                    s, u = score_slot(i)
                    at, n = CHUNKS[c]
                    if c == 0:
                        free(s, in_head(s, b, h, u))
                    rows = slice(i * R, (i + 1) * R)
                    last = product(slot[s][0:R, at:at + n], (qh[:, rows], ql[:, rows]),
                                   (kh[:, at:at + n], kl[:, at:at + n]), True, True)
                    if c == len(CHUNKS) - 1:
                        last.then_inc(filled[s], 1)

                def transposes(b, h, i, f):
                    s, u = PART_SLOT[i, f]
                    free(s, in_head(s, b, h, u))
                    j, m = PARTS[f]
                    for c in range(m):
                        last = pe.transpose(slot[s][0:R, c * R:(c + 1) * R],
                                            probs[:, i % 2, (j + c) * R:(j + c + 1) * R], ident[0:R, 0:R])
                    last.then_inc(filled[s], 1)

                def v_tiles(b, h, f):
                    s, u = V_SLOT[f]
                    free(s, in_head(s, b, h, u))
                    j, m = PARTS[f]
                    for c in range(m):
                        last = pe.transpose(slot[s][0:R, c * DH:(c + 1) * DH],
                                            vT[:, (j + c) * R:(j + c + 1) * R], ident[:, :])
                    last.then_inc(filled[s], 1)

                def head_out(b, h, g):
                    s, u = OUT_SLOT[g]
                    free(s, in_head(s, b, h, u))
                    for j in range(NT):
                        if j == PARTS[2][0]:
                            t, w = PART_SLOT[2 * g + 1, 2]
                            pe.wait_ge(drained[t], in_head(t, b, h, w) + 2)
                        last = product(slot[s][:, 0:2 * R], (vh[:, j, :], vl[:, j, :]),
                                       (probsTh[:, j, :], probsTl[:, j, :]), j == 0, j == NT - 1)
                    last.then_inc(filled[s], 1)

                def row_tiles(at, tile):
                    for s, tiles in OUT_BATCHES:
                        u = at[s]
                        at[s] = u + 1
                        free(s, u)
                        for c, i in enumerate(tiles):
                            last = tile(slot[s][0:R, c * 512:c * 512 + D], i)
                        last.then_inc(filled[s], 1)

                def down_tile(ps, i):
                    rows = slice(i * R, (i + 1) * R)
                    for k in range(KT):
                        last = product(ps, (uph[:, k, rows], upl[:, k, rows]), (w2h[:, k, :], w2l[:, k, :]),
                                       k == 0, k == KT - 1)
                    return last

                with pe.Fori(0, BLOCKS) as b:
                    weights_split(item(b, 1))
                    norm(b, 0, in_ln1)
                    with pe.Fori(0, HEADS) as h:
                        n = b * HEADS + h
                        weights_split(head_item(b, h, -1))
                        yT_whole(b, in_ln1)
                        for s, w in (("A", (wvh, wvl)), ("B", (wqh, wql))):
                            free(s, in_head(s, b, h, 0))
                            wide(s, lambda k: (w[0][:, k, :], w[1][:, k, :]), yT)
                        free("A", in_head("A", b, h, 1))
                        v_tiles(b, h, 0)
                        v_tiles(b, h, 1)
                        for c, (at, m) in enumerate(CHUNKS):
                            for k in range(KT):
                                last = product(slot["A"][:, at:at + m], (wkh[:, k, :], wkl[:, k, :]),
                                               (yTh[:, k, at:at + m], yTl[:, k, at:at + m]), k == 0, k == KT - 1)
                            last.then_inc(k_part if c < 2 else filled["A"], 1)
                            if c == 0:
                                v_tiles(b, h, 2)
                        for c in range(3):
                            if c < 2:
                                pe.wait_ge(k_lo, b * HEADS * 2 + h * 2 + (c + 1))
                            else:
                                pe.wait_ge(drained["A"], in_head("A", b, h, 1) + 2)
                            scores(b, h, 0, c)
                        for c in range(3):
                            scores(b, h, 1, c)
                        for i in range(NT):
                            pe.wait_ge(probs_ready, n * NT + (i + 1))
                            for f in range(3):
                                transposes(b, h, i, f)
                                if i + 2 < NT:
                                    scores(b, h, i + 2, f)
                            if i % 2 == 1:
                                head_out(b, h, i // 2)

                        def out_tile(ps, i):
                            if i % 2 == 0:
                                s, u = OUT_SLOT[i // 2]
                                pe.wait_ge(drained[s], in_head(s, b, h, u) + 2)
                            rows = slice(i * R, (i + 1) * R)
                            return product(ps, (oTh[:, rows], oTl[:, rows]), (woh[:, :], wol[:, :]), True, True)

                        weights_split(head_item(b, h, 0))
                        row_tiles({"A": in_head("A", b, h, 7), "B": in_head("B", b, h, 6)}, out_tile)
                    weights_split(head_item(b, HEADS - 1, 2))
                    norm(b, 1, in_ln2)
                    weights_split(item(b, mlp_first + KT - 1))
                    yT_whole(b, in_ln2)
                    for m in range(KT):
                        s = "AB"[m % 2]
                        free(s, in_mlp(s, b, m // 2))
                        cols = slice(m * 128, (m + 1) * 128)
                        wide(s, lambda k: (w1h[:, k, cols], w1l[:, k, cols]), yT)
                    weights_split(item(b, mlp_first + 2 * KT - 1))
                    for s in "AB":
                        pe.wait_ge(drained[s], in_mlp(s, b, 2) + 1)
                    row_tiles({"A": in_mlp("A", b, 2), "B": in_mlp("B", b, 2)}, down_tile)


def embed_noise(nc, noise, p, cond, condh, stage, eps_col, slot, ph, turns, turns_i, e):
    ctx = ExitStack()
    with ctx:
        def sb(name, shape, dt=F32):
            return ctx.enter_context(nc.sbuf_tensor("e_" + name, shape, dt))

        def sem(name):
            return ctx.enter_context(nc.semaphore("e_" + name))

        F2 = 2 * NFREQ
        ph, turns, turns_i, e = ph[:, :], turns[:, :], turns_i[:, :], e[:, :]
        freq, offset, start = sb("freq", [F2, 1]), sb("offset", [F2, 1]), sb("start", [F2, 1])
        fw1, fb1, fw2, fb2 = sb("fw1", [F2, NOISE]), sb("fb1", [NOISE, 1]), sb("fw2", [NOISE, NOISE]), sb("fb2", [NOISE, 1])
        neg_fb1 = sb("neg_fb1", [NOISE, 1])
        loaded, consts, step = sem("cond_loaded"), sem("cond_consts"), sem("cond_step")
        sin_done, z_done, e_done, silu_done, c_done = (sem(n) for n in ("sin_done", "z_done", "e_done", "silu_done", "c_done"))
        with nc.Block() as block:
            @block.sync
            def _(sp):
                sp.dma_start(ph, broadcast_rows(noise.rearrange("n a -> (n a)"), F2)).then_inc(loaded, 16)
                sp.dma_start(fw1[:, :], p["f_w1"]).then_inc(loaded, 16)
                sp.dma_start(fw2[:, :], p["f_w2"]).then_inc(loaded, 16)
                sp.dma_start(fb1[:, :], p["f_b1"].rearrange("(p a) -> p a", a=1)).then_inc(loaded, 16)
                sp.dma_start(fb2[:, :], p["f_b2"].rearrange("(p a) -> p a", a=1)).then_inc(loaded, 16)

            @block.gpsimd
            def _(pool):
                for half in range(2):
                    at = slice(half * NFREQ, (half + 1) * NFREQ)
                    pool.iota(freq[at, :], pattern=[[0, 1]], base=1, channel_multiplier=1,
                              allow_small_or_imprecise_dtypes=True).then_inc(consts, 1)
                    pool.memset(offset[at, :], 0.25 * half).then_inc(consts, 1)
                    pool.memset(start[at, :], float(np.pi / 2) * half).then_inc(consts, 1)
                    pool.wait_ge(consts, 3 * half + 3)
                pool.memset(eps_col[:, :], EPS).then_inc(consts, 1)
                pool.memset(stage[:, :], 0.0).then_inc(consts, 1)
                pool.memset(cond[:, :], 0.0).then_inc(consts, 1)
                pool.wait_ge(consts, 9)
                pool.affine_select(out=cond[:, :], in_=cond[:, :], compare_op=ALU.not_equal, fill=1.0,
                                   base=-NOISE, pattern=[[0, N]], channel_multiplier=1).then_inc(consts, 1)

            @block.vector
            def _(v):
                n = [0]

                def link(instruction):
                    n[0] += 1
                    instruction.then_inc(step, 1)
                    v.wait_ge(step, n[0])

                v.wait_ge(consts, 10)
                v.wait_ge(loaded, 80)
                link(v.tensor_scalar(freq[:, :], freq[:, :], float(np.float32(TWO_PI / 16)), None, ALU.mult))
                link(v.tensor_scalar(ph, ph, freq[:, 0:1], None, ALU.mult))
                link(v.tensor_scalar(turns, ph, float(1 / TWO_PI), offset[:, 0:1], ALU.mult, ALU.add))
                link(v.tensor_copy(turns_i, turns))
                link(v.tensor_copy(turns, turns_i))
                for part in (PI_A, PI_B, PI_C):
                    link(v.scalar_tensor_tensor(ph, turns, -part, ph, ALU.mult, ALU.add))
                link(v.tensor_scalar(ph, ph, start[:, 0:1], None, ALU.add))
                link(v.tensor_scalar(ph, ph, PI_MAX, -PI_MAX, ALU.min, ALU.max))
                link(v.tensor_scalar(neg_fb1[:, :], fb1[:, :], -1.0, None, ALU.mult))
                v.wait_ge(e_done, 1)
                link(v.tensor_scalar(e, e, 1.0, None, ALU.add))
                link(v.reciprocal(e, e))
                v.scalar_tensor_tensor(e, slot["A"][0:NOISE, 0:N], fb1[:, 0:1], e, ALU.add, ALU.mult)\
                    .then_inc(silu_done, 1)
                v.wait_ge(c_done, 1)
                link(v.tensor_scalar(cond[0:NOISE, :], slot["B"][0:NOISE, 0:N], fb2[:, 0:1], None, ALU.add))
                for q in (0, 1):
                    link(v.tensor_copy(condh[32 * q:32 * q + 32, :], cond[0:32, :]))
                for q in (2, 3):
                    link(v.tensor_tensor(condh[32 * q:32 * q + 32, :], cond[0:32, :],
                                         condh[0:32, :].bitcast(F32), ALU.subtract))

            @block.scalar
            def _(act):
                act.wait_ge(step, 11)
                act.activation(ph, ph, ACT.Sin).then_inc(sin_done, 1)
                act.wait_ge(z_done, 1)
                act.activation(e, slot["A"][0:NOISE, 0:N], ACT.Exp, bias=neg_fb1[:, 0:1], scale=-1.0)\
                    .then_inc(e_done, 1)

            @block.tensor
            def _(pe):
                pe.wait_ge(loaded, 80)
                for w, src, ps, before, after in ((fw1, ph, slot["A"], sin_done, z_done),
                                                  (fw2, e, slot["B"], silu_done, c_done)):
                    pe.wait_ge(before, 1)
                    for at, m in CHUNKS:
                        last = pe.matmul(ps[0:NOISE, at:at + m], w[:, :], src[:, at:at + m], start=True, stop=True)
                    last.then_inc(after, 1)


PARAMS = ["f_w1", "f_b1", "f_w2", "f_b2", "s1_w", "s1_b", "b1_w", "b1_b", "wq", "bq", "wk", "bk", "wv", "bv",
          "wo", "bo", "s2_w", "s2_b", "b2_w", "b2_b", "m_w1", "m_b1", "m_w2", "m_b2"]
GCN_PARAMS = ["W1", "b1", "W2", "b2", "Wd1", "bd1", "Wd2", "bd2", "Wd3", "bd3"]


def build(nc, ap, out):
    x_keep = nc.dram_tensor("x1_keep", [N, D], F32, kind="Internal").ap()
    ctx = ExitStack()
    with ctx:
        def sb(name, shape, dt=F32):
            return ctx.enter_context(nc.sbuf_tensor(name, shape, dt))

        ident = sb("ident", [128, 128])
        x = sb("x", [R, NT, D])
        logc = sb("logc", [R, NT, N])
        with nc.sbuf_tensor("counts", [R, NT, N], F32) as counts:
            onehot_a = logc[:, :, :].rearrange("p t n -> p (t n)")[:, 0:GT * N // 2].bitcast(BF16)\
                .rearrange("p (t n) -> p t n", t=GT)
            count_edges(nc, ap["src"], ap["dst"], counts[:, :, :], onehot_a,
                        x[:, :, :].rearrange("p t d -> p (t d)"))
            gcn_layer(nc, ap["x"], *(ap["L0_gnn_" + n] for n in GCN_PARAMS), x_keep, x[:, :, :],
                      counts[:, :, :], logc[:, :, :], ident[:, :])
        transformer(nc, ap["node_vec1"], {n: ap["L1_gnn_" + n] for n in PARAMS}, x_keep, out,
                    x[:, :, :], logc[:, :, :], ident[:, :])


INPUTS = ["x", "src", "dst", "node_vec1"] + ["L0_gnn_" + n for n in GCN_PARAMS] + ["L1_gnn_" + n for n in PARAMS]


def kernel(**inputs):
    import concourse.bacc as bacc
    from concourse.bass_utils import run_bass_kernel_spmd

    nc = bacc.Bacc("TRN2", target_bir_lowering=False, num_devices=1)
    arrays, ap = {}, {}
    for name in INPUTS:
        a = np.ascontiguousarray(inputs[name])
        arrays[f"in_{name}_dram"] = a
        ap[name] = nc.dram_tensor(f"in_{name}_dram", a.shape, mybir.dt.from_np(a.dtype), kind="ExternalInput").ap()
    out = nc.dram_tensor("out_0_dram", (N, D), F32, kind="ExternalOutput").ap()
    build(nc, ap, out)
    r = run_bass_kernel_spmd(nc, [arrays], core_ids=[0])
    return r.results[0]["out_0_dram"]
```

```python
from contextlib import ExitStack

import numpy as np

import concourse.bass as bass
from concourse import mybir

F32 = mybir.dt.float32
F32R = mybir.dt.float32r
BF16 = mybir.dt.bfloat16
F16 = mybir.dt.float16
I32 = mybir.dt.int32
ALU = mybir.AluOpType
ACT = mybir.ActivationFunctionType

N = 1250
NT = 10
R = N // NT
E = 20000
D = 512
KT = D // 128
EPS = 1e-5
BLOCKS, HEADS = 4, 4
DH = D // HEADS
QSCALE = float(DH) ** -0.5
NEVER = -1e37
NEVER_MAX = 1e30

ET = E // R
GT = 16
GROUPS = ET // GT
HALF = N // 2
HPITCH = HALF + 1
SHIFT = 11
BASE = 1 << SHIFT
assert GT * R < BASE and GROUPS * GT == ET

NFREQ = 32
NOISE = 16
TWO_PI = 2.0 * np.pi
PI_A = 6.28125
PI_B = float(np.float32(np.float16(TWO_PI - PI_A)))
PI_C = float(np.float32(TWO_PI - PI_A - PI_B))
PI_MAX = 3.1415925

CHUNKS = [(0, 512), (512, 512), (1024, N - 1024)]


def broadcast_rows(row_ap, rows):
    return bass.AP(row_ap.tensor, row_ap.offset, [[0, rows]] + [list(p) for p in row_ap.ap])


def identity(pool, zeroed, done, t):
    pool.memset(t, 0.0).then_inc(zeroed, 1)
    pool.wait_ge(zeroed, 1)
    pool.affine_select(out=t, in_=t, compare_op=ALU.not_equal, fill=1.0, base=0,
                       pattern=[[-1, 128]], channel_multiplier=1).then_inc(done, 1)


def count_edges(nc, src, dst, counts, onehot_a, ids, scratch):
    ctx = ExitStack()
    with ctx:
        def sb(name, shape, dt):
            return ctx.enter_context(nc.sbuf_tensor(name, shape, dt))

        def sem(name):
            return ctx.enter_context(nc.semaphore(name))

        onehot_b = sb("onehot_b", [R, GT, N], BF16)
        ohs = [onehot_a, onehot_b[:, :, :]]
        ohd = sb("onehot_dst", [R, 2, GT, HPITCH], BF16)
        raw = sb("raw_edges", [R, 2, ET], I32)
        ends = sb("edge_ends", [R, 2, ET], F32)
        upper = sb("upper_half", [R, ET], F32)
        weight = sb("weight", [R, ET], F32)
        now = sb("group_pair", [R, 3, 2 * GT], F32)
        packed = scratch[:, 0:2 * HALF].bitcast(I32).rearrange("p (b c) -> p b c", b=2)
        parts = scratch[:, 2 * HALF:4 * HALF].bitcast(I32).rearrange("p (b c) -> p b c", b=2)
        ps = ctx.enter_context(nc.psum_tensor("count_ps", [128, 4, 2, 512], F32))
        edges_in, ids_in, counts_zero = sem("edges_in"), sem("ids_in"), sem("counts_zero")
        prep, group_copied, onehots_ready = sem("prep"), sem("group_copied"), sem("onehots_ready")
        ps_filled, ps_drained = sem("ps_filled"), sem("ps_drained")
        parts_ready, parts_added = sem("parts_ready"), sem("parts_added")
        H1 = 313
        split = [(0, H1), (H1, HALF - H1)]

        with nc.Block() as block:
            @block.sync
            def _(sp):
                sp.dma_start(raw[:, 0, :], src.rearrange("(p t) -> p t", t=ET)).then_inc(edges_in, 16)
                sp.dma_start(raw[:, 1, :], dst.rearrange("(p t) -> p t", t=ET)).then_inc(edges_in, 16)

            @block.gpsimd
            def _(pool):
                pool.iota(ids[:, :], pattern=[[1, N]], base=0, channel_multiplier=0,
                          allow_small_or_imprecise_dtypes=True).then_inc(ids_in, 1)
                pool.sem_inc(ps_drained, 1)
                pool.sem_inc(parts_added, 1)
                for i in range(NT):
                    pool.memset(counts[:, i, :], 0.0).then_inc(counts_zero, 1)

            @block.vector
            def _(v):
                v.wait_ge(edges_in, 32)
                v.tensor_copy(ends[:, :, :], raw[:, :, :]).then_inc(prep, 1)
                v.wait_ge(prep, 1)
                v.tensor_scalar(upper[:, :], ends[:, 1, :], float(HALF), None, ALU.is_ge).then_inc(prep, 1)
                v.wait_ge(prep, 2)
                v.tensor_scalar(weight[:, :], upper[:, :], float(BASE - 1), 1.0, ALU.mult,
                                ALU.add).then_inc(prep, 1)
                v.scalar_tensor_tensor(ends[:, 1, :], upper[:, :], -float(HALF), ends[:, 1, :],
                                       ALU.mult, ALU.add).then_inc(prep, 1)
                v.wait_ge(prep, 4)
                v.wait_ge(ids_in, 1)

                def onehots(half, first, pair):
                    for k, of in enumerate((ends[:, 0, :], ends[:, 1, :], weight[:, :])):
                        v.tensor_copy(now[:, k, half * GT:(half + 1) * GT],
                                      of[:, bass.ds(first, GT)]).then_inc(group_copied, 1)
                    v.wait_ge(group_copied, pair * 6 + (half + 1) * 3)
                    for t in range(GT):
                        c = half * GT + t
                        v.tensor_scalar(ohs[half][:, t, :], ids[:, :], now[:, 0, c:c + 1], None,
                                        ALU.is_equal)
                        last = v.tensor_scalar(ohd[:, half, t, 0:HALF], ids[:, 0:HALF], now[:, 1, c:c + 1],
                                               now[:, 2, c:c + 1], ALU.is_equal, ALU.mult)
                    last.then_inc(onehots_ready, 1)

                def add_group(half, p):
                    for m in range(NT):
                        k = half * NT + m
                        v.wait_ge(ps_drained, p * 2 * NT + (k + 2))
                        v.tensor_scalar(parts[:, 0, :], packed[:, k % 2, :], BASE - 1, None, ALU.bitwise_and)
                        v.tensor_scalar(parts[:, 1, :], packed[:, k % 2, :], SHIFT, None,
                                        ALU.logical_shift_right).then_inc(parts_ready, 1)
                        v.wait_ge(parts_ready, p * 2 * NT + (k + 1))
                        both = counts[:, m, :].rearrange("p (b c) -> p b c", b=2)
                        v.tensor_tensor(both, both, parts, ALU.add).then_inc(parts_added, 1)
                        v.wait_ge(parts_added, p * 2 * NT + (k + 2))

                onehots(0, 0, 0)
                onehots(1, GT, 0)
                v.wait_ge(counts_zero, NT)
                with v.Fori(0, GROUPS // 2 - 1) as p:
                    for half in range(2):
                        add_group(half, p)
                        onehots(half, p * (2 * GT) + (2 + half) * GT, p + 1)
                for half in range(2):
                    add_group(half, GROUPS // 2 - 1)

            @block.tensor
            def _(pe):
                with pe.Fori(0, GROUPS // 2) as p:
                    for half in range(2):
                        pe.wait_ge(onehots_ready, 2 * p + (half + 1))
                        for m in range(NT):
                            k = half * NT + m
                            pe.wait_ge(ps_drained, p * 2 * NT + (max(k - 3, 0) + 1))
                            for t in range(GT):
                                for c, (at, n) in enumerate(split):
                                    last = pe.matmul(ps[0:R, k % 4, c, 0:n], ohs[half][:, t, m * R:(m + 1) * R],
                                                     ohd[:, half, t, at:at + n], start=(t == 0),
                                                     stop=(t == GT - 1))
                            last.then_inc(ps_filled, 1)

            @block.scalar
            def _(act):
                with act.Fori(0, GROUPS // 2) as p:
                    for half in range(2):
                        for m in range(NT):
                            k = half * NT + m
                            act.wait_ge(ps_filled, p * 2 * NT + (k + 1))
                            act.wait_ge(parts_added, p * 2 * NT + (max(k - 1, 0) + 1))
                            act.activation(packed[:, k % 2, 0:H1], ps[0:R, k % 4, 0, 0:H1], ACT.Copy)
                            act.activation(packed[:, k % 2, H1:HALF], ps[0:R, k % 4, 1, 0:HALF - H1],
                                           ACT.Copy).then_inc(ps_drained, 1)


def row_stats(v, x, i, stats, mean_var, done, count):
    v.bn_stats(stats[:, i, :], x[:, i, :]).then_inc(done, 1)
    v.wait_ge(done, count + 1)
    v.bn_aggr(mean_var[:, i, :], stats[:, i, :]).then_inc(done, 1)


def embed_noise(nc, ctx, noise, p, condh, scratch, ring, filled, drained, z_fill, c_fill):
    def sb(name, shape, dt=F32):
        return ctx.enter_context(nc.sbuf_tensor("e_" + name, shape, dt))

    def sem(name):
        return ctx.enter_context(nc.semaphore("e_" + name))

    F2 = 2 * NFREQ
    ph, turns, turns_i = scratch[0:F2, 0:N], scratch[0:F2, N:2 * N], scratch[0:F2, 2 * N:3 * N].bitcast(I32)
    z, e = scratch[0:NOISE, N:2 * N], scratch[0:NOISE, 3 * N:4 * N]
    cond = scratch[0:32, 2 * N:3 * N]
    freq, offset, start = sb("freq", [F2, 1]), sb("offset", [F2, 1]), sb("start", [F2, 1])
    rest = scratch[:, 4 * N:]
    fw1, fw2 = rest[0:F2, 0:NOISE], rest[0:NOISE, NOISE:2 * NOISE]
    fb1, fb2 = rest[0:NOISE, 2 * NOISE:2 * NOISE + 1], rest[0:NOISE, 2 * NOISE + 1:2 * NOISE + 2]
    neg_fb1 = sb("neg_fb1", [NOISE, 1])
    loaded, consts, cond_ones, step = sem("cond_loaded"), sem("cond_consts"), sem("cond_ones"), sem("cond_step")
    sin_done, silu_done = sem("sin_done"), sem("silu_done")
    steps = [0]

    def load(sp):
        sp.dma_start(ph, broadcast_rows(noise.rearrange("n a -> (n a)"), F2)).then_inc(loaded, 16)
        sp.dma_start(fw1, p["f_w1"]).then_inc(loaded, 16)
        sp.dma_start(fw2, p["f_w2"]).then_inc(loaded, 16)
        sp.dma_start(fb1, p["f_b1"].rearrange("(p a) -> p a", a=1)).then_inc(loaded, 16)
        sp.dma_start(fb2, p["f_b2"].rearrange("(p a) -> p a", a=1)).then_inc(loaded, 16)

    def constants(pool):
        for half in range(2):
            at = slice(half * NFREQ, (half + 1) * NFREQ)
            pool.iota(freq[at, :], pattern=[[0, 1]], base=1, channel_multiplier=1,
                      allow_small_or_imprecise_dtypes=True).then_inc(consts, 1)
            pool.memset(offset[at, :], 0.25 * half).then_inc(consts, 1)
            pool.memset(start[at, :], float(np.pi / 2) * half).then_inc(consts, 1)
            pool.wait_ge(consts, 3 * half + 3)

    def ones_row(pool):
        pool.wait_ge(step, 11)
        pool.memset(cond, 0.0).then_inc(cond_ones, 1)
        pool.wait_ge(cond_ones, 1)
        pool.affine_select(out=cond, in_=cond, compare_op=ALU.not_equal, fill=1.0,
                           base=-NOISE, pattern=[[0, N]], channel_multiplier=1).then_inc(cond_ones, 1)

    def link(v, instruction):
        steps[0] += 1
        instruction.then_inc(step, 1)
        v.wait_ge(step, steps[0])

    def angles(v):
        v.wait_ge(consts, 6)
        v.wait_ge(loaded, 80)
        link(v, v.tensor_scalar(freq[:, :], freq[:, :], float(np.float32(TWO_PI / 16)), None, ALU.mult))
        link(v, v.tensor_scalar(ph, ph, freq[:, 0:1], None, ALU.mult))
        link(v, v.tensor_scalar(turns, ph, float(1 / TWO_PI), offset[:, 0:1], ALU.mult, ALU.add))
        link(v, v.tensor_copy(turns_i, turns))
        link(v, v.tensor_copy(turns, turns_i))
        for part in (PI_A, PI_B, PI_C):
            link(v, v.scalar_tensor_tensor(ph, turns, -part, ph, ALU.mult, ALU.add))
        link(v, v.tensor_scalar(ph, ph, start[:, 0:1], None, ALU.add))
        link(v, v.tensor_scalar(ph, ph, PI_MAX, -PI_MAX, ALU.min, ALU.max))
        link(v, v.tensor_scalar(neg_fb1[:, :], fb1, -1.0, None, ALU.mult))

    def sine(act):
        act.wait_ge(step, 11)
        act.activation(ph, ph, ACT.Sin).then_inc(sin_done, 1)

    def product(pe, w, src, ready, fill, free):
        pe.wait_ge(ready, 1)
        for c, (at, m) in enumerate(CHUNKS):
            free(fill + c)
            pe.matmul(ring[0:NOISE, (fill + c) % 4, 0:m], w, src[:, at:at + m], start=True, stop=True)\
                .then_inc(filled, 1)

    def first_product(pe, free):
        product(pe, fw1, ph, sin_done, z_fill, free)

    def second_product(pe, free):
        product(pe, fw2, e, silu_done, c_fill, free)

    def sigmoid_parts(act):
        for c, (at, m) in enumerate(CHUNKS):
            k = z_fill + c
            act.wait_ge(filled, k + 1)
            act.activation(z[:, at:at + m], ring[0:NOISE, k % 4, 0:m], ACT.Identity, bias=fb1[:, 0:1])
            act.activation(e[:, at:at + m], ring[0:NOISE, k % 4, 0:m], ACT.Exp, bias=neg_fb1[:, 0:1], scale=-1.0)\
                .then_inc(drained, 1)

    def silu(v):
        v.wait_ge(drained, z_fill + len(CHUNKS))
        link(v, v.tensor_scalar(e, e, 1.0, None, ALU.add))
        link(v, v.reciprocal(e, e))
        v.tensor_tensor(e, z, e, ALU.mult).then_inc(silu_done, 1)

    def with_bias(act):
        act.wait_ge(cond_ones, 2)
        for c, (at, m) in enumerate(CHUNKS):
            k = c_fill + c
            act.wait_ge(filled, k + 1)
            act.activation(cond[0:NOISE, at:at + m], ring[0:NOISE, k % 4, 0:m], ACT.Identity, bias=fb2[:, 0:1])\
                .then_inc(drained, 1)

    def halves(v):
        v.wait_ge(drained, c_fill + len(CHUNKS))
        v.wait_ge(cond_ones, 2)
        for q in (0, 1):
            link(v, v.tensor_copy(condh[32 * q:32 * q + 32, :], cond[0:32, :]))
        for q in (2, 3):
            link(v, v.tensor_tensor(condh[32 * q:32 * q + 32, :], cond[0:32, :],
                                    condh[0:32, :].bitcast(F32), ALU.subtract))

    return {"load": load, "constants": constants, "ones_row": ones_row, "angles": angles, "sine": sine,
            "first_product": first_product, "second_product": second_product,
            "sigmoid_parts": sigmoid_parts, "silu": silu, "with_bias": with_bias, "halves": halves}


def gcn_layer(nc, noise, noise_params, condh, x_in, w1, b1, w2, b2, wd1, bd1, wd2, bd2, wd3, bd3,
              x_keep, x, counts, logc, ident):
    HID, LAT, DEC = w1.shape[0], w2.shape[0], wd2.shape[0]
    MC = DEC // 128
    ctx = ExitStack()
    with ctx:
        def sb(name, shape, dt=F32):
            return ctx.enter_context(nc.sbuf_tensor(name, shape, dt))

        def sem(name):
            return ctx.enter_context(nc.semaphore(name))

        xb = sb("xb", [R, NT, D])
        h = sb("h_tile", [R, 2, D])
        hT = sb("hT", [128, KT, N])
        y1T = hT[:, 0, :]
        y2T = hT[:, 1:1 + MC, :]
        no_edge = hT[0:R, 1 + MC, :]
        g1, t1 = sb("g1", [R, NT, HID]), sb("t1", [R, NT, HID])
        g2, t2 = sb("g2", [R, NT, LAT]), sb("t2", [R, NT, LAT])
        rT, zT = sb("rT", [HID, N]), sb("zT", [LAT, N])
        w1r, w1T = sb("w1r", [HID, D]), sb("w1T", [128, KT, HID])
        w2r, w2T = sb("w2r", [LAT, HID]), sb("w2T", [HID, LAT])
        wd1r, wd1T = sb("wd1r", [HID, LAT]), sb("wd1T", [LAT, HID])
        wd2r, wd2T = sb("wd2r", [128, MC, HID]), sb("wd2T", [HID, DEC])
        wd3r, wd3T = sb("wd3r", [128, KT, DEC]), sb("wd3T", [128, MC, D])
        b1c, b2c, bd1c, bd2c = sb("b1c", [HID, 1]), sb("b2c", [LAT, 1]), sb("bd1c", [HID, 1]), sb("bd2c", [128, MC])
        bd3b = h[:, 0, :]
        eps_col = sb("eps_col", [R, 1])
        stats, mean_var = sb("stats", [R, NT, 6]), sb("mean_var", [R, NT, 2])
        rstd, shift = sb("rstd", [R, NT]), sb("shift", [R, NT])
        ones, deg, dinv = sb("ones", [R, 1]), sb("deg", [R, NT]), sb("dinv", [R, NT])
        psd = ctx.enter_context(nc.psum_tensor("ring_dve", [128, 4, 512], F32))
        psa = ctx.enter_context(nc.psum_tensor("ring_act", [128, 4, 512], F32))
        x_loaded, w_loaded, b_loaded = sem("x_loaded"), sem("w_loaded"), sem("b_loaded")
        bd3_loaded = sem("bd3_loaded")
        ones_in, zeroed, ident_in = sem("ones_in"), sem("ident_zeroed"), sem("ident_in")
        stats_done, sqrt_done, rstd_done, h_ready = sem("stats_done"), sem("sqrt_done"), sem("rstd_done"), sem("h_ready")
        d_filled, d_drained = sem("d_filled"), sem("d_drained")
        a_filled, a_drained = sem("a_filled"), sem("a_drained")
        deg_ready, deg_sqrt, dinv_ready = sem("deg_ready"), sem("deg_sqrt"), sem("dinv_ready")
        t_sum, t_ready = sem("t_sum"), sem("t_ready")
        x_biased, x1_ready, x1_stored = sem("x_biased"), sem("x1_ready"), sem("x1_stored")
        log_in, log_done, log_masked = sem("log_in"), sem("log_done"), sem("log_masked")

        a_jobs = {"w": 0}
        a_jobs["z"] = 4 + MC
        a_jobs["t1T"] = a_jobs["z"] + len(CHUNKS)
        a_jobs["c"] = a_jobs["t1T"] + NT
        a_jobs["t2T"] = a_jobs["c"] + len(CHUNKS)
        a_jobs["y1"] = a_jobs["t2T"] + NT
        a_jobs["y2"] = a_jobs["y1"] + len(CHUNKS)
        a_end = a_jobs["y2"] + MC * len(CHUNKS)
        d_jobs = {"deg_row": 0, "hT": len(CHUNKS), "deg": len(CHUNKS) + NT}
        for at, name in enumerate(["hw1", "agg1", "hw2", "agg2", "y3"]):
            d_jobs[name] = d_jobs["deg"] + 1 + at * NT
        deg_row = x.rearrange("p t d -> p (t d)")[0:1, 3 * N:4 * N]
        cond = embed_noise(nc, ctx, noise, noise_params, condh, x.rearrange("p t d -> p (t d)"), psa,
                           a_filled, a_drained, a_jobs["z"], a_jobs["c"])

        with nc.Block() as block:
            @block.sync
            def _(sp):
                cond["load"](sp)
                xv = x_in.rearrange("(t p) d -> p t d", p=R)
                for i in range(NT):
                    sp.dma_start(xb[:, i, :], xv[:, i, :]).then_inc(x_loaded, 16)
                sp.dma_start(b1c[:, :], b1.rearrange("(p a) -> p a", a=1)).then_inc(b_loaded, 16)
                sp.dma_start(b2c[:, :], b2.rearrange("(p a) -> p a", a=1)).then_inc(b_loaded, 16)
                sp.dma_start(bd1c[:, :], bd1.rearrange("(p a) -> p a", a=1)).then_inc(b_loaded, 16)
                with nc.allow_non_contiguous_dma(reason="a bias of 256"):
                    sp.dma_start(bd2c[:, :], bd2.rearrange("(m p) -> p m", p=128)).then_inc(b_loaded, 16)
                sp.wait_ge(d_filled, d_jobs["hT"] + NT)
                sp.dma_start(bd3b, broadcast_rows(bd3, R)).then_inc(bd3_loaded, 16)
                for i in range(NT):
                    sp.wait_ge(x1_ready, i + 1)
                    sp.dma_start(x_keep.rearrange("(t p) d -> p t d", p=R)[:, i, :], xb[:, i, :])\
                      .then_inc(x1_stored, 16)
                sp.wait_ge(x1_stored, 16 * NT)

            @block.gpsimd
            def _(pool):
                pool.memset(ones[:, :], 1.0).then_inc(ones_in, 1)
                cond["constants"](pool)
                pool.memset(eps_col[:, :], EPS).then_inc(ones_in, 1)
                identity(pool, zeroed, ident_in, ident)
                cond["ones_row"](pool)
                pool.wait_ge(bd3_loaded, 16)
                for i in range(NT):
                    pool.wait_ge(h_ready, i + 1)
                    pool.tensor_tensor(xb[:, i, :], xb[:, i, :], bd3b, ALU.add).then_inc(x_biased, 1)

            @block.vector
            def _(v):
                cond["angles"](v)
                for i in range(NT):
                    v.wait_ge(x_loaded, 160)
                    row_stats(v, xb, i, stats, mean_var, stats_done, 2 * i)
                v.wait_ge(sqrt_done, 1)
                v.reciprocal(rstd[:, :], rstd[:, :]).then_inc(rstd_done, 1)
                v.wait_ge(rstd_done, 1)
                v.scalar_tensor_tensor(shift[:, :], mean_var[:, :, 0], -1.0, rstd[:, :], ALU.mult,
                                       ALU.mult).then_inc(rstd_done, 1)
                for c, (at, n) in enumerate(CHUNKS):
                    v.wait_ge(d_filled, c + 1)
                    v.tensor_scalar(deg_row[:, at:at + n], psd[0:1, c, 0:n], 1.0, None, ALU.add)\
                        .then_inc(d_drained, 1)
                for i in range(NT):
                    k = d_jobs["hT"] + i
                    v.wait_ge(d_filled, k + 1)
                    v.tensor_copy(hT[:, :, i * R:(i + 1) * R],
                                  psd[:, k % 4, 0:KT * R].rearrange("p (k n) -> p k n", k=KT))\
                        .then_inc(d_drained, 1)
                k = d_jobs["deg"]
                v.wait_ge(d_filled, k + 1)
                v.tensor_copy(deg[:, :], psd[0:R, k % 4, 0:NT]).then_inc(d_drained, 1)
                v.wait_ge(deg_sqrt, 1)
                v.reciprocal(dinv[:, :], deg[:, :]).then_inc(dinv_ready, 1)
                v.wait_ge(dinv_ready, 1)

                def scale_rows(job, g, width):
                    for i in range(NT):
                        k = d_jobs[job] + i
                        v.wait_ge(d_filled, k + 1)
                        v.tensor_scalar(g[:, i, :], psd[0:R, k % 4, 0:width], dinv[:, i:i + 1], None,
                                        ALU.mult).then_inc(d_drained, 1)

                def mask(i):
                    v.tensor_scalar(no_edge, counts[:, i, :], 0.0, NEVER, ALU.is_equal, ALU.mult)\
                        .then_inc(log_masked, 1)
                    v.wait_ge(log_done, i + 1)
                    v.wait_ge(log_masked, 2 * i + 1)
                    v.scalar_tensor_tensor(logc[:, i, :], logc[:, i, :], 1 / QSCALE, no_edge, ALU.mult,
                                           ALU.add).then_inc(log_masked, 1)
                    v.wait_ge(log_masked, 2 * i + 2)

                def aggregate(job, g, t, width, masks, between):
                    for i in range(NT):
                        k = d_jobs[job] + i
                        v.wait_ge(d_filled, k + 1)
                        v.tensor_tensor(t[:, i, :], psd[0:R, k % 4, 0:width], g[:, i, :], ALU.add)\
                            .then_inc(d_drained, 1)
                        v.wait_ge(d_drained, k + 1)
                        v.tensor_scalar(t[:, i, :], t[:, i, :], dinv[:, i:i + 1], None, ALU.mult)\
                            .then_inc(t_ready, 1)
                        if i % 2 == 1:
                            mask(masks[i // 2])
                        if i == 2:
                            between(v)

                scale_rows("hw1", g1, HID)
                for i in range(NT):
                    v.tensor_scalar(logc[:, i, :], counts[:, i, :], 1.0, None, ALU.max).then_inc(log_in, 1)
                aggregate("agg1", g1, t1, HID, range(0, NT // 2), cond["silu"])
                scale_rows("hw2", g2, LAT)
                aggregate("agg2", g2, t2, LAT, range(NT // 2, NT), cond["halves"])
                def norm_x1(i):
                    v.wait_ge(sqrt_done, i + 2)
                    v.reciprocal(rstd[:, i:i + 1], rstd[:, i:i + 1]).then_inc(rstd_done, 1)
                    v.wait_ge(rstd_done, 2 * i + 3)
                    v.scalar_tensor_tensor(shift[:, i:i + 1], mean_var[:, i, 0:1], -1.0, rstd[:, i:i + 1],
                                           ALU.mult, ALU.mult).then_inc(rstd_done, 1)

                for i in range(NT):
                    k = d_jobs["y3"] + i
                    v.wait_ge(d_filled, k + 1)
                    v.wait_ge(x_biased, i + 1)
                    v.tensor_tensor(xb[:, i, :], xb[:, i, :], psd[0:R, k % 4, :], ALU.add)\
                        .then_inc(d_drained, 1)
                    v.wait_ge(d_drained, k + 1)
                    v.bn_stats(stats[:, i, :], xb[:, i, :]).then_inc(x1_ready, 1)
                    v.wait_ge(x1_ready, i + 1)
                    v.bn_aggr(mean_var[:, i, :], stats[:, i, :]).then_inc(stats_done, 1)
                    if i >= 1:
                        norm_x1(i - 1)
                norm_x1(NT - 1)

            @block.scalar
            def _(act):
                act.dma_start(w1r[:, :], w1).then_inc(w_loaded, 16)
                act.dma_start(w2r[:, :], w2).then_inc(w_loaded, 16)
                act.dma_start(wd1r[:, :], wd1).then_inc(w_loaded, 16)
                act.dma_start(wd2r[:, :, :], wd2.rearrange("(m p) k -> p m k", p=128)).then_inc(w_loaded, 16)
                act.dma_start(wd3r[:, :, :], wd3.rearrange("(m p) k -> p m k", p=128)).then_inc(w_loaded, 16)

                act.wait_ge(ones_in, 2)
                cond["sine"](act)

                def drain(k, out, rows, cols, func=ACT.Copy, bias=0.0):
                    act.wait_ge(a_filled, k + 1)
                    act.activation(out, psa[0:rows, k % 4, 0:cols], func, bias=bias).then_inc(a_drained, 1)

                act.wait_ge(stats_done, 2 * NT)
                act.activation(rstd[:, :], mean_var[:, :, 1], ACT.Sqrt, bias=eps_col[:, 0:1]).then_inc(sqrt_done, 1)
                drain(0, w1T[:, :, :].rearrange("p k m -> p (k m)"), 128, KT * HID)
                drain(1, w2T[:, :], HID, LAT)
                drain(2, wd1T[:, :], LAT, HID)
                drain(3, wd2T[:, :], HID, DEC)
                for c in range(MC):
                    drain(4 + c, wd3T[:, c, :], 128, D)
                for i in range(NT):
                    if i == 0:
                        act.wait_ge(rstd_done, 2)
                    if i >= 2:
                        act.wait_ge(d_filled, d_jobs["hT"] + i - 1)
                    act.activation(h[:, i % 2, :], xb[:, i, :], ACT.Relu, bias=shift[:, i:i + 1],
                                   scale=rstd[:, i:i + 1]).then_inc(h_ready, 1)
                act.wait_ge(d_drained, d_jobs["deg"] + 1)
                act.activation(deg[:, :], deg[:, :], ACT.Sqrt).then_inc(deg_sqrt, 1)
                cond["sigmoid_parts"](act)
                for i in range(NT):
                    act.wait_ge(log_in, i + 1)
                    act.activation(logc[:, i, :], logc[:, i, :], ACT.Ln).then_inc(log_done, 1)
                act.wait_ge(b_loaded, 64)
                for i in range(NT):
                    drain(a_jobs["t1T"] + i, rT[:, i * R:(i + 1) * R], HID, R, ACT.Relu, b1c[:, 0:1])
                cond["with_bias"](act)
                for i in range(NT):
                    drain(a_jobs["t2T"] + i, zT[:, i * R:(i + 1) * R], LAT, R, ACT.Identity, b2c[:, 0:1])
                for c, (at, n) in enumerate(CHUNKS):
                    drain(a_jobs["y1"] + c, y1T[:, at:at + n], HID, n, ACT.Relu, bd1c[:, 0:1])
                for m in range(MC):
                    for c, (at, n) in enumerate(CHUNKS):
                        drain(a_jobs["y2"] + m * len(CHUNKS) + c, y2T[:, m, at:at + n], 128, n, ACT.Relu,
                              bd2c[:, m:m + 1])
                for t in range(NT + 1):
                    if t < NT:
                        act.wait_ge(stats_done, 2 * NT + t + 1)
                        act.activation(rstd[:, t:t + 1], mean_var[:, t, 1:2], ACT.Sqrt, bias=eps_col[:, 0:1])\
                            .then_inc(sqrt_done, 1)
                    i = t - 1
                    if i < 0:
                        continue
                    act.wait_ge(rstd_done, 2 * i + 4)
                    act.activation(x[:, i, :], xb[:, i, :], ACT.Relu, bias=shift[:, i:i + 1],
                                   scale=rstd[:, i:i + 1])

            @block.tensor
            def _(pe):
                def free_a(k):
                    if k >= 4:
                        pe.wait_ge(a_drained, k - 3)

                def free_d(k):
                    if k >= 4:
                        pe.wait_ge(d_drained, k - 3)

                pe.wait_ge(ones_in, 2)
                for c, (at, n) in enumerate(CHUNKS):
                    for s in range(NT):
                        last = pe.matmul(psd[0:1, c, 0:n], ones[:, :], counts[:, s, at:at + n],
                                         start=(s == 0), stop=(s == NT - 1))
                    last.then_inc(d_filled, 1)
                pe.wait_ge(w_loaded, 80)
                pe.wait_ge(ident_in, 1)
                for k in range(KT):
                    last = pe.transpose(psa[:, 0, k * 128:k * 128 + HID], w1r[:, k * 128:(k + 1) * 128],
                                        ident[0:HID, 0:HID])
                last.then_inc(a_filled, 1)
                pe.transpose(psa[0:HID, 1, 0:LAT], w2r[:, :], ident[0:LAT, 0:LAT]).then_inc(a_filled, 1)
                pe.transpose(psa[0:LAT, 2, 0:HID], wd1r[:, :], ident[0:HID, 0:HID]).then_inc(a_filled, 1)
                for m in range(MC):
                    last = pe.transpose(psa[0:HID, 3, m * 128:(m + 1) * 128], wd2r[:, m, :], ident)
                last.then_inc(a_filled, 1)
                for c in range(MC):
                    free_a(4 + c)
                    for m in range(KT):
                        last = pe.transpose(psa[:, (4 + c) % 4, m * 128:(m + 1) * 128],
                                            wd3r[:, m, c * 128:(c + 1) * 128], ident)
                    last.then_inc(a_filled, 1)
                for i in range(NT):
                    at = d_jobs["hT"] + i
                    free_d(at)
                    pe.wait_ge(h_ready, i + 1)
                    for k in range(KT):
                        last = pe.transpose(psd[:, at % 4, k * R:(k + 1) * R],
                                            h[:, i % 2, k * 128:(k + 1) * 128], ident[0:R, 0:R])
                    last.then_inc(d_filled, 1)
                k = d_jobs["deg"]
                free_d(k)
                for i in range(NT):
                    last = pe.matmul(psd[0:R, k % 4, i:i + 1], deg_row[:, i * R:(i + 1) * R], ones[0:1, :],
                                     start=True, stop=True)
                last.then_inc(d_filled, 1)
                pe.wait_ge(d_drained, d_jobs["hT"] + NT)
                pe.wait_ge(a_drained, 1)

                def rows(job, srcT, w, width, tiles):
                    for i in range(NT):
                        k = d_jobs[job] + i
                        free_d(k)
                        for c in range(tiles):
                            last = pe.matmul(psd[0:R, k % 4, 0:width], srcT(c)[:, i * R:(i + 1) * R], w(c),
                                             start=(c == 0), stop=(c == tiles - 1))
                        last.then_inc(d_filled, 1)

                def neighbours(job, g, width):
                    for i in range(NT):
                        k = d_jobs[job] + i
                        free_d(k)
                        for s in range(NT):
                            last = pe.matmul(psd[0:R, k % 4, 0:width], counts[:, s, i * R:(i + 1) * R],
                                             g[:, s, :], start=(s == 0), stop=(s == NT - 1))
                        last.then_inc(d_filled, 1)

                def transposes(job, t, width, ready):
                    for i in range(NT):
                        k = a_jobs[job] + i
                        free_a(k)
                        pe.wait_ge(t_ready, ready + i + 1)
                        pe.transpose(psa[0:width, k % 4, 0:R], t[:, i, :], ident[0:R, 0:R])\
                            .then_inc(a_filled, 1)

                rows("hw1", lambda c: hT[:, c, :], lambda c: w1T[:, c, :], HID, KT)
                cond["first_product"](pe, free_a)
                pe.wait_ge(d_drained, d_jobs["hw1"] + NT)
                neighbours("agg1", g1, HID)
                transposes("t1T", t1, HID, 0)
                cond["second_product"](pe, free_a)
                pe.wait_ge(a_drained, a_jobs["t1T"] + NT)
                rows("hw2", lambda c: rT[:, :], lambda c: w2T[:, :], LAT, 1)
                pe.wait_ge(d_drained, d_jobs["hw2"] + NT)
                neighbours("agg2", g2, LAT)
                transposes("t2T", t2, LAT, NT)
                pe.wait_ge(a_drained, a_jobs["t2T"] + NT)
                for c, (at, n) in enumerate(CHUNKS):
                    k = a_jobs["y1"] + c
                    free_a(k)
                    pe.matmul(psa[:, k % 4, 0:n], wd1T[:, :], zT[:, at:at + n], start=True, stop=True)\
                        .then_inc(a_filled, 1)
                pe.wait_ge(a_drained, a_jobs["y2"])
                for m in range(MC):
                    for c, (at, n) in enumerate(CHUNKS):
                        k = a_jobs["y2"] + m * len(CHUNKS) + c
                        free_a(k)
                        pe.matmul(psa[:, k % 4, 0:n], wd2T[:, m * 128:(m + 1) * 128], y1T[:, at:at + n],
                                  start=True, stop=True).then_inc(a_filled, 1)
                pe.wait_ge(a_drained, a_end)
                rows("y3", lambda c: y2T[:, c, :], lambda c: wd3T[:, c, :], D, MC)


PAIRS = NT // 2
XN = 3


def turns():
    uses, v_parts, parts, outs, at = {"T": 0, "U": 0}, [], {}, {}, 0

    def take():
        nonlocal at
        s = "TU"[at % 2]
        at += 1
        uses[s] += 1
        return s, uses[s] - 1

    for f in range(2):
        v_parts.append(take())
    for g in range(PAIRS):
        if g < PAIRS - 1:
            for i in (2 * g, 2 * g + 1):
                for f in range(3):
                    if (i, f) == (1, 2):
                        v_parts.append(take())
                    parts[i, f] = take()
        outs[g] = take()
    return uses, v_parts, parts, outs


TU_USES, V_SLOT, PART_SLOT, OUT_SLOT = turns()
PARTS = [(0, 4), (4, 4), (8, 2)]
HEAD_USES = {"A": 10, "B": 9, **TU_USES}
LAST_SLOT = {NT - 2: ("A", 7), NT - 1: ("B", 6)}
LAST_PARTS = [(i, f) for f in range(3) for i in (NT - 2, NT - 1)]
HEADS_USES = {s: HEADS * HEAD_USES[s] - (2 if s in "AB" else 0) for s in "ABTU"}
MLP_USES = {"A": 2, "B": 2, "T": 0, "U": 0}
BLOCK_USES = {s: HEADS_USES[s] + MLP_USES[s] for s in "ABTU"}
OUT_BATCHES = [("A", (0, 1, 2)), ("B", (3, 4, 5)), ("A", (6, 7)), ("B", (8, 9))]
TOP_ITEMS, HEAD_ITEMS, LAST_ITEMS, MLP_ITEMS = 5, 4, 3, 2 * KT
BLOCK_ITEMS = TOP_ITEMS + (HEADS - 1) * HEAD_ITEMS + LAST_ITEMS + MLP_ITEMS


def mlp_order(last):
    order = [("w", n) for n in range(2 * KT)]
    if not last:
        order.insert(PAIRS, ("mod", 0))
        order.insert(PAIRS + 3, ("mod", 1))
    return order


def mlp_place(kind, n, last):
    return mlp_order(last).index((kind, n))


def in_head(s, b, h, u):
    return b * BLOCK_USES[s] + h * HEAD_USES[s] + u


def in_mlp(s, b, u):
    return b * BLOCK_USES[s] + (HEADS_USES[s] + u)


V_USE = 2


def score_slot(i):
    if i == 0:
        return "A", 1
    return ("A", V_USE + i // 2) if i % 2 == 0 else ("B", 1 + i // 2)


def transformer(nc, condh, p, x_keep, out, x, logc, ident):
    ctx = ExitStack()
    with ctx:
        def sb(name, shape, dt=F32):
            return ctx.enter_context(nc.sbuf_tensor("c_" + name, shape, dt))

        def halves(name, shape):
            return sb(name + "h", shape, F32R), sb(name + "l", shape, F32R)

        def sem(name):
            return ctx.enter_context(nc.semaphore("c_" + name))

        def overlay(*tensors):
            with ExitStack() as scope:
                return [scope.enter_context(nc.sbuf_tensor("c_" + n, s, d)) for n, s, d in tensors]

        yTh, yTl = halves("yT", [128, KT, N])
        wqh, wql = halves("wq", [128, KT, DH])
        wkh, wkl = halves("wk", [128, KT, DH])
        wvh, wvl = halves("wv", [128, KT, DH])
        stage = sb("stage", [128, D])
        mod_w = sb("mod_w", [128, 2, D], F32R)
        bq, bk, bv = sb("bq", [DH, 1]), sb("bk", [DH, 1]), sb("bv", [DH, 1])
        row_bias, mb1 = sb("row_bias", [R, D]), sb("mb1", [128, KT])
        stats, mean_var = sb("stats", [R, NT, 6]), sb("mean_var", [R, NT, 2])
        rstd, shift, eps_col = sb("rstd", [R, NT]), sb("shift", [R, NT]), sb("eps_col", [R, 1])
        row_max, neg_max = sb("row_max", [R, NT]), sb("neg_max", [R, NT])
        row_sum, inv_sum = sb("row_sum", [R, NT]), sb("inv_sum", [R, NT])
        uph, upl, w1h, w1l, w2h, w2l = overlay(*((n, [128, KT, N], F32R) for n in ("uph", "upl")),
                                               *((n, [128, KT, D], F32R) for n in ("w1h", "w1l", "w2h", "w2l")))
        _, _, _, stage2 = overlay(("before4", [128, KT, N], F32), ("before5", [128, KT, N], F32),
                                  ("before6", [128, 4 * KT, D], F32), ("stage2", [128, D], F32))
        _, _, xn1, yT1 = overlay(("before1", [128, KT, N], F32), ("before2", [128, KT, N], F32),
                                 ("xn1", [R, XN, D], F32), ("yT1", [128, 2, KT, R], F32))
        _, xn2, yT2 = overlay(("before3", [128, KT, N], F32), ("xn2", [R, XN, D], F32), ("yT2", [128, 2, KT, R], F32))
        xn, yT_tile = (xn1, xn2), (yT1, yT2)
        probsTh, probsTl = halves("probsT", [R, NT, 2 * R])
        probs = sb("probs", [R, 2, N])
        qh, ql = halves("q", [DH, N])
        kh, kl = halves("k", [DH, N])
        vh, vl = halves("v", [R, NT, DH])
        vT, = overlay(("vT", [DH, N], F32))
        oTh, oTl = halves("oT", [DH, N])
        woh, wol = halves("wo", [DH, D])
        sb("stage2_end", [128, 120])

        slot = {"A": ctx.enter_context(nc.psum_tensor("slot_A", [128, 3 * 512], F32)),
                "B": ctx.enter_context(nc.psum_tensor("slot_B", [128, 3 * 512], F32)),
                "T": ctx.enter_context(nc.psum_tensor("slot_T", [128, 512], F32)),
                "U": ctx.enter_context(nc.psum_tensor("slot_U", [128, 512], F32))}
        filled = {s: sem(f"slot_{s}_filled") for s in "ABTU"}
        drained = {s: sem(f"slot_{s}_drained") for s in "ABTU"}
        mod_staged = sem("scale_weights_staged"), sem("bias_weights_staged")
        staged, hi_split, lo_split = sem("staged"), sem("weight_hi"), sem("weight_lo")
        head_b_in, mlp_b_in, row_bias_in = sem("head_biases_in"), sem("mlp_bias_in"), sem("row_bias_in")
        product_filled, product_drained = sem("product_filled"), sem("product_drained")
        scale_filled, y_ready = sem("scale_filled"), sem("y_ready")
        stats_done, var_ready, root_done = sem("stats_done"), sem("var_ready"), sem("root_done")
        inv_root, shift_ready, xn_ready = sem("inv_root"), sem("shift_ready"), sem("xn_ready")
        x_biased, scaled, stage2_cleared = sem("x_biased"), sem("scaled"), sem("stage2_cleared")
        cleared = sem("cleared")
        yT_filled, yT_taken, yT_lo, q_hi, k_hi, v_hi, probsT_hi, oT_hi, up_hi = (
            sem(n) for n in ("yT_filled", "yT_taken", "yT_lo", "q_hi", "k_hi", "v_hi", "probsT_hi", "oT_hi", "up_hi"))
        v_part, v_copied = sem("v_part_filled"), sem("v_part_copied")
        k_part, k_lo, up_relu = sem("k_part_filled"), sem("k_lo"), sem("up_relu")
        last_filled, last_split = sem("last_pair_filled"), sem("last_pair_split")
        max_ready, probs_ready, inv_ready = sem("max_ready"), sem("probs_ready"), sem("inv_ready")
        x1_in, sum_ready, stored = sem("x1_in"), sem("sum_ready"), sem("stored")
        waits_passed = {nc.vector: sem("dve_waits_passed"), nc.sync: sem("sp_waits_passed"),
                        nc.gpsimd: sem("pool_waits_passed")}

        product_banks = (slot["A"][0:R, 0:D], slot["A"][0:R, 512:512 + D])
        scale_banks = ((slot["A"][0:R, 1024:1024 + D], slot["B"][0:R, 0:D]),
                       (slot["B"][0:R, 512:512 + D], slot["B"][0:R, 1024:1024 + D]))

        def apart(engine):
            engine.sem_inc(waits_passed[engine], 1)

        def item(b, n):
            return b * BLOCK_ITEMS + n

        def head_item(b, h, n):
            return b * BLOCK_ITEMS + h * HEAD_ITEMS + (TOP_ITEMS + n)

        mlp_first = TOP_ITEMS + (HEADS - 1) * HEAD_ITEMS + LAST_ITEMS

        with nc.Block() as block:
            @block.sync
            def _(sp):
                def mod_weights(b, n, c, w, bias, t=stage):
                    sp.wait_ge(lo_split, n + 1)
                    apart(sp)
                    for q in range(4):
                        sp.dma_start(t[32 * q:32 * q + NOISE, :], p[w][b]).then_inc(mod_staged[c], 16)
                        sp.dma_start(t[32 * q + NOISE:32 * q + NOISE + 1, :], p[bias][bass.ds(b, 1)])\
                            .then_inc(mod_staged[c], 16)

                def matrix(n, w, t=None):
                    sp.wait_ge(lo_split, n + 1)
                    apart(sp)
                    sp.dma_start(stage[:, :] if t is None else t, w).then_inc(staged, 16)

                def head_matrix(b, h, n, name):
                    matrix(n, p[name].rearrange("b (k p) (h c) -> b h p k c", p=128, h=HEADS)[b, h],
                           stage[:, :].rearrange("p (k c) -> p k c", k=KT))

                def head_out_matrix(b, h, n):
                    matrix(n, p["wo"].rearrange("b (h c) n -> (b h) c n", h=HEADS)[b * HEADS + h])

                def head_biases(b, h):
                    for t, w in ((bq, p["bq"]), (bk, p["bk"]), (bv, p["bv"])):
                        w = w.rearrange("b (h c) -> (b h) c", h=HEADS)
                        sp.dma_start(t[:, :], w[bass.ds(b * HEADS + h, 1)].rearrange("a c -> c a"))\
                            .then_inc(head_b_in, 16)

                def row_biases(b, name):
                    sp.dma_start(row_bias[:, :], p[name][bass.ds(b, 1)].to_broadcast([R, D]))\
                        .then_inc(row_bias_in, 16)

                def mod1(b, n, c, t):
                    mod_weights(b, n, c, ("s1_w", "b1_w")[c], ("s1_b", "b1_b")[c], t)

                def top(b):
                    row_biases(b, "bo")
                    head_biases(b, 0)
                    with nc.allow_non_contiguous_dma(reason="a bias of 512 by columns"):
                        sp.dma_start(mb1[:, :], p["m_b1"].rearrange("b (k p) -> b p k", p=128)[b])\
                            .then_inc(mlp_b_in, 16)
                    for n, name in enumerate(("wq", "wk", "wv")):
                        head_matrix(b, 0, item(b, 2 + n), name)

                def body(b, last):
                    with sp.Fori(0, HEADS - 1) as h:
                        head_out_matrix(b, h, head_item(b, h, 0))
                        for n, name in enumerate(("wq", "wk", "wv")):
                            head_matrix(b, h + 1, head_item(b, h, 1 + n), name)
                        sp.wait_ge(drained["A"], in_head("A", b, h, V_USE + 1) + 1)
                        apart(sp)
                        sp.wait_ge(drained["B"], in_head("B", b, h, 1) + 1)
                        apart(sp)
                        head_biases(b, h + 1)
                    head_out_matrix(b, HEADS - 1, head_item(b, HEADS - 1, 0))
                    mod_weights(b, head_item(b, HEADS - 1, 1), 0, "s2_w", "s2_b")
                    mod_weights(b, head_item(b, HEADS - 1, 2), 1, "b2_w", "b2_b")
                    sp.wait_ge(x_biased, b * 2 * NT + NT)
                    apart(sp)
                    row_biases(b, "m_b2")
                    order = mlp_order(last)
                    for at, (kind, n) in enumerate(order):
                        if kind == "w":
                            before = at - 1 if at > 0 and order[at - 1][0] == "mod" else at
                            k = n % KT
                            matrix(item(b, mlp_first + before),
                                   p["m_w1" if n < KT else "m_w2"][b, k * 128:(k + 1) * 128, :])
                        else:
                            if n == 0:
                                sp.wait_ge(stage2_cleared, b + 1)
                                apart(sp)
                            mod1(b + 1, item(b, mlp_first + (mlp_place("mod", 0, last) + 1 if n else 0)), n, stage2)
                    if not last:
                        sp.wait_ge(x_biased, b * 2 * NT + 2 * NT)
                        apart(sp)
                        for s in "AB":
                            sp.wait_ge(drained[s], in_mlp(s, b, 2) + 1)
                            apart(sp)
                        top(b + 1)

                sp.wait_ge(cleared, 3)
                mod1(0, 0, 0, stage)
                mod1(0, 0, 1, stage2)
                top(0)
                with sp.Fori(0, BLOCKS - 1) as b:
                    body(b, False)
                body(BLOCKS - 1, True)
                for s in "AB":
                    sp.wait_ge(drained[s], in_mlp(s, BLOCKS - 1, 0) + 1)
                sp.dma_start(logc[:, :, 0:D], x_keep.rearrange("(t p) d -> p t d", p=R)).then_inc(x1_in, 16)
                outv = out.rearrange("(t p) d -> p t d", p=R)
                for i in range(NT):
                    sp.wait_ge(sum_ready, i + 1)
                    sp.dma_start(outv[:, i, :], x[:, i, :]).then_inc(stored, 16)
                sp.wait_ge(stored, 16 * NT)

            @block.gpsimd
            def _(pool):
                pool.memset(eps_col[:, :], EPS).then_inc(cleared, 1)
                pool.memset(stage[:, :], 0.0).then_inc(cleared, 1)
                pool.memset(stage2[:, :], 0.0).then_inc(cleared, 1)
                for s in "ABTU":
                    pool.sem_inc(drained[s], 1)
                pool.sem_inc(lo_split, 1)

                def lo(n, dest, hi):
                    pool.wait_ge(hi_split, n + 1)
                    pool.tensor_tensor(dest, stage[:, :], hi.bitcast(F32), ALU.subtract).then_inc(lo_split, 1)
                    pool.wait_ge(lo_split, n + 2)

                def mod_lo(n, c, t=stage):
                    pool.wait_ge(hi_split, n + 1)
                    for q in (1, 3):
                        rows = slice(32 * q, 32 * q + NOISE + 1)
                        last = pool.tensor_tensor(mod_w[rows, c, :], t[rows, :],
                                                  mod_w[rows, c, :].bitcast(F32), ALU.subtract)
                    last.then_inc(lo_split, 1)
                    pool.wait_ge(lo_split, n + 2)

                def flat(t):
                    return t[:, :, :].rearrange("p k c -> p (k c)")

                qkv = ((wqh, wql), (wkh, wkl), (wvh, wvl))

                def norm(b, ln, between):
                    for i in range(NT):
                        pool.wait_ge(yT_taken, b * 2 * NT + (ln * NT + i + 1))
                        cols = slice(i * R, (i + 1) * R)
                        pool.tensor_tensor(yTl[:, :, cols], yT_tile[ln][:, i % 2], yTh[:, :, cols].bitcast(F32),
                                           ALU.subtract).then_inc(yT_lo, 1)
                        pool.wait_ge(yT_lo, b * 2 * NT + (ln * NT + i + 1))
                        if i % 2 == 1:
                            between(i // 2)

                def add_bias(b, ln, i):
                    if i == 0:
                        pool.wait_ge(row_bias_in, b * 32 + (16 * ln + 16))
                    pool.wait_ge(xn_ready, b * 2 * NT + (ln * NT + i + 1))
                    pool.tensor_tensor(x[:, i, :], x[:, i, :], row_bias[:, :], ALU.add).then_inc(x_biased, 1)
                    pool.wait_ge(x_biased, b * 2 * NT + (ln * NT + i + 1))

                def top_weights(b, n):
                    if n < len(qkv):
                        lo(item(b, 2 + n), flat(qkv[n][1]), flat(qkv[n][0]))

                def mlp_weights(b, n, last):
                    k = n % KT
                    h_, l_ = (w1h, w1l) if n < KT else (w2h, w2l)
                    lo(item(b, mlp_first + mlp_place("w", n, last)), l_[:, k, :], h_[:, k, :])

                def body(b, last):
                    with pool.Fori(0, HEADS - 1) as h:
                        lo(head_item(b, h, 0), wol[:, :], woh[:, :])
                        for n, (h_, l_) in enumerate(qkv):
                            lo(head_item(b, h, 1 + n), flat(l_), flat(h_))
                    lo(head_item(b, HEADS - 1, 0), wol[:, :], woh[:, :])
                    mod_lo(head_item(b, HEADS - 1, 1), 0)
                    mod_lo(head_item(b, HEADS - 1, 2), 1)
                    norm(b, 1, lambda n: mlp_weights(b, n, last))
                    if not last:
                        pool.wait_ge(product_filled, b * 2 * NT + NT)
                        apart(pool)
                        pool.memset(stage2[:, :], 0.0).then_inc(stage2_cleared, 1)
                        pool.wait_ge(stage2_cleared, b + 1)
                    done = 0
                    for at, (kind, n) in enumerate(mlp_order(last)[PAIRS:]):
                        if kind == "w":
                            mlp_weights(b, n, last)
                            for i in range(done, min(done + 2, NT)):
                                add_bias(b, 1, i)
                                done = i + 1
                        else:
                            mod_lo(item(b, mlp_first + PAIRS + at), n, stage2)
                    for i in range(done, NT):
                        add_bias(b, 1, i)
                    if not last:
                        norm(b + 1, 0, lambda n: top_weights(b + 1, n))
                        for i in range(NT):
                            add_bias(b + 1, 0, i)

                mod_lo(0, 0)
                mod_lo(1, 1, stage2)
                norm(0, 0, lambda n: top_weights(0, n))
                for i in range(NT):
                    add_bias(0, 0, i)
                with pool.Fori(0, BLOCKS - 1) as b:
                    body(b, False)
                body(BLOCKS - 1, True)

            @block.vector
            def _(v):
                def norm(b, ln, add, products=0):
                    def count(i):
                        return b * 2 * NT + (ln * NT + i + 1)

                    for t in range(NT + 2):
                        if t < NT and add is not None:
                            add(t)
                        i = t - 1
                        if 0 <= i < NT:
                            v.wait_ge(root_done, count(i))
                            v.reciprocal(rstd[:, i:i + 1], rstd[:, i:i + 1]).then_inc(inv_root, 1)
                            v.wait_ge(inv_root, count(i))
                            v.scalar_tensor_tensor(shift[:, i:i + 1], mean_var[:, i, 0:1], -1.0, rstd[:, i:i + 1],
                                                   ALU.mult, ALU.mult).then_inc(shift_ready, 1)
                        if t < NT:
                            if add is not None:
                                v.wait_ge(product_drained, products + (t + 1))
                            v.bn_stats(stats[:, t, :], x[:, t, :]).then_inc(stats_done, 1)
                        i = t - 2
                        if i >= 0:
                            y = xn[ln][:, i % XN, :]
                            scale, bias = scale_banks[i % 2]
                            v.wait_ge(scale_filled, count(i))
                            v.wait_ge(xn_ready, count(i))
                            v.scalar_tensor_tensor(y, scale, 1.0, y, ALU.add, ALU.mult)\
                                .then_inc(scaled if ln == 0 else y_ready, 1)
                        if t < NT:
                            v.wait_ge(stats_done, count(t))
                            apart(v)
                            v.bn_aggr(mean_var[:, t, :], stats[:, t, :]).then_inc(var_ready, 1)
                        if i >= 0 and ln == 0:
                            v.wait_ge(scaled, b * NT + (i + 1))
                            v.tensor_tensor(y, y, bias, ALU.add).then_inc(y_ready, 1)

                def add_out(b, i):
                    v.wait_ge(product_filled, b * 2 * NT + (i + 1))
                    v.scalar_tensor_tensor(x[:, i, :], product_banks[i % 2], inv_sum[:, i:i + 1], x[:, i, :],
                                           ALU.mult, ALU.add).then_inc(product_drained, 1)

                def add_down(b, i):
                    v.wait_ge(x_biased, b * 2 * NT + (NT + i + 1))
                    v.wait_ge(product_filled, b * 2 * NT + (NT + i + 1))
                    v.tensor_tensor(x[:, i, :], x[:, i, :], product_banks[i % 2], ALU.add)\
                        .then_inc(product_drained, 1)

                def scores(b, h, i):
                    s, u = score_slot(i)
                    v.wait_ge(filled[s], in_head(s, b, h, u) + 1)
                    if i >= 2:
                        t, w = PART_SLOT[i - 2, 2]
                        v.wait_ge(filled[t], in_head(t, b, h, w) + 1)
                    apart(v)
                    v.tensor_tensor_reduce(out=probs[:, i % 2, :], in0=slot[s][0:R, 0:N], in1=logc[:, i, :],
                                           scale=1.0, scalar=-3e38, op0=ALU.add, op1=ALU.max,
                                           accum_out=row_max[:, i:i + 1]).then_inc(drained[s], 1)
                    v.wait_ge(drained[s], in_head(s, b, h, u) + 2)
                    v.tensor_scalar(neg_max[:, i:i + 1], row_max[:, i:i + 1], -QSCALE, NEVER_MAX, ALU.mult,
                                    ALU.min).then_inc(max_ready, 1)

                def transposed(b, h, i, f):
                    j, m = PARTS[f]
                    s, u = PART_SLOT[i, f]
                    v.wait_ge(probsT_hi, b * HEADS * NT * 3 + h * NT * 3 + (3 * i + f + 1))
                    dest = (slice(0, R), slice(j, j + m), slice(i % 2 * R, (i % 2 + 1) * R))
                    v.tensor_tensor(probsTl[dest], slot[s][0:R, 0:m * R].rearrange("p (j n) -> p j n", j=m),
                                    probsTh[dest].bitcast(F32), ALU.subtract).then_inc(drained[s], 1)

                def last_pair(b, h):
                    for at, (i, f) in enumerate(LAST_PARTS):
                        j, m = PARTS[f]
                        s = LAST_SLOT[i][0]
                        v.wait_ge(probsT_hi, b * HEADS * NT * 3 + h * NT * 3 + (3 * (NT - 2) + at + 1))
                        dest = (slice(0, R), slice(j, j + m), slice(i % 2 * R, (i % 2 + 1) * R))
                        v.tensor_tensor(probsTl[dest], slot[s][0:R, f * 512:f * 512 + m * R]
                                        .rearrange("p (j n) -> p j n", j=m), probsTh[dest].bitcast(F32),
                                        ALU.subtract).then_inc(last_split if f < 2 else drained[s], 1)

                def k_low(b, h, c):
                    at, n = CHUNKS[c]
                    v.wait_ge(k_hi, b * HEADS * 3 + h * 3 + (c + 1))
                    v.scalar_tensor_tensor(kl[:, at:at + n], slot["B"][:, at:at + n], bk[:, 0:1],
                                           kh[:, at:at + n].bitcast(F32), ALU.add, ALU.subtract)\
                        .then_inc(k_lo if c < 2 else drained["B"], 1)

                def v_low(b, h, f):
                    j, m = PARTS[f]
                    s, u = V_SLOT[f]
                    v.wait_ge(v_hi, b * HEADS * 3 + h * 3 + (f + 1))
                    v.tensor_tensor(vl[:, j:j + m, :], slot[s][0:R, 0:m * DH].rearrange("p (j c) -> p j c", j=m),
                                    vh[:, j:j + m, :].bitcast(F32), ALU.subtract).then_inc(drained[s], 1)

                def head_out(b, h, g):
                    s, u = OUT_SLOT[g]
                    v.wait_ge(oT_hi, b * HEADS * PAIRS + h * PAIRS + (g + 1))
                    cols = slice(g * 2 * R, (g + 1) * 2 * R)
                    v.tensor_tensor(oTl[:, cols], slot[s][:, 0:2 * R], oTh[:, cols].bitcast(F32),
                                    ALU.subtract).then_inc(drained[s], 1)

                def add_tiles(at):
                    for s, tiles in OUT_BATCHES:
                        u = at[s]
                        at[s] = u + 1
                        v.wait_ge(filled[s], u + 1)
                        for c, i in enumerate(tiles):
                            last = v.scalar_tensor_tensor(x[:, i, :], slot[s][0:R, c * 512:c * 512 + D],
                                                          inv_sum[:, i:i + 1], x[:, i, :], ALU.mult, ALU.add)
                        last.then_inc(drained[s], 1)

                def head(b, h):
                    n = b * HEADS + h
                    v.wait_ge(q_hi, n + 1)
                    v.scalar_tensor_tensor(ql[:, :], slot["A"][:, 0:N], bq[:, 0:1], qh[:, :].bitcast(F32),
                                           ALU.add, ALU.subtract).then_inc(drained["A"], 1)
                    for c in range(3):
                        k_low(b, h, c)
                    scores(b, h, 0)
                    scores(b, h, 1)
                    v_low(b, h, 0)
                    v_low(b, h, 1)
                    for g in range(PAIRS - 1):
                        if g > 0:
                            head_out(b, h, g - 1)
                        for f in range(3):
                            transposed(b, h, 2 * g, f)
                        scores(b, h, 2 * g + 2)
                        transposed(b, h, 2 * g + 1, 0)
                        transposed(b, h, 2 * g + 1, 1)
                        if g == 0:
                            v_low(b, h, 2)
                        scores(b, h, 2 * g + 3)
                        transposed(b, h, 2 * g + 1, 2)
                    last_pair(b, h)
                    head_out(b, h, PAIRS - 2)
                    v.tensor_scalar(row_sum[:, :], row_sum[:, :], 1e-30, None, ALU.max).then_inc(inv_ready, 1)
                    v.wait_ge(inv_ready, 2 * n + 1)
                    v.reciprocal(inv_sum[:, :], row_sum[:, :]).then_inc(inv_ready, 1)
                    head_out(b, h, PAIRS - 1)
                    v.wait_ge(inv_ready, 2 * n + 2)
                    v.wait_ge(x_biased, b * 2 * NT + NT)

                def body(b, last):
                    with v.Fori(0, HEADS - 1) as h:
                        head(b, h)
                        add_tiles({"A": in_head("A", b, h, 8), "B": in_head("B", b, h, 7)})
                    head(b, HEADS - 1)
                    norm(b, 1, lambda i: add_out(b, i), b * 2 * NT)
                    for m in range(KT):
                        s = "AB"[m % 2]
                        v.wait_ge(up_hi, b * KT + (m + 1))
                        v.tensor_tensor(upl[:, m, :], slot[s][:, 0:N], uph[:, m, :].bitcast(F32), ALU.subtract)\
                            .then_inc(drained[s], 1)
                    if not last:
                        norm(b + 1, 0, lambda i: add_down(b, i), b * 2 * NT + NT)

                norm(0, 0, None)
                with v.Fori(0, BLOCKS - 1) as b:
                    body(b, False)
                body(BLOCKS - 1, True)
                v.wait_ge(x1_in, 16)
                for i in range(NT):
                    add_down(BLOCKS - 1, i)
                    v.wait_ge(product_drained, BLOCKS * 2 * NT - NT + (i + 1))
                    v.tensor_tensor(x[:, i, :], x[:, i, :], logc[:, i, 0:D], ALU.add).then_inc(sum_ready, 1)

            @block.scalar
            def _(act):
                def hi(dest, loads, sem_in, t=stage):
                    act.wait_ge(sem_in, loads)
                    act.activation(dest, t[:, :], ACT.Copy).then_inc(hi_split, 1)

                matrices = BLOCK_ITEMS - 4

                def matrix_hi(b, n, dest, h=None):
                    count = b * matrices * 16 + (16 * (n + 1))
                    if h is not None:
                        count = b * matrices * 16 + h * HEAD_ITEMS * 16 + (16 * (3 + n + 1))
                    hi(dest, count, staged)

                def mod_hi(b, n, t=stage):
                    hi(mod_w[:, n % 2, :], b * 256 + 128 * (n // 2 + 1), mod_staged[n % 2], t)

                def flat(t):
                    return t[:, :, :].rearrange("p k c -> p (k c)")

                def norm(b, ln, between):
                    for t in range(NT + 3):
                        if t < NT:
                            act.wait_ge(var_ready, b * 2 * NT + (ln * NT + t + 1))
                            act.activation(rstd[:, t:t + 1], mean_var[:, t, 1:2], ACT.Sqrt, bias=eps_col[:, 0:1])\
                                .then_inc(root_done, 1)
                        i = t - 1
                        if 0 <= i < NT:
                            act.wait_ge(shift_ready, b * 2 * NT + (ln * NT + i + 1))
                            act.activation(xn[ln][:, i % XN, :], x[:, i, :], ACT.Identity, bias=shift[:, i:i + 1],
                                           scale=rstd[:, i:i + 1]).then_inc(xn_ready, 1)
                        i = t - 3
                        if i >= 0:
                            act.wait_ge(yT_filled, b * 2 * NT + (ln * NT + i + 1))
                            yT_i = slot["TU"[i % 2]][:, 0:KT * R].rearrange("p (k n) -> p k n", k=KT)
                            act.activation(yTh[:, :, i * R:(i + 1) * R], yT_i, ACT.Copy)
                            if i >= 2:
                                act.wait_ge(yT_lo, b * 2 * NT + (ln * NT + i - 1))
                            act.activation(yT_tile[ln][:, i % 2], yT_i, ACT.Copy).then_inc(yT_taken, 1)
                            if i % 2 == 1:
                                between(i // 2)

                def exponentials(b, h, i):
                    n = b * HEADS * NT + h * NT + i
                    act.wait_ge(max_ready, n + 1)
                    act.activation(probs[:, i % 2, :], probs[:, i % 2, :], ACT.Exp, bias=neg_max[:, i:i + 1],
                                   scale=QSCALE, accum_out=row_sum[:, i:i + 1]).then_inc(probs_ready, 1)

                def transposed(b, h, i, f):
                    j, m = PARTS[f]
                    s, u = PART_SLOT[i, f]
                    act.wait_ge(filled[s], in_head(s, b, h, u) + 1)
                    act.activation(probsTh[0:R, j:j + m, i % 2 * R:(i % 2 + 1) * R],
                                   slot[s][0:R, 0:m * R].rearrange("p (j n) -> p j n", j=m), ACT.Copy)\
                        .then_inc(probsT_hi, 1)

                def head_out(b, h, g):
                    s, u = OUT_SLOT[g]
                    act.wait_ge(filled[s], in_head(s, b, h, u) + 1)
                    act.activation(oTh[:, g * 2 * R:(g + 1) * 2 * R], slot[s][:, 0:2 * R], ACT.Copy)\
                        .then_inc(oT_hi, 1)

                def last_pair(b, h):
                    for at, (i, f) in enumerate(LAST_PARTS):
                        j, m = PARTS[f]
                        s, u = LAST_SLOT[i]
                        if f < 2:
                            act.wait_ge(last_filled, b * HEADS * 4 + h * 4 + (at + 1))
                        else:
                            act.wait_ge(filled[s], in_head(s, b, h, u) + 1)
                        act.activation(probsTh[0:R, j:j + m, i % 2 * R:(i % 2 + 1) * R],
                                       slot[s][0:R, f * 512:f * 512 + m * R].rearrange("p (j n) -> p j n", j=m),
                                       ACT.Copy).then_inc(probsT_hi, 1)

                def k_high(b, h, c):
                    at, n = CHUNKS[c]
                    if c < 2:
                        act.wait_ge(k_part, b * HEADS * 2 + h * 2 + (c + 1))
                    else:
                        act.wait_ge(filled["B"], in_head("B", b, h, 0) + 1)
                    act.activation(kh[:, at:at + n], slot["B"][:, at:at + n], ACT.Identity, bias=bk[:, 0:1])\
                        .then_inc(k_hi, 1)

                def v_copy(b, h, c):
                    at, n = CHUNKS[c]
                    if c < 2:
                        act.wait_ge(v_part, b * HEADS * 2 + h * 2 + (c + 1))
                    else:
                        act.wait_ge(filled["A"], in_head("A", b, h, V_USE) + 1)
                    act.activation(vT[:, at:at + n], slot["A"][:, at:at + n], ACT.Identity, bias=bv[:, 0:1])\
                        .then_inc(v_copied if c < 2 else drained["A"], 1)

                def v_high(b, h, f):
                    j, m = PARTS[f]
                    s, u = V_SLOT[f]
                    act.wait_ge(filled[s], in_head(s, b, h, u) + 1)
                    act.activation(vh[:, j:j + m, :], slot[s][0:R, 0:m * DH].rearrange("p (j c) -> p j c", j=m),
                                   ACT.Copy).then_inc(v_hi, 1)

                def head(b, h, weights):
                    act.wait_ge(filled["A"], in_head("A", b, h, 0) + 1)
                    act.activation(qh[:, :], slot["A"][:, 0:N], ACT.Identity, bias=bq[:, 0:1])\
                        .then_inc(q_hi, 1)
                    for c in range(3):
                        k_high(b, h, c)
                    exponentials(b, h, 0)
                    exponentials(b, h, 1)
                    v_copy(b, h, 0)
                    v_copy(b, h, 1)
                    v_high(b, h, 0)
                    v_copy(b, h, 2)
                    v_high(b, h, 1)
                    for g in range(PAIRS - 1):
                        if g > 0:
                            head_out(b, h, g - 1)
                        for f in range(3):
                            transposed(b, h, 2 * g, f)
                        weights(g)
                        transposed(b, h, 2 * g + 1, 0)
                        transposed(b, h, 2 * g + 1, 1)
                        if g == 0:
                            v_high(b, h, 2)
                        exponentials(b, h, 2 * g + 2)
                        transposed(b, h, 2 * g + 1, 2)
                        exponentials(b, h, 2 * g + 3)
                    last_pair(b, h)
                    head_out(b, h, PAIRS - 2)
                    head_out(b, h, PAIRS - 1)

                qkv_high = (wqh, wkh, wvh)

                def top_weights(b, n):
                    if n < len(qkv_high):
                        matrix_hi(b, n, flat(qkv_high[n]))

                def mlp_weights(b, n):
                    before = 3 + (HEADS - 1) * HEAD_ITEMS + 1
                    matrix_hi(b, before + n, (w1h if n < KT else w2h)[:, n % KT, :])

                def last_head_weights(b, g):
                    if g == 0:
                        matrix_hi(b, 0, woh[:, :], HEADS - 1)
                    elif g < 3:
                        mod_hi(b, g + 1)

                def body(b, last):
                    with act.Fori(0, HEADS - 1) as h:
                        act.wait_ge(head_b_in, b * HEADS * 48 + h * 48 + 48)
                        head(b, h, lambda g: matrix_hi(b, g, (woh[:, :], flat(wqh), flat(wkh), flat(wvh))[g], h))
                    act.wait_ge(head_b_in, b * HEADS * 48 + HEADS * 48)
                    head(b, HEADS - 1, lambda g: last_head_weights(b, g))
                    norm(b, 1, lambda n: mlp_weights(b, n))
                    act.wait_ge(mlp_b_in, b * 16 + 16)
                    order = mlp_order(last)
                    for m in range(KT):
                        s = "AB"[m % 2]
                        act.wait_ge(filled[s], in_mlp(s, b, m // 2) + 1)
                        act.activation(slot[s][:, 0:N], slot[s][:, 0:N], ACT.Relu, bias=mb1[:, m:m + 1])\
                            .then_inc(up_relu, 1)
                        act.wait_ge(up_relu, b * KT + (m + 1))
                        act.activation(uph[:, m, :], slot[s][:, 0:N], ACT.Copy).then_inc(up_hi, 1)
                        for kind, n in (order[PAIRS:PAIRS + 2], order[PAIRS + 2:PAIRS + 3], order[PAIRS + 3:], [])[m]:
                            if kind == "w":
                                mlp_weights(b, n)
                            else:
                                mod_hi(b + 1, n, stage2)
                    if not last:
                        norm(b + 1, 0, lambda n: top_weights(b + 1, n))

                act.wait_ge(cleared, 3)
                mod_hi(0, 0)
                mod_hi(0, 1, stage2)
                norm(0, 0, lambda n: top_weights(0, n))
                with act.Fori(0, BLOCKS - 1) as b:
                    body(b, False)
                body(BLOCKS - 1, True)

            @block.tensor
            def _(pe):
                def free(s, u):
                    pe.wait_ge(drained[s], u + 1)

                def product(ps, w, src, start, stop):
                    (wh, wl), (sh, sl) = w, src
                    pe.matmul(ps, wh, sh, start=start, stop=False)
                    pe.matmul(ps, wh, sl, start=False, stop=False)
                    return pe.matmul(ps, wl, sh, start=False, stop=stop)

                def weights_split(n):
                    pe.wait_ge(lo_split, n + 2)

                def norm(b, ln, product_tile):
                    for t in range(NT + 3):
                        if t < NT and product_tile is not None:
                            product_tile(t)
                        i = t - 1
                        if 0 <= i < NT:
                            if i >= 2:
                                pe.wait_ge(y_ready, b * 2 * NT + (ln * NT + i - 1))
                            rows = condh[:, i * R:(i + 1) * R]
                            scale, bias = scale_banks[i % 2]
                            last = pe.matmul(scale, rows, mod_w[:, 0, :], start=True, stop=True)
                            if ln == 0:
                                last = pe.matmul(bias, rows, mod_w[:, 1, :], start=True, stop=True)
                            last.then_inc(scale_filled, 1)
                        i = t - 3
                        if i >= 0:
                            s = "TU"[i % 2]
                            pe.wait_ge(y_ready, b * 2 * NT + (ln * NT + i + 1))
                            if i >= 2:
                                pe.wait_ge(yT_taken, b * 2 * NT + (ln * NT + i - 1))
                            elif ln == 1:
                                free(s, in_mlp(s, b, 0))
                            for k in range(KT):
                                part, cols = slot[s][:, k * R:(k + 1) * R], slice(k * 128, (k + 1) * 128)
                                if ln == 0:
                                    last = pe.transpose(part, xn[ln][:, i % XN, cols], ident[0:R, 0:R])
                                else:
                                    pe.matmul(part, xn[ln][:, i % XN, cols], ident[0:R, 0:R], start=True, stop=False)
                                    last = pe.matmul(part, mod_w[:, 1, cols].bitcast(F32),
                                                     condh[:, i * R:(i + 1) * R].bitcast(F32), start=False, stop=True)
                            last.then_inc(yT_filled, 1)

                def by_chunk(s, w, c, done):
                    at, m = CHUNKS[c]
                    for k in range(KT):
                        last = product(slot[s][:, at:at + m], w(k), (yTh[:, k, at:at + m], yTl[:, k, at:at + m]),
                                       k == 0, k == KT - 1)
                    if done is not None:
                        last.then_inc(done, 1)

                def wide(s, w, b, ln):
                    for c, (at, m) in enumerate(CHUNKS):
                        pe.wait_ge(yT_lo, b * 2 * NT + (ln * NT + -(-(at + m) // R)))
                        by_chunk(s, w, c, filled[s] if c == len(CHUNKS) - 1 else None)

                def scores(b, h, i, c):
                    s, u = score_slot(i)
                    at, n = CHUNKS[c]
                    if c == 0:
                        free(s, in_head(s, b, h, u))
                    rows = slice(i * R, (i + 1) * R)
                    last = product(slot[s][0:R, at:at + n], (qh[:, rows], ql[:, rows]),
                                   (kh[:, at:at + n], kl[:, at:at + n]), True, True)
                    if c == len(CHUNKS) - 1:
                        last.then_inc(filled[s], 1)

                def transposes(b, h, i, f):
                    j, m = PARTS[f]
                    s, u = LAST_SLOT[i] if i in LAST_SLOT else PART_SLOT[i, f]
                    bank = f * 512 if i in LAST_SLOT else 0
                    if f == 0 or i not in LAST_SLOT:
                        free(s, in_head(s, b, h, u))
                    for c in range(m):
                        last = pe.transpose(slot[s][0:R, bank + c * R:bank + (c + 1) * R],
                                            probs[:, i % 2, (j + c) * R:(j + c + 1) * R], ident[0:R, 0:R])
                    last.then_inc(last_filled if i in LAST_SLOT and f < 2 else filled[s], 1)

                def v_tiles(b, h, f):
                    s, u = V_SLOT[f]
                    free(s, in_head(s, b, h, u))
                    j, m = PARTS[f]
                    for c in range(m):
                        last = pe.transpose(slot[s][0:R, c * DH:(c + 1) * DH],
                                            vT[:, (j + c) * R:(j + c + 1) * R], ident[:, :])
                    last.then_inc(filled[s], 1)

                def head_out(b, h, g):
                    s, u = OUT_SLOT[g]
                    free(s, in_head(s, b, h, u))
                    for j in range(NT):
                        if g == PAIRS - 1:
                            if j == PARTS[0][0]:
                                pe.wait_ge(last_split, b * HEADS * 4 + h * 4 + 2)
                            elif j == PARTS[1][0]:
                                pe.wait_ge(last_split, b * HEADS * 4 + h * 4 + 4)
                            elif j == PARTS[2][0]:
                                for t, w in LAST_SLOT.values():
                                    pe.wait_ge(drained[t], in_head(t, b, h, w) + 2)
                        elif j == PARTS[2][0]:
                            t, w = PART_SLOT[2 * g + 1, 2]
                            pe.wait_ge(drained[t], in_head(t, b, h, w) + 2)
                        last = product(slot[s][:, 0:2 * R], (vh[:, j, :], vl[:, j, :]),
                                       (probsTh[:, j, :], probsTl[:, j, :]), j == 0, j == NT - 1)
                    last.then_inc(filled[s], 1)

                def out_tile(b, h, ps, i):
                    if i % 2 == 0:
                        s, u = OUT_SLOT[i // 2]
                        pe.wait_ge(drained[s], in_head(s, b, h, u) + 2)
                    rows = slice(i * R, (i + 1) * R)
                    return product(ps, (oTh[:, rows], oTl[:, rows]), (woh[:, :], wol[:, :]), True, True)

                def down_tile(b, ps, i):
                    rows = slice(i * R, (i + 1) * R)
                    for k in range(KT):
                        if i == 0 and k == KT - 1:
                            free("B", in_mlp("B", b, 2))
                        last = product(ps, (uph[:, k, rows], upl[:, k, rows]), (w2h[:, k, :], w2l[:, k, :]),
                                       k == 0, k == KT - 1)
                    return last

                def into_bank(n, i, tile):
                    if i >= 2:
                        pe.wait_ge(product_drained, n + (i - 1))
                    tile(product_banks[i % 2], i).then_inc(product_filled, 1)

                def head(b, h):
                    n = b * HEADS + h
                    weights_split(head_item(b, h, -1))
                    free("A", in_head("A", b, h, 0))
                    wide("A", lambda k: (wqh[:, k, :], wql[:, k, :]), b, 0)
                    free("B", in_head("B", b, h, 0))
                    for c in range(3):
                        by_chunk("B", lambda k: (wkh[:, k, :], wkl[:, k, :]), c, k_part if c < 2 else filled["B"])
                    for c in range(3):
                        if c < 2:
                            pe.wait_ge(k_lo, b * HEADS * 2 + h * 2 + (c + 1))
                        else:
                            pe.wait_ge(drained["B"], in_head("B", b, h, 0) + 2)
                        scores(b, h, 0, c)
                    for c in range(3):
                        scores(b, h, 1, c)
                    def wv(k):
                        return wvh[:, k, :], wvl[:, k, :]

                    free("A", in_head("A", b, h, V_USE))
                    by_chunk("A", wv, 0, v_part)
                    by_chunk("A", wv, 1, v_part)
                    pe.wait_ge(v_copied, b * HEADS * 2 + h * 2 + 1)
                    v_tiles(b, h, 0)
                    by_chunk("A", wv, 2, filled["A"])
                    pe.wait_ge(v_copied, b * HEADS * 2 + h * 2 + 2)
                    v_tiles(b, h, 1)
                    for i in range(NT - 2):
                        pe.wait_ge(probs_ready, n * NT + (i + 1))
                        for f in range(3):
                            if (i, f) == (1, 2):
                                v_tiles(b, h, 2)
                            transposes(b, h, i, f)
                            scores(b, h, i + 2, f)
                        if i % 2 == 1:
                            head_out(b, h, i // 2)
                    for i, f in LAST_PARTS:
                        if f == 0:
                            pe.wait_ge(probs_ready, n * NT + (i + 1))
                        transposes(b, h, i, f)
                    head_out(b, h, PAIRS - 1)
                    weights_split(head_item(b, h, 0))

                def body(b, last):
                    with pe.Fori(0, HEADS - 1) as h:
                        head(b, h)
                        at = {"A": in_head("A", b, h, 8), "B": in_head("B", b, h, 7)}
                        for s, tiles in OUT_BATCHES:
                            u = at[s]
                            at[s] = u + 1
                            free(s, u)
                            for c, i in enumerate(tiles):
                                end = out_tile(b, h, slot[s][0:R, c * 512:c * 512 + D], i)
                            end.then_inc(filled[s], 1)
                    head(b, HEADS - 1)
                    for s in "AB":
                        free(s, in_mlp(s, b, 0))
                    weights_split(head_item(b, HEADS - 1, 2))
                    norm(b, 1, lambda i: into_bank(
                        b * 2 * NT, i, lambda ps, i: out_tile(b, HEADS - 1, ps, i)))
                    weights_split(item(b, mlp_first + KT - 1))
                    for m in range(KT):
                        s = "AB"[m % 2]
                        free(s, in_mlp(s, b, m // 2))
                        cols = slice(m * 128, (m + 1) * 128)
                        wide(s, lambda k: (w1h[:, k, cols], w1l[:, k, cols]), b, 1)
                    weights_split(item(b, mlp_first + len(mlp_order(last)) - 1))
                    free("A", in_mlp("A", b, 2))
                    if last:
                        for i in range(NT):
                            into_bank(b * 2 * NT + NT, i, lambda ps, i: down_tile(b, ps, i))
                    else:
                        norm(b + 1, 0, lambda i: into_bank(
                            b * 2 * NT + NT, i, lambda ps, i: down_tile(b, ps, i)))

                weights_split(1)
                norm(0, 0, None)
                with pe.Fori(0, BLOCKS - 1) as b:
                    body(b, False)
                body(BLOCKS - 1, True)


PARAMS = ["f_w1", "f_b1", "f_w2", "f_b2", "s1_w", "s1_b", "b1_w", "b1_b", "wq", "bq", "wk", "bk", "wv", "bv",
          "wo", "bo", "s2_w", "s2_b", "b2_w", "b2_b", "m_w1", "m_b1", "m_w2", "m_b2"]
GCN_PARAMS = ["W1", "b1", "W2", "b2", "Wd1", "bd1", "Wd2", "bd2", "Wd3", "bd3"]


def build(nc, ap, out):
    x_keep = nc.dram_tensor("x1_keep", [N, D], F32, kind="Internal").ap()
    ctx = ExitStack()
    with ctx:
        def sb(name, shape, dt=F32):
            return ctx.enter_context(nc.sbuf_tensor(name, shape, dt))

        ident = sb("ident", [128, 128])
        x = sb("x", [R, NT, D])
        logc = sb("logc", [R, NT, N])
        with nc.sbuf_tensor("ids", [R, N], F16) as ids:
            pass
        condh = sb("cond_parts", [128, N], F32R)
        gnn = {n: ap["L1_gnn_" + n] for n in PARAMS}
        with nc.sbuf_tensor("counts", [R, NT, N], F32) as counts:
            onehot_a = logc[:, :, :].rearrange("p t n -> p (t n)")[:, 0:GT * N // 2].bitcast(BF16)\
                .rearrange("p (t n) -> p t n", t=GT)
            count_edges(nc, ap["src"], ap["dst"], counts[:, :, :], onehot_a, ids,
                        x[:, :, :].rearrange("p t d -> p (t d)"))
            gcn_layer(nc, ap["node_vec1"], gnn, condh[:, :], ap["x"],
                      *(ap["L0_gnn_" + n] for n in GCN_PARAMS), x_keep, x[:, :, :],
                      counts[:, :, :], logc[:, :, :], ident[:, :])
        transformer(nc, condh[:, :], gnn, x_keep, out,
                    x[:, :, :], logc[:, :, :], ident[:, :])


INPUTS = ["x", "src", "dst", "node_vec1"] + ["L0_gnn_" + n for n in GCN_PARAMS] + ["L1_gnn_" + n for n in PARAMS]


def kernel(**inputs):
    import concourse.bacc as bacc
    from concourse.bass_utils import run_bass_kernel_spmd

    nc = bacc.Bacc("TRN2", target_bir_lowering=False, num_devices=1)
    arrays, ap = {}, {}
    for name in INPUTS:
        a = np.ascontiguousarray(inputs[name])
        arrays[f"in_{name}_dram"] = a
        ap[name] = nc.dram_tensor(f"in_{name}_dram", a.shape, mybir.dt.from_np(a.dtype), kind="ExternalInput").ap()
    out = nc.dram_tensor("out_0_dram", (N, D), F32, kind="ExternalOutput").ap()
    build(nc, ap, out)
    r = run_bass_kernel_spmd(nc, [arrays], core_ids=[0])
    return r.results[0]["out_0_dram"]
```
